# Optimizing a Trainium2 kernel written in Bass

```python
import numpy as np
import jax
import jax.numpy as jnp

def _softmax(x, axis=-1):
    return jax.nn.softmax(x, axis=axis)

def _gelu(x):
    return jax.nn.gelu(x, approximate=True)

def _silu(x):
    return jax.nn.silu(x)

def _sigmoid(x):
    return jax.nn.sigmoid(x)

def _layernorm(x, axis=-1, eps=1e-05):
    m = jnp.mean(x, axis=axis, keepdims=True)
    v = jnp.var(x, axis=axis, keepdims=True)
    return (x - m) / jnp.sqrt(v + eps)

def _scatter_add(tgt, idx, src, axis=0):
    return tgt.at[idx].add(src)

def _segment_sum(src, seg, n):
    return jax.ops.segment_sum(src, seg, n)
kernel_name = 'mk_seq_preln_d2_jaxref_r4_5911bb'

def setup_inputs(seed: int=0):
    np.random.seed(seed)
    _w = jnp.asarray

    def _L0_attn_setup():
        import jax, jax.numpy as jnp
        import numpy as np
        B, T, D, H = (2, 512, 256, 16)
        key = jax.random.key(seed)
        kx, kq, kk, kv, ko = jax.random.split(key, 5)
        s = D ** (-0.5)
        return {'x': jax.random.normal(kx, (B, T, D), dtype=jnp.float32), 'Wq': jax.random.normal(kq, (D, D), dtype=jnp.float32) * s, 'Wk': jax.random.normal(kk, (D, D), dtype=jnp.float32) * s, 'Wv': jax.random.normal(kv, (D, D), dtype=jnp.float32) * s, 'Wo': jax.random.normal(ko, (D, D), dtype=jnp.float32) * s, 'quadrant_weights': jnp.array([1.0, -0.5, -0.5, 0.25], dtype=jnp.float32)}
    _L0_attn_in = _L0_attn_setup()

    def _L0_ffn_setup():
        import jax, jax.numpy as jnp
        import numpy as np

        def _bitlinear(x, w_latent):
            scale = jax.lax.stop_gradient(jnp.clip(jnp.mean(jnp.abs(w_latent), axis=1, keepdims=True), 1e-05, None))
            tern = jnp.clip(jnp.round(w_latent / scale), -1.0, 1.0)
            w = w_latent + jax.lax.stop_gradient(tern - w_latent)
            return x @ (w * scale).T
        key = jax.random.key(seed)
        ks = jax.random.split(key, 6)
        dim, hidden, rank = (256, 1024, 16)
        B, S = (4, 1024)
        x = jax.random.normal(ks[0], (B, S, dim), dtype=jnp.float32)
        w_fc = 0.02 * jax.random.normal(ks[1], (hidden, dim), dtype=jnp.float32)
        w_proj = 0.02 * jax.random.normal(ks[2], (dim, hidden), dtype=jnp.float32)
        u = 0.02 * jax.random.normal(ks[3], (hidden, rank), dtype=jnp.float32)
        v = 0.02 * jax.random.normal(ks[4], (rank, dim), dtype=jnp.float32)
        fast_b = jax.random.normal(ks[5], (rank, rank), dtype=jnp.float32)
        gate = jnp.float32(0.05)
        return {'x': x, 'fast_b': fast_b, 'w_fc': w_fc, 'w_proj': w_proj, 'u': u, 'v': v, 'gate': gate}
    _L0_ffn_in = _L0_ffn_setup()

    def _L1_attn_setup():
        import jax, jax.numpy as jnp
        import numpy as np
        B_, S_, D_, N_ = (4, 512, 256, 16)

        def _layernorm(y, w, b, eps=1e-05):
            mu = jnp.mean(y, axis=-1, keepdims=True)
            var = jnp.mean((y - mu) ** 2, axis=-1, keepdims=True)
            return (y - mu) * jax.lax.rsqrt(var + eps) * w + b
        key = jax.random.key(seed)
        ks = jax.random.split(key, 8)
        x = jax.random.normal(ks[0], (B_, S_, D_), dtype=jnp.float32)
        A = jax.random.normal(ks[1], (D_, N_, N_), dtype=jnp.float32) * 0.1
        Bm = jax.random.normal(ks[2], (D_, N_), dtype=jnp.float32) * 0.1
        Cm = jax.random.normal(ks[3], (D_, N_), dtype=jnp.float32) * 0.1
        Dm = jax.random.normal(ks[4], (D_,), dtype=jnp.float32) * 0.1
        ln_w = jnp.ones((D_,), dtype=jnp.float32)
        ln_b = jnp.zeros((D_,), dtype=jnp.float32)
        W_out = jax.random.normal(ks[5], (D_, D_), dtype=jnp.float32) * (1.0 / np.sqrt(D_))
        b_out = jnp.zeros((D_,), dtype=jnp.float32)
        return {'x': x, 'A': A, 'Bm': Bm, 'Cm': Cm, 'Dm': Dm, 'ln_w': ln_w, 'ln_b': ln_b, 'W_out': W_out, 'b_out': b_out}
    _L1_attn_in = _L1_attn_setup()

    def _L1_ffn_setup():
        import jax, jax.numpy as jnp
        import numpy as np
        D_MODEL, EXPERT_DIM, NUM_EXPERTS, TOP_K = (256, 512, 16, 2)
        SEQ_LEN, BATCH = (512, 2)
        key = jax.random.key(seed)
        ks = jax.random.split(key, 8)
        s_d = 1.0 / np.sqrt(D_MODEL)
        s_h = 1.0 / np.sqrt(EXPERT_DIM)
        return {'x': jax.random.normal(ks[0], (SEQ_LEN, BATCH, D_MODEL), jnp.float32), 'Wg': jax.random.uniform(ks[1], (D_MODEL, NUM_EXPERTS), jnp.float32, -s_d, s_d), 'bg': jax.random.uniform(ks[2], (NUM_EXPERTS,), jnp.float32, -s_d, s_d), 'bias': jnp.zeros((NUM_EXPERTS,), jnp.float32), 'W1': jax.random.uniform(ks[3], (NUM_EXPERTS, D_MODEL, EXPERT_DIM), jnp.float32, -s_d, s_d), 'b1': jax.random.uniform(ks[4], (NUM_EXPERTS, EXPERT_DIM), jnp.float32, -s_d, s_d), 'W2': jax.random.uniform(ks[5], (NUM_EXPERTS, EXPERT_DIM, D_MODEL), jnp.float32, -s_h, s_h), 'b2': jax.random.uniform(ks[6], (NUM_EXPERTS, D_MODEL), jnp.float32, -s_h, s_h)}
    _L1_ffn_in = _L1_ffn_setup()
    _d = {'L0_attn_x': _L0_attn_in['x'], 'L0_attn_Wq': _L0_attn_in['Wq'], 'L0_attn_Wk': _L0_attn_in['Wk'], 'L0_attn_Wv': _L0_attn_in['Wv'], 'L0_attn_Wo': _L0_attn_in['Wo'], 'L0_attn_quadrant_weights': _L0_attn_in['quadrant_weights'], 'L0_ffn_fast_b': _L0_ffn_in['fast_b'], 'L0_ffn_w_fc': _L0_ffn_in['w_fc'], 'L0_ffn_w_proj': _L0_ffn_in['w_proj'], 'L0_ffn_u': _L0_ffn_in['u'], 'L0_ffn_v': _L0_ffn_in['v'], 'L0_ffn_gate': _L0_ffn_in['gate'], 'L1_attn_A': _L1_attn_in['A'], 'L1_attn_Bm': _L1_attn_in['Bm'], 'L1_attn_Cm': _L1_attn_in['Cm'], 'L1_attn_Dm': _L1_attn_in['Dm'], 'L1_attn_ln_w': _L1_attn_in['ln_w'], 'L1_attn_ln_b': _L1_attn_in['ln_b'], 'L1_attn_W_out': _L1_attn_in['W_out'], 'L1_attn_b_out': _L1_attn_in['b_out'], 'L1_ffn_Wg': _L1_ffn_in['Wg'], 'L1_ffn_bg': _L1_ffn_in['bg'], 'L1_ffn_bias': _L1_ffn_in['bias'], 'L1_ffn_W1': _L1_ffn_in['W1'], 'L1_ffn_b1': _L1_ffn_in['b1'], 'L1_ffn_W2': _L1_ffn_in['W2'], 'L1_ffn_b2': _L1_ffn_in['b2']}
    _x0 = _d['L0_attn_x']
    _d['L0_attn_x'] = jax.random.normal(jax.random.fold_in(jax.random.key(seed), 1), (4, 1024, 256), dtype=_x0.dtype)
    del _x0
    return _d

def reference(L0_attn_x, L0_attn_Wq, L0_attn_Wk, L0_attn_Wv, L0_attn_Wo, L0_attn_quadrant_weights, L0_ffn_fast_b, L0_ffn_w_fc, L0_ffn_w_proj, L0_ffn_u, L0_ffn_v, L0_ffn_gate, L1_attn_A, L1_attn_Bm, L1_attn_Cm, L1_attn_Dm, L1_attn_ln_w, L1_attn_ln_b, L1_attn_W_out, L1_attn_b_out, L1_ffn_Wg, L1_ffn_bg, L1_ffn_bias, L1_ffn_W1, L1_ffn_b1, L1_ffn_W2, L1_ffn_b2):

    def _L0_attn_ref(x, Wq, Wk, Wv, Wo, quadrant_weights):
        import jax, jax.numpy as jnp
        import numpy as np
        B, T, D, H = (2, 512, 256, 16)
        Bx, Tx, Dx = x.shape
        d = Dx // H
        h = d // 2
        scale = h ** (-0.5)
        q = (x @ Wq).reshape(Bx, Tx, H, d).transpose(0, 2, 1, 3)
        k = (x @ Wk).reshape(Bx, Tx, H, d).transpose(0, 2, 1, 3)
        v = (x @ Wv).reshape(Bx, Tx, H, d).transpose(0, 2, 1, 3)
        q1, q2 = (q[..., :h], q[..., h:])
        k1, k2 = (k[..., :h], k[..., h:])
        w = jax.nn.softmax(quadrant_weights)
        k_eff1 = w[0] * k1 + w[1] * k2
        k_eff2 = w[2] * k1 + w[3] * k2
        attn = (jnp.einsum('bhqc,bhkc->bhqk', q1, k_eff1) + jnp.einsum('bhqc,bhkc->bhqk', q2, k_eff2)) * scale
        attn = jax.nn.softmax(attn, axis=-1)
        out = jnp.einsum('bhqk,bhkd->bhqd', attn, v)
        out = out.transpose(0, 2, 1, 3).reshape(Bx, Tx, Dx)
        return out @ Wo

    def _L0_ffn_ref(x, fast_b, w_fc, w_proj, u, v, gate):
        import jax, jax.numpy as jnp
        import numpy as np

        def _bitlinear(x, w_latent):
            scale = jax.lax.stop_gradient(jnp.clip(jnp.mean(jnp.abs(w_latent), axis=1, keepdims=True), 1e-05, None))
            tern = jnp.clip(jnp.round(w_latent / scale), -1.0, 1.0)
            w = w_latent + jax.lax.stop_gradient(tern - w_latent)
            return x @ (w * scale).T
        h = _bitlinear(x, w_fc) + gate * (x @ v.T @ fast_b.T @ u.T)
        r = jnp.maximum(h, 0.0)
        return _bitlinear(r * r, w_proj)

    def _L1_attn_ref(x, A, Bm, Cm, Dm, ln_w, ln_b, W_out, b_out):
        import jax, jax.numpy as jnp
        import numpy as np
        B_, S_, D_, N_ = (4, 512, 256, 16)

        def _layernorm(y, w, b, eps=1e-05):
            mu = jnp.mean(y, axis=-1, keepdims=True)
            var = jnp.mean((y - mu) ** 2, axis=-1, keepdims=True)
            return (y - mu) * jax.lax.rsqrt(var + eps) * w + b
        bsz = x.shape[0]
        h0 = jnp.zeros((bsz, A.shape[0], A.shape[1]), dtype=x.dtype)

        def step(h, x_t):
            h = jnp.einsum('dnm,bdm->bdn', A, h) + Bm[None] * x_t[..., None]
            y_t = jnp.einsum('dn,bdn->bd', Cm, h) + Dm * x_t
            return (h, y_t)
        _, y = jax.lax.scan(step, h0, jnp.swapaxes(x, 0, 1))
        y = jnp.swapaxes(y, 0, 1)
        y = _layernorm(y, ln_w, ln_b)
        y = jax.nn.gelu(y, approximate=False)
        y = y @ W_out.T + b_out
        return x + y

    def _L1_ffn_ref(x, Wg, bg, bias, W1, b1, W2, b2):
        import jax, jax.numpy as jnp
        import numpy as np
        D_MODEL, EXPERT_DIM, NUM_EXPERTS, TOP_K = (256, 512, 16, 2)
        SEQ_LEN, BATCH = (512, 2)
        logits = jnp.einsum('sbd,de->sbe', x, Wg) + bg + bias
        vals, idx = jax.lax.top_k(logits, TOP_K)
        w = jax.nn.softmax(vals - jnp.max(vals, axis=-1, keepdims=True), axis=-1)
        cw = jnp.einsum('sbk,sbke->sbe', w, jax.nn.one_hot(idx, NUM_EXPERTS, dtype=x.dtype))
        h = jax.nn.relu(jnp.einsum('sbd,edh->esbh', x, W1) + b1[:, None, None, :])
        y = jnp.einsum('esbh,ehd->esbd', h, W2) + b2[:, None, None, :]
        out = jnp.einsum('esbd,sbe->sbd', y, cw)
        return out
    x = L0_attn_x
    x = x + _L0_attn_ref(_layernorm(x, axis=-1), L0_attn_Wq, L0_attn_Wk, L0_attn_Wv, L0_attn_Wo, L0_attn_quadrant_weights)
    x = x + _L0_ffn_ref(_layernorm(x, axis=-1), L0_ffn_fast_b, L0_ffn_w_fc, L0_ffn_w_proj, L0_ffn_u, L0_ffn_v, L0_ffn_gate)
    x = x + _L1_attn_ref(_layernorm(x, axis=-1), L1_attn_A, L1_attn_Bm, L1_attn_Cm, L1_attn_Dm, L1_attn_ln_w, L1_attn_ln_b, L1_attn_W_out, L1_attn_b_out)
    x = x + _L1_ffn_ref(_layernorm(x, axis=-1), L1_ffn_Wg, L1_ffn_bg, L1_ffn_bias, L1_ffn_W1, L1_ffn_b1, L1_ffn_W2, L1_ffn_b2)
    return x

_drawn_inputs = setup_inputs


def setup_inputs(seed=0):
    import zlib

    import numpy as np

    out = dict(_drawn_inputs(seed))
    spreads = {'L1_attn_ln_w': (1.0, 0.2),
     'L1_attn_ln_b': (0.0, 0.1),
     'L1_attn_b_out': (0.0, 0.1),
     'L1_ffn_bias': (0.0, 0.1)}
    factors = {}
    for name, (base, spread) in spreads.items():
        noise = np.random.default_rng([zlib.crc32(name.encode()), seed]).standard_normal(out[name].shape)
        drawn = base * np.exp(spread * noise) if base else spread * noise
        out[name] = jnp.asarray(drawn.astype(out[name].dtype))
    for name, factor in factors.items():
        out[name] = (out[name] * factor).astype(out[name].dtype)
    return out
```

```python
from contextlib import ExitStack

import concourse.bass as bass
from concourse import mybir

F32 = mybir.dt.float32
BF16 = mybir.dt.bfloat16
I32 = mybir.dt.int32
U32 = mybir.dt.uint32
ALU = mybir.AluOpType
ACT = mybir.ActivationFunctionType
AX = mybir.AxisListType.X
ds = bass.ds

P = 128
BATCH, SEQ, D = 4, 1024, 256
T = BATCH * SEQ
NT = T // P
DK = D // P
CT = 4
CW = CT * P
NC = T // CW
BANK = 512
EPS = 1e-5

H, HD = 16, 16
HH = HD // 2
HG = 4
UNITS = BATCH * H // HG
UPB = H // HG
KT = SEQ // P
QT = SEQ // P
QC = SEQ // BANK
PARTS = 3
PAIR_Q = [0, 0, 1, 0, 2, 1]
PAIR_K = [0, 1, 0, 2, 0, 1]
KROWS = len(PAIR_Q) * HD
AROWS = KROWS + PARTS
RING = 3


E = 16
EH = 512
EK = EH // P
MT = 2 * NT + E


class Count:

    def __init__(self, sem):
        self.sem, self.n = sem, 0

    def mark(self, ins):
        ins.then_inc(self.sem, 1)
        self.n += 1

    def wait(self, eng):
        eng.wait_ge(self.sem, self.n)


def transformer_kernel(nc, ins, out):
    (x_in, wq_in, wk_in, wv_in, wo_in, quad_in, fastb_in, wfc_in, wproj_in, u_in, v_in, gate_in,
     a_in, bm_in, cm_in, dm_in, lnw_in, lnb_in, wout_in, bout_in,
     wg_in, bg_in, bias_in, w1_in, b1_in, w2_in, b2_in) = ins
    x_rows = x_in.rearrange("b s d -> (b s) d")
    out_rows = out.rearrange("b s d -> (b s) d")
    x_tiles = x_rows.rearrange("(t p) d -> p t d", p=P)
    out_tiles = out_rows.rearrange("(t p) d -> p t d", p=P)
    by_k = lambda w: w.rearrange("(k p) n -> p k n", p=P)

    outer = ExitStack()
    phase_sems = []

    def sem(name):
        phase_sems.append(nc.alloc_semaphore(name))
        return phase_sems[-1]

    def reuse_sems(kept=()):
        with nc.Block() as block:
            @block.gpsimd
            def _(pool):
                nc.clear_and_free_semaphores([s for s in phase_sems if s not in kept])
        phase_sems.clear()

    def sbuf(stack, name, shape, dt=F32):
        return stack.enter_context(nc.sbuf_tensor(name, shape, dt))

    with outer:
        ps = outer.enter_context(nc.psum_tensor("ps", [P, 8, BANK], F32))
        X = sbuf(outer, "X", [P, NT, D])
        ident = sbuf(outer, "ident", [P, P])
        identb = sbuf(outer, "identb", [P, P], BF16)
        bn = sbuf(outer, "bn", [P, NT, 6])
        mv = sbuf(outer, "mv", [P, NT, 2])
        rstd = sbuf(outer, "rstd", [P, NT])
        lnt = sbuf(outer, "lnt", [P, 3, NT])

        ln_sems = [(sem(f"ln{n}_steps"), sem(f"ln{n}_sqrt")) for n in range(5)]

        def layernorm_scale_dve(dve, n):
            steps, rooted = Count(ln_sems[n][0]), ln_sems[n][1]
            for t in range(NT):
                steps.mark(nc.vector.bn_aggr(mv[:, t, :], bn[:, t, :]))
            steps.wait(dve)
            ve, r0, w = lnt[:, 0], lnt[:, 1], lnt[:, 2]
            steps.mark(nc.vector.tensor_scalar_add(ve, mv[:, :, 1], EPS))
            dve.wait_ge(rooted, 1)
            steps.mark(nc.vector.reciprocal(rstd[:], r0))
            steps.wait(dve)
            steps.mark(nc.vector.tensor_tensor(w, rstd[:], rstd[:], op=ALU.mult))
            steps.wait(dve)
            steps.mark(nc.vector.tensor_tensor(r0, w, ve, op=ALU.mult))
            steps.wait(dve)
            steps.mark(nc.vector.tensor_scalar(w, r0, -0.5, 1.5, ALU.mult, ALU.add))
            steps.wait(dve)
            steps.mark(nc.vector.tensor_tensor(rstd[:], rstd[:], w, op=ALU.mult))
            steps.wait(dve)

        def layernorm_root_act(act, n):
            act.wait_ge(ln_sems[n][0], NT + 1)
            nc.scalar.activation(lnt[:, 1], lnt[:, 0], ACT.Sqrt).then_inc(ln_sems[n][1], 1)

        def normalise(dst, t, src=X):
            return nc.vector.tensor_scalar(dst, src[:, ds(t, 1), :].rearrange("p a d -> p (a d)"),
                                           mv[:, ds(t, 1), 0:1].rearrange("p a s -> p (a s)"),
                                           rstd[:, ds(t, 1)], ALU.subtract, ALU.mult)

        xs_steps = [sem(f"x_steps{n}") for n in range(4)]

        def add_chunk(dve, c, bank, done, added, credit, steps):
            dve.wait_ge(done, c + 1)
            chunk = X[:, ds(CT * c, CT), :].rearrange("p k d -> p (k d)")
            nc.vector.tensor_tensor(chunk, ps[:, bank:bank + 2].rearrange("p a n -> p (a n)"), chunk, op=ALU.add).then_inc(added, 1)
            dve.wait_ge(added, c + 1 + credit)
            for k in range(CT):
                nc.vector.bn_stats(bn[:, ds(CT * c + k, 1), :].rearrange("p a s -> p (a s)"),
                                   X[:, ds(CT * c + k, 1), :].rearrange("p a d -> p (a d)")).then_inc(steps, 1)

        xsort = nc.dram_tensor("tokens_by_expert", [MT * P, D], F32, kind="Internal").ap()
        zero = sbuf(outer, "zero", [P, D])
        x_zeroed, zero_ready = sem("tokens_zeroed"), sem("zero_set")
        lasting = list(phase_sems)
        pqk = nc.dram_tensor("qk_parts", [2, PARTS, DK, P, T], BF16, kind="Internal").ap()

        mid = ExitStack()
        with mid:
            ATT = sbuf(mid, "ATT", [P, NT, D])
            wo = sbuf(mid, "wo", [P, DK, D])
            with ExitStack() as st:
                V = sbuf(st, "V", [P, NT, D])
                wqk = sbuf(st, "wqk", [P, 2, DK, D])
                wv = sbuf(st, "wv", [P, DK, D])
                with ExitStack() as s0:
                    wk = sbuf(s0, "wk", [P, DK, H, 2, HH])
                    wkt = sbuf(s0, "wkt", [P, DK, H, 2, HH])
                    quad = sbuf(s0, "quad", [P, 4])
                    qs = sbuf(s0, "qs", [P, 8])
                    x_loaded = [sem(f"x_loaded{c}") for c in range(4)]
                    w_loaded, k_loaded, quad_loaded = sem("w_loaded"), sem("k_loaded"), sem("quad_loaded")
                    quad_steps, quad_max, quad_exp = sem("quad_steps"), sem("quad_max"), sem("quad_exp")
                    idz, id_ready = sem("idz"), sem("id_ready")
                    with nc.Block() as block:
                        @block.sync
                        def _(sp):
                            for c in range(4):
                                sp.dma_start(X[:, 8 * c:8 * c + 8, :], x_tiles[:, 8 * c:8 * c + 8, :]).then_inc(x_loaded[c], 16)

                        @block.scalar
                        def _(act):
                            act.dma_start(quad[:], quad_in.partition_broadcast(P)).then_inc(quad_loaded, 16)
                            act.dma_start(wk[:].rearrange("p k h a c -> p k (h a c)"), by_k(wk_in)).then_inc(k_loaded, 16)
                            act.dma_start(wqk[:, 0], by_k(wq_in)).then_inc(w_loaded, 16)
                            act.dma_start(wv[:], by_k(wv_in)).then_inc(w_loaded, 16)
                            act.dma_start(wo[:], by_k(wo_in)).then_inc(w_loaded, 16)
                            act.wait_ge(quad_max, 1)
                            nc.scalar.activation(qs[:, 4:8], quad[:], ACT.Exp, bias=qs[:, 1:2]).then_inc(quad_exp, 1)
                            layernorm_root_act(act, 0)
                            act.wait_ge(w_loaded, 48)

                        @block.gpsimd
                        def _(pool):
                            nc.gpsimd.memset(zero[:], 0.0).then_inc(zero_ready, 1)
                            nc.gpsimd.memset(ident[:], 0.0).then_inc(idz, 1)
                            nc.gpsimd.memset(identb[:], 0.0).then_inc(idz, 1)
                            pool.wait_ge(idz, 2)
                            for m in (ident, identb):
                                nc.gpsimd.affine_select(out=m[:], in_=m[:], compare_op=ALU.not_equal, fill=1.0, base=0,
                                                        pattern=[[-1, P]], channel_multiplier=1).then_inc(id_ready, 1)

                        @block.vector
                        def _(dve):
                            dve.wait_ge(quad_loaded, 16)
                            steps = Count(quad_steps)
                            steps.mark(nc.vector.reduce_max(qs[:, 0:1], quad[:], AX))
                            steps.wait(dve)
                            nc.vector.tensor_scalar_mul(qs[:, 1:2], qs[:, 0:1], -1.0).then_inc(quad_max, 1)
                            dve.wait_ge(quad_exp, 1)
                            steps.mark(nc.vector.reduce_sum(qs[:, 2:3], qs[:, 4:8], AX))
                            steps.wait(dve)
                            steps.mark(nc.vector.reciprocal(qs[:, 3:4], qs[:, 2:3]))
                            steps.wait(dve)
                            steps.mark(nc.vector.tensor_scalar(quad[:], qs[:, 4:8], qs[:, 3:4], float(HH) ** -0.5, ALU.mult, ALU.mult))
                            steps.wait(dve)
                            dve.wait_ge(k_loaded, 16)
                            for a in range(2):
                                half = wqk[:, 1].rearrange("p k (h a c) -> p k h a c", h=H, a=2)
                                for k in range(DK):
                                    steps.mark(nc.vector.tensor_scalar(wkt[:, k, :, a, :], wk[:, k, :, 1, :], quad[:, 2 * a + 1:2 * a + 2], None, ALU.mult))
                                    steps.wait(dve)
                                    steps.mark(nc.vector.scalar_tensor_tensor(half[:, k, :, a, :], wk[:, k, :, 0, :], quad[:, 2 * a:2 * a + 1],
                                                                              wkt[:, k, :, a, :], op0=ALU.mult, op1=ALU.add))
                            for c in range(4):
                                dve.wait_ge(x_loaded[c], 16)
                                with dve.Fori(8 * c, 8 * c + 8) as t:
                                    nc.vector.bn_stats(bn[:, ds(t, 1), :].rearrange("p a s -> p (a s)"),
                                                       X[:, ds(t, 1), :].rearrange("p a d -> p (a d)")).then_inc(quad_steps, 1)
                            steps.n += NT
                            steps.wait(dve)
                            layernorm_scale_dve(dve, 0)

                with ExitStack() as s1:
                    xn = sbuf(s1, "xn", [P, 2, CT, D])
                    xT = sbuf(s1, "xT", [P, 2, DK, CW])
                    parts = sbuf(s1, "parts", [P, 2, 2, PARTS, DK, CW], BF16)
                    part = lambda h, m, a: parts[:, h, m // DK, a, m % DK]
                    rest = sbuf(s1, "rest", [P, 2 * DK, CW])
                    xn_ready, xn_tr, xT_ready = sem("xn_ready"), sem("xn_tr"), sem("xT_ready")
                    qk_done, hi_ready, rest_ready, mid_ready, lo_ready = (sem(n) for n in ("qk_done", "hi_ready", "rest_ready", "mid_ready", "lo_ready"))
                    v_done, v_kept = sem("v_done"), sem("v_kept")
                    stored = [sem(f"parts_stored{h}") for h in range(2)]
                    with nc.Block() as block:
                        @block.vector
                        def _(dve):
                            def norm(c, h):
                                for k in range(CT):
                                    last = normalise(xn[:, h, k, :], CT * c + k)
                                last.then_inc(xn_ready, 1)
                            norm(0, 0)
                            with dve.Fori(0, NC // 2) as i:
                                for h in range(2):
                                    c = 2 * i + h
                                    norm((c + 1) % NC, 1 - h)
                                    for m in range(2 * DK):
                                        dve.wait_ge(hi_ready, 2 * DK * c + m + 1)
                                        dve.wait_ge(lo_ready, 2 * DK * c + m + 1)
                                        nc.vector.tensor_tensor(rest[:, m], ps[:, 2 + m], part(h, m, 0), op=ALU.subtract).then_inc(rest_ready, 1)

                        @block.scalar
                        def _(act):
                            with act.Fori(0, NC // 2) as i:
                                for h in range(2):
                                    c = 2 * i + h
                                    act.wait_ge(xn_tr, c + 1)
                                    nc.scalar.copy(xT[:, h].rearrange("p k n -> p (k n)"), ps[:, 0:2].rearrange("p a n -> p (a n)")).then_inc(xT_ready, 1)
                                    act.wait_ge(stored[h], 16 * i + 16)
                                    for m in range(2 * DK):
                                        act.wait_ge(qk_done, 2 * DK * c + m + 1)
                                        nc.scalar.copy(part(h, m, 0), ps[:, 2 + m]).then_inc(hi_ready, 1)
                                    for m in range(2 * DK):
                                        act.wait_ge(rest_ready, 2 * DK * c + m + 1)
                                        nc.scalar.copy(part(h, m, 1), rest[:, m]).then_inc(mid_ready, 1)
                                    act.wait_ge(v_done, c + 1)
                                    nc.scalar.copy(V[:, ds(CT * c, CT), :].rearrange("p t n -> p (t n)"), ps[:, 6:8].rearrange("p a n -> p (a n)")).then_inc(v_kept, 1)

                        @block.gpsimd
                        def _(pool):
                            pool.wait_ge(zero_ready, 1)
                            pool.dma_start(xsort.rearrange("(a p) d -> p a d", p=P), zero[:].unsqueeze(1).broadcast_to([P, MT, D])).then_inc(x_zeroed, 16)
                            pool.sem_inc(lo_ready, 2 * DK)
                            with pool.Fori(0, NC // 2) as i:
                                for h in range(2):
                                    c = 2 * i + h
                                    for m in range(2 * DK):
                                        pool.wait_ge(mid_ready, 2 * DK * c + m + 1)
                                        nc.gpsimd.tensor_tensor(part(h, m, 2), rest[:, m], part(h, m, 1), op=ALU.subtract).then_inc(lo_ready, 1)

                        @block.sync
                        def _(sp):
                            for h in range(2):
                                sp.sem_inc(stored[h], 16)
                            with sp.Fori(0, NC // 2) as i:
                                for h in range(2):
                                    c = 2 * i + h
                                    sp.wait_ge(lo_ready, 2 * DK * (c + 2))
                                    sp.dma_start(pqk[:, :, :, :, ds(CW * c, CW)].rearrange("s a k p n -> p (s a k) n"),
                                                 parts[:, h].rearrange("p s a k n -> p (s a k) n")).then_inc(stored[h], 16)
                            for h in range(2):
                                sp.wait_ge(stored[h], 16 * (NC // 2 + 1))

                        @block.tensor
                        def _(pe):
                            pe.sem_inc(v_kept, 1)
                            with pe.Fori(0, NC // 2) as i:
                                for h in range(2):
                                    c = 2 * i + h
                                    pe.wait_ge(xn_ready, c + 1)
                                    for dk in range(DK):
                                        for k in range(CT):
                                            last = nc.tensor.transpose(ps[:, dk, k * P:(k + 1) * P], xn[:, h, k, dk * P:(dk + 1) * P], ident[:])
                                    last.then_inc(xn_tr, 1)
                                    pe.wait_ge(xT_ready, c + 1)
                                    for m in range(2 * DK):
                                        pe.wait_ge(lo_ready, 2 * DK * c + m + 1)
                                        for dk in range(DK):
                                            last = nc.tensor.matmul(ps[:, 2 + m], wqk[:, m // DK, dk, (m % DK) * P:(m % DK + 1) * P], xT[:, h, dk],
                                                                    start=(dk == 0), stop=(dk == DK - 1))
                                        last.then_inc(qk_done, 1)
                                    pe.wait_ge(v_kept, c + 1)
                                    for k in range(CT):
                                        for dk in range(DK):
                                            last = nc.tensor.matmul(ps[:, 6 + k // 2, (k % 2) * D:(k % 2 + 1) * D], xT[:, h, dk, k * P:(k + 1) * P], wv[:, dk],
                                                                    start=(dk == 0 and k % 2 == 0), stop=(dk == DK - 1), skip_group_check=True)
                                    last.then_inc(v_done, 1)

                with ExitStack() as s2:
                    attention(nc, sem, s2, sbuf, ps, ident, identb, pqk, V, ATT)

            reuse_sems(kept=lasting)

            with ExitStack() as s3:
                stage = sbuf(s3, "stage", [P, 2, CT, D])
                aT = sbuf(s3, "aT", [P, 2, DK, CW])
                staged, at_tr, aT_ready, o_done, o_added = (sem(n) for n in ("staged", "at_tr", "aT_ready", "o_done", "o_added"))
                with nc.Block() as block:
                    @block.gpsimd
                    def _(pool):
                        with pool.Fori(0, NC // 2) as i:
                            for h in range(2):
                                c = 2 * i + h
                                pool.wait_ge(at_tr, c + 1)
                                nc.gpsimd.tensor_copy(stage[:, h].rearrange("p k d -> p (k d)"),
                                                      ATT[:, ds(CT * c, CT), :].rearrange("p k d -> p (k d)")).then_inc(staged, 1)

                    @block.tensor
                    def _(pe):
                        pe.sem_inc(at_tr, 2)
                        with pe.Fori(0, NC // 2) as i:
                            for h in range(2):
                                c = 2 * i + h
                                pe.wait_ge(staged, c + 1)
                                for dk in range(DK):
                                    for k in range(CT):
                                        last = nc.tensor.transpose(ps[:, dk, k * P:(k + 1) * P], stage[:, h, k, dk * P:(dk + 1) * P], ident[:])
                                last.then_inc(at_tr, 1)
                                pe.wait_ge(aT_ready, c + 1)
                                pe.wait_ge(o_added, c + 1)
                                for k in range(CT):
                                    for dk in range(DK):
                                        last = nc.tensor.matmul(ps[:, 2 + 2 * h + k // 2, (k % 2) * D:(k % 2 + 1) * D], aT[:, h, dk, k * P:(k + 1) * P], wo[:, dk],
                                                                start=(dk == 0 and k % 2 == 0), stop=(dk == DK - 1), skip_group_check=True)
                                last.then_inc(o_done, 1)

                    @block.scalar
                    def _(act):
                        with act.Fori(0, NC // 2) as i:
                            for h in range(2):
                                c = 2 * i + h
                                act.wait_ge(at_tr, c + 3)
                                act.wait_ge(o_added, c + 1)
                                nc.scalar.copy(aT[:, h].rearrange("p k n -> p (k n)"), ps[:, 0:2].rearrange("p a n -> p (a n)")).then_inc(aT_ready, 1)
                        layernorm_root_act(act, 1)

                    @block.vector
                    def _(dve):
                        dve.sem_inc(o_added, 2)
                        with dve.Fori(0, NC // 2) as i:
                            for h in range(2):
                                add_chunk(dve, 2 * i + h, 2 + 2 * h, o_done, o_added, 2, xs_steps[0])
                        dve.wait_ge(xs_steps[0], NT)
                        layernorm_scale_dve(dve, 1)

        ffn(nc, sem, sbuf, ps, X, bn, ident, normalise, add_chunk, layernorm_root_act, layernorm_scale_dve, xs_steps,
            fastb_in, wfc_in, wproj_in, u_in, v_in, gate_in, by_k)
        ssm(nc, sem, sbuf, ps, X, bn, ident, normalise, add_chunk, layernorm_root_act, layernorm_scale_dve, xs_steps,
            a_in, bm_in, cm_in, dm_in, lnw_in, lnb_in, wout_in, bout_in, by_k)
        moe(nc, sem, sbuf, ps, X, ident, normalise, xsort, x_zeroed, out_tiles, wg_in, bg_in, bias_in, w1_in, b1_in, w2_in, b2_in)


FH = 1024
FK = FH // P
RANK = 16


def ffn(nc, sem, sbuf, ps, X, bn, ident, normalise, add_chunk, layernorm_root_act, layernorm_scale_dve, xs_steps,
        fastb_in, wfc_in, wproj_in, u_in, v_in, gate_in, by_k):
    with ExitStack() as st:
        wfT = sbuf(st, "wfT", [P, DK, FH])
        wpT = sbuf(st, "wpT", [P, FK, D])
        with ExitStack() as s0:
            wf = sbuf(s0, "wf", [P, FK, D])
            wp = sbuf(s0, "wp", [P, DK, FH])
            u = sbuf(s0, "u", [P, FK, RANK])
            uT = sbuf(s0, "uT", [RANK, FH])
            fb = sbuf(s0, "fb", [RANK, RANK])
            fbT = sbuf(s0, "fbT", [RANK, RANK])
            v = sbuf(s0, "v", [RANK, D])
            fv = sbuf(s0, "fv", [RANK, D])
            gate = sbuf(s0, "gate", [P, 1])
            NR = FK + DK
            sc = sbuf(s0, "sc", [P, 4, NR])
            mag, tp, tn = (sbuf(s0, n, [P, FK * D + DK * FH]) for n in ("magnitude", "above", "ternary"))
            f_loaded, p_loaded, small_loaded = sem("wf_loaded"), sem("wp_loaded"), sem("lowrank_loaded")
            mags, f_steps, f_rows, f_tr, f_lr, f_kept, t_done, t_kept = (
                sem(n) for n in ("ffn_mags", "ffn_steps", "ffn_rows", "lowrank_tr", "lowrank_done", "lowrank_kept", "ffn_w_tr", "ffn_w_kept"))
            rows = ([(wf, k, slice(k * D, (k + 1) * D)) for k in range(FK)]
                    + [(wp, k, slice(FK * D + k * FH, FK * D + (k + 1) * FH)) for k in range(DK)])
            QSTEPS = 4 + 5 * NR
            with nc.Block() as block:
                @block.sync
                def _(sp):
                    sp.dma_start(wf[:], by_k(wfc_in)).then_inc(f_loaded, 16)
                    sp.dma_start(wp[:], by_k(wproj_in)).then_inc(p_loaded, 16)
                    sp.dma_start(u[:], by_k(u_in)).then_inc(small_loaded, 16)
                    sp.dma_start(fb[:], fastb_in).then_inc(small_loaded, 16)
                    sp.dma_start(v[:], v_in).then_inc(small_loaded, 16)
                    sp.dma_start(gate[:], gate_in.partition_broadcast(P)).then_inc(small_loaded, 16)

                @block.scalar
                def _(act):
                    act.wait_ge(f_loaded, 16)
                    for r, (w, k, n) in enumerate(rows):
                        if r == FK:
                            act.wait_ge(p_loaded, 16)
                        nc.scalar.activation(mag[:, n], w[:, k], ACT.Abs, accum_out=sc[:, 0, r:r + 1]).then_inc(mags, 1)
                    act.wait_ge(f_tr, 1)
                    nc.scalar.copy(uT[:], ps[0:RANK, 0:2].rearrange("p a n -> p (a n)")).then_inc(f_kept, 1)
                    nc.scalar.copy(fbT[:], ps[0:RANK, 2, 0:RANK]).then_inc(f_kept, 1)
                    act.wait_ge(f_lr, 1)
                    nc.scalar.copy(fv[:], ps[0:RANK, 3, 0:D]).then_inc(f_kept, 1)
                    for half in range(4):
                        act.wait_ge(t_done, half + 1)
                        o = (wfT[:, half] if half < 2 else wpT[:, :].rearrange("p k d -> p (k d)")[:, (half - 2) * FH:(half - 1) * FH])
                        nc.scalar.copy(o, ps[:, 2 * (half % 2):2 * (half % 2) + 2].rearrange("p a n -> p (a n)")).then_inc(t_kept, 1)

                @block.vector
                def _(dve):
                    steps = Count(f_steps)
                    dve.wait_ge(mags, NR)
                    for a, b, n in ((0, FK, D), (FK, NR, FH)):
                        steps.mark(nc.vector.tensor_scalar(sc[:, 1, a:b], sc[:, 0, a:b], 1.0 / n, 1e-5, ALU.mult, ALU.max))
                    steps.wait(dve)
                    steps.mark(nc.vector.tensor_scalar_mul(sc[:, 2], sc[:, 1], 0.5))
                    steps.mark(nc.vector.tensor_scalar_mul(sc[:, 3], sc[:, 1], -0.5))
                    steps.wait(dve)
                    for r, (w, k, n) in enumerate(rows):
                        steps.mark(nc.vector.tensor_scalar(tp[:, n], w[:, k], sc[:, 2, r:r + 1], None, ALU.is_gt))
                    steps.wait(dve)
                    for r, (w, k, n) in enumerate(rows):
                        steps.mark(nc.vector.scalar_tensor_tensor(tn[:, n], w[:, k], sc[:, 3, r:r + 1], tp[:, n], op0=ALU.is_lt, op1=ALU.subtract))
                    steps.wait(dve)
                    for r, (w, k, n) in enumerate(rows):
                        steps.mark(nc.vector.scalar_tensor_tensor(tp[:, n], tn[:, n], -1.0, w[:, k], op0=ALU.mult, op1=ALU.subtract))
                    steps.wait(dve)
                    for r, (w, k, n) in enumerate(rows):
                        steps.mark(nc.vector.tensor_tensor(tn[:, n], w[:, k], tp[:, n], op=ALU.add))
                    steps.wait(dve)
                    for r, (w, k, n) in enumerate(rows):
                        steps.mark(nc.vector.tensor_scalar(w[:, k], tn[:, n], sc[:, 1, r:r + 1], None, ALU.mult))
                    steps.wait(dve)
                    dve.wait_ge(f_lr, 2)
                    for k in range(FK):
                        nc.vector.scalar_tensor_tensor(wf[:, k], ps[:, 4 + k // 2, (k % 2) * D:(k % 2 + 1) * D], gate[:], wf[:, k],
                                                       op0=ALU.mult, op1=ALU.add).then_inc(f_rows, 1)

                @block.tensor
                def _(pe):
                    pe.wait_ge(small_loaded, 64)
                    for k in range(FK):
                        nc.tensor.transpose(ps[0:RANK, k // 4, (k % 4) * P:(k % 4 + 1) * P], u[:, k], ident[:])
                    nc.tensor.transpose(ps[0:RANK, 2, 0:RANK], fb[:], ident[0:RANK, 0:RANK]).then_inc(f_tr, 1)
                    pe.wait_ge(f_kept, 2)
                    nc.tensor.matmul(ps[0:RANK, 3, 0:D], fbT[:], v[:], start=True, stop=True).then_inc(f_lr, 1)
                    pe.wait_ge(f_kept, 3)
                    for k in range(FK):
                        last = nc.tensor.matmul(ps[:, 4 + k // 2, (k % 2) * D:(k % 2 + 1) * D], uT[:, k * P:(k + 1) * P], fv[:],
                                                start=(k % 2 == 0), stop=True, skip_group_check=True)
                    last.then_inc(f_lr, 1)
                    pe.wait_ge(f_steps, QSTEPS)
                    pe.wait_ge(f_rows, FK)
                    for half in range(4):
                        if half >= 2:
                            pe.wait_ge(t_kept, half - 1)
                        for k in range(FK):
                            bank, col = 2 * (half % 2) + k // 4, (k % 4) * P
                            if half < 2:
                                src = wf[:, k, half * P:(half + 1) * P]
                            else:
                                kk, o = divmod(k + (half - 2) * FK, DK)
                                src = wp[:, o, kk * P:(kk + 1) * P]
                            last = nc.tensor.transpose(ps[:, bank, col:col + P], src, ident[:])
                        last.then_inc(t_done, 1)

        with ExitStack() as s1:
            xn = sbuf(s1, "f_xn", [P, 2, CT, D])
            xT = sbuf(s1, "f_xT", [P, 2, DK, CW])
            relu = sbuf(s1, "relu", [P, 2, CW])
            sq = sbuf(s1, "sq", [P, 2, FK, CW])
            n_ready, n_tr, T_ready, h_done, relu_ready, sq_ready, o_done, o_added = (
                sem("f_" + n) for n in ("n_ready", "n_tr", "T_ready", "h_done", "relu_ready", "sq_ready", "o_done", "o_added"))
            HB = 4
            with nc.Block() as block:
                @block.vector
                def _(dve):
                    def norm(c, h):
                        for k in range(CT):
                            last = normalise(xn[:, h, k, :], CT * c + k)
                        last.then_inc(n_ready, 1)
                    dve.sem_inc(o_added, 1)
                    norm(0, 0)
                    with dve.Fori(0, NC // 2) as i:
                        for h in range(2):
                            c = 2 * i + h
                            norm((c + 1) % NC, 1 - h)
                            for m in range(FK):
                                dve.wait_ge(relu_ready, FK * c + m + 1)
                                nc.vector.tensor_tensor(sq[:, h, m], relu[:, m % 2], relu[:, m % 2], op=ALU.mult).then_inc(sq_ready, 1)
                            add_chunk(dve, c, 6, o_done, o_added, 1, xs_steps[1])
                    dve.wait_ge(xs_steps[1], NT)
                    layernorm_scale_dve(dve, 2)

                @block.scalar
                def _(act):
                    def keep(c, h):
                        act.wait_ge(n_tr, c + 1)
                        nc.scalar.copy(xT[:, h].rearrange("p k n -> p (k n)"), ps[:, 0:2].rearrange("p a n -> p (a n)")).then_inc(T_ready, 1)
                    keep(0, 0)
                    act.sem_inc(sq_ready, HB)
                    with act.Fori(0, NC // 2) as i:
                        for h in range(2):
                            c = 2 * i + h
                            for m in range(FK):
                                act.wait_ge(h_done, FK * c + m + 1)
                                act.wait_ge(sq_ready, FK * c + m + HB - 1)
                                nc.scalar.activation(relu[:, m % 2], ps[:, 2 + m % HB], ACT.Relu).then_inc(relu_ready, 1)
                            keep(c + 1, 1 - h)
                    layernorm_root_act(act, 2)

                @block.tensor
                def _(pe):
                    def turn(c, h):
                        pe.wait_ge(n_ready, c + 1)
                        for dk in range(DK):
                            for k in range(CT):
                                last = nc.tensor.transpose(ps[:, dk, k * P:(k + 1) * P], xn[:, h, k, dk * P:(dk + 1) * P], ident[:])
                        last.then_inc(n_tr, 1)
                    turn(0, 0)
                    with pe.Fori(0, NC // 2) as i:
                        for h in range(2):
                            c = 2 * i + h
                            pe.wait_ge(T_ready, c + 1)
                            for m in range(FK):
                                pe.wait_ge(sq_ready, FK * c + m + 1)
                                for dk in range(DK):
                                    last = nc.tensor.matmul(ps[:, 2 + m % HB], wfT[:, dk, m * P:(m + 1) * P], xT[:, h, dk],
                                                            start=(dk == 0), stop=(dk == DK - 1))
                                last.then_inc(h_done, 1)
                            turn(c + 1, 1 - h)
                            pe.wait_ge(sq_ready, FK * (c + 1) + HB)
                            pe.wait_ge(o_added, c + 1)
                            for k in range(CT):
                                for m in range(FK):
                                    last = nc.tensor.matmul(ps[:, 6 + k // 2, (k % 2) * D:(k % 2 + 1) * D], sq[:, h, m, k * P:(k + 1) * P], wpT[:, m],
                                                            start=(m == 0 and k % 2 == 0), stop=(m == FK - 1), skip_group_check=True)
                            last.then_inc(o_done, 1)


N = 16
GC = P // N
NG = D // GC
SLOT = 4
LEVELS = 7
TPB = SEQ // P
GT_, OB_, PT1_ = range(3)
KEPT = 5


def ssm(nc, sem, sbuf, ps, X, bn, ident, normalise, add_chunk, layernorm_root_act, layernorm_scale_dve, xs_steps,
        a_in, bm_in, cm_in, dm_in, lnw_in, lnb_in, wout_in, bout_in, by_k):
    zline = nc.dram_tensor("toeplitz_lines", [D, 2 * P], F32, kind="Internal").ap()
    with ExitStack() as st:
        S = sbuf(st, "S", [P, NG, KEPT, P])
        mask = sbuf(st, "mask", [P, GC])
        woT = sbuf(st, "woT", [P, DK, D])
        lnwb = sbuf(st, "lnwb", [P, 2, DK])
        bout = sbuf(st, "bout", [P, D])
        turned = sbuf(st, "turned", [P, P])
        c_loaded, small_kept = sem("s_consts_loaded"), sem("s_small_kept")
        with ExitStack() as s0:
            vA = sbuf(s0, "vA", [P, NG, N])
            bB = sbuf(s0, "bB", [P, NG, N])
            ab = sbuf(s0, "ab", [P, NG])
            abt = sbuf(s0, "abt", [P, NG, N])
            rowsB = sbuf(s0, "rowsB", [NG, 2, P])
            rowsD = sbuf(s0, "rowsD", [NG, GC])
            rowsL = sbuf(s0, "rowsL", [DK, 2, P])
            vBC = sbuf(s0, "vBC", [P, 2, NG])
            dcol = sbuf(s0, "dcol", [GC, NG])
            rowBC = sbuf(s0, "rowBC", [GC, 2, NG, N])
            cb = sbuf(s0, "cb", [GC, NG, N])
            k0 = sbuf(s0, "k0", [GC, NG])
            wo = sbuf(s0, "wo_rows", [P, DK, D])
            W1 = sbuf(s0, "W1", [P, SLOT, 2 * P])
            W2 = sbuf(s0, "W2", [P, SLOT, 2 * P])
            Cbd = sbuf(s0, "Cbd", [P, SLOT, GC])
            zk = sbuf(s0, "zk", [GC, 2, SLOT, P])
            zero = sbuf(s0, "zeros", [P, DK, P])
            a_loaded, bc_loaded, z_zeroed, z_turn, t_steps, mz, mask_ready, zero_ready = (
                sem(n) for n in ("s_a_loaded", "s_bc_loaded", "z_zeroed", "z_turn", "turned_steps", "mask_steps", "mask_ready", "zero_ready"))
            bc_tr, wo_tr, ab_steps, built, o_copied, k_done, k_kept, gt_done, gt_kept = (
                sem(n) for n in ("s_bc_tr", "s_wo_tr", "ab_steps", "s_built", "s_o_copied", "s_k_done", "s_k_kept", "s_gt_done", "s_gt_kept"))
            stored = [sem(f"z_stored{h}") for h in range(2)]
            lv, w1r, w2r = ([sem(f"s_{n}{h}") for h in range(2)] for n in ("level", "w1_ready", "w2_ready"))
            HS = SLOT // 2
            NB = NG // SLOT
            LV, W1N, W2N = LEVELS + 3, LEVELS + 1, LEVELS + 3
            with nc.Block() as block:
                @block.sync
                def _(sp):
                    sp.dma_start(rowsB[:, 0], bm_in.rearrange("(g c) n -> g (c n)", c=GC)).then_inc(bc_loaded, 16)
                    sp.dma_start(rowsB[:, 1], cm_in.rearrange("(g c) n -> g (c n)", c=GC)).then_inc(bc_loaded, 16)
                    sp.dma_start(vA[:], a_in.rearrange("(g c) n m -> (c n) g m", c=GC)).then_inc(a_loaded, 16)
                    sp.dma_start(rowBC[:, 0], bm_in.rearrange("(g c) n -> c g n", c=GC)).then_inc(a_loaded, 16)
                    sp.dma_start(rowBC[:, 1], cm_in.rearrange("(g c) n -> c g n", c=GC)).then_inc(a_loaded, 16)
                    for c in range(GC):
                        sp.dma_start(bB[c * N:(c + 1) * N], bm_in.rearrange("(g c) m -> c g m", c=GC)[c].partition_broadcast(N)).then_inc(a_loaded, 16)
                    sp.dma_start(rowsD[:], dm_in.rearrange("(g c) -> g c", c=GC)).then_inc(bc_loaded, 16)
                    sp.dma_start(rowsL[:, 0], lnw_in.rearrange("(k p) -> k p", p=P)).then_inc(bc_loaded, 16)
                    sp.dma_start(rowsL[:, 1], lnb_in.rearrange("(k p) -> k p", p=P)).then_inc(bc_loaded, 16)
                    sp.dma_start(wo[:], by_k(wout_in)).then_inc(c_loaded, 16)
                    sp.dma_start(bout[:], bout_in.partition_broadcast(P)).then_inc(c_loaded, 16)
                    sp.wait_ge(zero_ready, 1)
                    sp.dma_start(zline.rearrange("(k p) n -> p k n", p=P)[:, :, P:2 * P], zero[:]).then_inc(z_zeroed, 16)
                    for h in range(2):
                        sp.sem_inc(stored[h], 16)
                    with sp.Fori(0, NB // 2) as i:
                        for h in range(2):
                            b = 2 * i + h
                            sp.wait_ge(k_kept, 2 * b + 4)
                            sp.sem_inc(z_turn, 1)
                            sp.dma_start(zline.rearrange("(g c) n -> c g n", c=GC)[:, ds(SLOT * b, SLOT), 0:P], zk[:, h]).then_inc(stored[h], 16)
                    for h in range(2):
                        sp.wait_ge(stored[h], 16 * (NB // 2 + 1))
                    sp.wait_ge(z_zeroed, 16)

                @block.gpsimd
                def _(pool):
                    nc.gpsimd.memset(zero[:], 0.0).then_inc(zero_ready, 1)
                    nc.gpsimd.memset(mask[:], 1.0).then_inc(mz, 1)
                    nc.gpsimd.memset(turned[:], 0.0).then_inc(t_steps, 1)
                    pool.wait_ge(t_steps, 1)
                    nc.gpsimd.affine_select(out=turned[:], in_=turned[:], compare_op=ALU.not_equal, fill=1.0, base=1 - P,
                                            pattern=[[1, P]], channel_multiplier=1).then_inc(t_steps, 1)
                    pool.wait_ge(mz, 1)
                    nc.gpsimd.affine_select(out=mask[:], in_=mask[:], compare_op=ALU.is_ge, fill=0.0, base=0,
                                            pattern=[[-N, GC]], channel_multiplier=1).then_inc(mz, 1)
                    pool.wait_ge(mz, 2)
                    nc.gpsimd.affine_select(out=mask[:], in_=mask[:], compare_op=ALU.is_ge, fill=0.0, base=N - 1,
                                            pattern=[[N, GC]], channel_multiplier=-1).then_inc(mask_ready, 1)
                    with pool.Fori(0, NB) as b:
                        for h in range(2):
                            pool.wait_ge(w2r[h], W2N * b + LEVELS + 2)
                            nc.gpsimd.tensor_copy(S[:, ds(SLOT * b + HS * h, HS), OB_], W2[:, HS * h:HS * h + HS, 0:P]).then_inc(o_copied, 1)

                def group(t, h):
                    return t[:, HS * h:HS * h + HS]

                def pair(side, h):
                    return ps[:, 2 * h + side].rearrange("p (s n) -> p s n", s=HS)

                @block.vector
                def _(dve):
                    dve.wait_ge(a_loaded, 16 * (GC + 3))
                    nc.vector.tensor_tensor(abt[:], vA[:], bB[:], op=ALU.mult).then_inc(ab_steps, 1)
                    dve.wait_ge(ab_steps, 1)
                    nc.vector.reduce_sum(ab[:], abt[:], AX).then_inc(ab_steps, 1)
                    dve.wait_ge(ab_steps, 2)
                    dve.wait_ge(bc_tr, 1)
                    nc.vector.tensor_copy(vBC[:].rearrange("p s g -> p (s g)"), ps[:, 7, 0:2 * NG]).then_inc(ab_steps, 1)
                    nc.vector.tensor_copy(dcol[:], ps[0:GC, 7, 2 * NG:3 * NG]).then_inc(ab_steps, 1)
                    nc.vector.tensor_copy(lnwb[:].rearrange("p s k -> p (s k)"), ps[:, 7, 3 * NG:3 * NG + 2 * DK]).then_inc(ab_steps, 1)
                    nc.vector.tensor_tensor(cb[:], rowBC[:, 0], rowBC[:, 1], op=ALU.mult).then_inc(ab_steps, 1)
                    dve.wait_ge(ab_steps, 6)
                    nc.vector.reduce_sum(k0[:], cb[:], AX).then_inc(ab_steps, 1)
                    dve.wait_ge(ab_steps, 7)
                    nc.vector.tensor_tensor(k0[:], k0[:], dcol[:], op=ALU.add).then_inc(ab_steps, 1)
                    dve.wait_ge(ab_steps, 8)
                    dve.wait_ge(mask_ready, 1)

                    with dve.Fori(0, NB // 2) as i:
                        for z in range(2):
                            b = 2 * i + z
                            these = ds(SLOT * b, SLOT)
                            dve.wait_ge(o_copied, 2 * b + 2)
                            for h in range(2):
                                dve.wait_ge(w2r[h], W2N * b + 1)
                            spread = mask[:].unsqueeze(1).broadcast_to([P, SLOT, GC])
                            nc.vector.tensor_tensor(W1[:, :, P:2 * P].rearrange("p s (c n) -> p s c n", n=N),
                                                    vA[:, these, :].unsqueeze(2).broadcast_to([P, SLOT, GC, N]),
                                                    spread.unsqueeze(3).broadcast_to([P, SLOT, GC, N]), op=ALU.mult)
                            nc.vector.tensor_copy(W1[:, :, P - 1], ab[:, these])
                            nc.vector.tensor_copy(W2[:, :, P - 1], vBC[:, 1, these])
                            nc.vector.tensor_tensor(Cbd[:], vBC[:, 1, these].unsqueeze(2).broadcast_to([P, SLOT, GC]), spread, op=ALU.mult).then_inc(built, 1)
                            for l in range(LEVELS + 1):
                                m = 1 << l
                                for h in range(2):
                                    dve.wait_ge(lv[h], LV * b + l + 2)
                                    src, dst = pair(0, h), group(W1, h)
                                    if l < LEVELS:
                                        nc.vector.tensor_copy(dst[:, :, P - 2 * m:P - m], src[:, :, 0:m])
                                    o = m if l < LEVELS else 0
                                    nc.vector.tensor_copy(dst[:, :, P:2 * P], src[:, :, o:o + P]).then_inc(w1r[h], 1)
                            for h in range(2):
                                dve.wait_ge(gt_done, 2 * b + h + 1)
                                nc.vector.tensor_copy(S[:, ds(SLOT * b + HS * h, HS), GT_], ps[:, 4 + h, 0:HS * P].rearrange("p (s n) -> p s n", n=P)).then_inc(gt_kept, 1)
                            dve.wait_ge(k_done, b + 1)
                            dve.wait_ge(stored[z], 16 * i + 16)
                            k = ps[0:GC, 6].rearrange("p (s n) -> p s n", n=P)
                            nc.vector.tensor_copy(zk[:, z, :, 0:P - 1], k[:, :, 1:P]).then_inc(k_kept, 1)
                            nc.vector.tensor_copy(zk[:, z, :, P - 1:P], k0[:, these].unsqueeze(2)).then_inc(k_kept, 1)

                @block.scalar
                def _(act):
                    act.wait_ge(wo_tr, 1)
                    nc.scalar.copy(woT[:].rearrange("p k n -> p (k n)"), ps[:, 5]).then_inc(small_kept, 1)
                    act.sem_inc(o_copied, 2)
                    for h in range(2):
                        act.sem_inc(w2r[h], 1)
                    with act.Fori(0, NB) as b:
                        for h in range(2):
                            act.wait_ge(lv[h], LV * b + 1)
                            nc.scalar.copy(group(W2, h)[:, :, P:2 * P], pair(1, h)[:, :, 0:P]).then_inc(w2r[h], 1)
                        for l in range(LEVELS + 2):
                            m = 1 << l
                            for h in range(2):
                                act.wait_ge(lv[h], LV * b + l + 2)
                                src, dst = pair(1, h), group(W2, h)
                                o = m if l < LEVELS else 0
                                if l < LEVELS:
                                    nc.scalar.copy(dst[:, :, P - 2 * m:P - m], src[:, :, 0:m])
                                if l >= LEVELS - 1:
                                    last = nc.scalar.copy(S[:, ds(SLOT * b + HS * h, HS), PT1_ + l - LEVELS + 1], src[:, :, o:o + P])
                                if l <= LEVELS:
                                    last = nc.scalar.copy(dst[:, :, P:2 * P], src[:, :, o:o + P])
                                last.then_inc(w2r[h], 1)

                @block.tensor
                def _(pe):
                    pe.wait_ge(bc_loaded, 80)
                    for s in range(2):
                        nc.tensor.transpose(ps[:, 7, s * NG:(s + 1) * NG], rowsB[:, s], ident[0:NG, 0:NG])
                    nc.tensor.transpose(ps[0:GC, 7, 2 * NG:3 * NG], rowsD[:], ident[0:NG, 0:NG])
                    for s in range(2):
                        last = nc.tensor.transpose(ps[:, 7, 3 * NG + s * DK:3 * NG + (s + 1) * DK], rowsL[:, s], ident[0:DK, 0:DK])
                    last.then_inc(bc_tr, 1)
                    pe.wait_ge(c_loaded, 32)
                    for dk in range(DK):
                        for o in range(DK):
                            last = nc.tensor.transpose(ps[:, 5, dk * D + o * P:dk * D + (o + 1) * P], wo[:, o, dk * P:(dk + 1) * P], ident[:])
                    last.then_inc(wo_tr, 1)
                    pe.wait_ge(small_kept, 1)
                    pe.sem_inc(gt_kept, 2)
                    pe.sem_inc(k_kept, 2)
                    with pe.Fori(0, NB) as b:
                        pe.wait_ge(built, b + 1)
                        for h in range(2):
                            pe.wait_ge(w2r[h], W2N * b + 1)
                            for s in range(HS * h, HS * h + HS):
                                last = nc.tensor.transpose(pair(1, h)[:, s - HS * h, 0:P], W1[:, s, P:2 * P], ident[:])
                            last.then_inc(lv[h], 1)
                        for l in range(LEVELS + 2):
                            m = 1 << l
                            if l == LEVELS:
                                for h in range(2):
                                    pe.wait_ge(w1r[h], W1N * b + l)
                                    pe.wait_ge(gt_kept, 2 * b + h + 1)
                                    for s in range(HS):
                                        last = nc.tensor.transpose(ps[:, 4 + h, s * P:(s + 1) * P], W1[:, HS * h + s, 0:P], ident[:])
                                    last.then_inc(gt_done, 1)
                                pe.wait_ge(k_kept, 2 * b + 2)
                                for s in range(SLOT):
                                    last = nc.tensor.matmul(ps[0:GC, 6, s * P:(s + 1) * P], Cbd[:, s], W1[:, s, 0:P], start=True, stop=True, skip_group_check=True)
                                last.then_inc(k_done, 1)
                            for h in range(2):
                                if l > 0:
                                    pe.wait_ge(w1r[h], W1N * b + l)
                                pe.wait_ge(w2r[h], W2N * b + l + 2)
                                for s in range(HS * h, HS * h + HS):
                                    p, pt = W1[:, s, P:2 * P], W2[:, s, P:2 * P]
                                    if l <= LEVELS:
                                        c = m if l < LEVELS else 0
                                        nc.tensor.matmul(pair(0, h)[:, s - HS * h, 0:c + P], pt, W1[:, s, P - c:2 * P], start=True, stop=True, skip_group_check=True)
                                    c = m if l < LEVELS else 0
                                    last = nc.tensor.matmul(pair(1, h)[:, s - HS * h, 0:c + P], p, W2[:, s, P - c:2 * P], start=True, stop=True, skip_group_check=True)
                                last.then_inc(lv[h], 1)

        with ExitStack() as s1:
            Y = sbuf(s1, "Y", [P, NT, D])
            ssm_tiles(nc, sem, sbuf, ps, X, Y, S, zline, mask, bout, ident, normalise)
            ssm_output(nc, sem, sbuf, ps, X, Y, bn, ident, normalise, add_chunk, layernorm_root_act, layernorm_scale_dve, xs_steps, woT, lnwb, turned)


def ssm_tiles(nc, sem, sbuf, ps, X, Y, S, zline, mask, bout, ident, normalise):
    NB, PAIRS = NG // SLOT, SLOT // 2
    with ExitStack() as st:
        TB = sbuf(st, "TB", [P, 2, SLOT, GC, P])
        SG = sbuf(st, "SG", [P, SLOT, KEPT, P])
        xs = sbuf(st, "xs", [P, SLOT, GC, NT])
        yl = sbuf(st, "yl", [P, SLOT, 2, P])
        gm = sbuf(st, "gm", [P, 2, GC, NT])
        hs = sbuf(st, "hs", [P, SLOT, NT])
        hm = sbuf(st, "hm", [P, SLOT, GC, BATCH, TPB])
        xn_done, x_steps, hmz = (sem("t_" + n) for n in ("xn_done", "x_steps", "hm_zeroed"))
        loaded = [[sem(f"t_loaded{z}{j}") for j in range(SLOT)] for z in range(2)]
        xs_ready, g_done, g_steps, T_done, T_kept, ks_done, hs_ready, hm_ready, y_done, y_kept = (
            sem("t_" + n) for n in ("xs_ready", "g_done", "g_steps", "T_done", "T_kept", "ks_done", "hs_ready", "hm_ready", "y_done", "y_kept"))
        G_BANK, T_BANK, Y_BANK, SCAN_BANKS = 0, 2, 4, (6, 7)
        W = GC * NT
        slot = lambda bank, j: ps[:, bank + j // 2, (j % 2) * W:(j % 2 + 1) * W]
        of = lambda p: range(2 * p, 2 * p + 2)
        STEPS = [1, 2, 4]
        NS = len(STEPS)
        scan = lambda p, d: (ps[:, SCAN_BANKS[p], 0:2 * NT].rearrange("p (s n) -> p s n", s=2)[:, :, 0:BATCH * (TPB - 1 - d)])
        with nc.Block() as block:
            @block.sync
            def _(sp):
                sp.sem_inc(y_done, 2 * PAIRS)
                with sp.Fori(0, NB // 2) as i:
                    for z in range(2):
                        b = 2 * i + z
                        for j in range(SLOT):
                            g = SLOT * b + j
                            line = zline.rearrange("(g c) n -> g c n", c=GC)[ds(g, 1), :, 0:P]
                            sp.wait_ge(y_done, PAIRS * b + j // 2 + 1)
                            sp.sem_inc(loaded[z][j], 16)
                            sp.dma_start(TB[:, z, j], toeplitz(line)).then_inc(loaded[z][j], 16)
                            sp.wait_ge(y_done, PAIRS * b + j // 2 + PAIRS + 1)
                            sp.sem_inc(loaded[z][j], 16)
                            sp.dma_start(SG[:, j], S[:, ds(g, 1)].rearrange("p a k n -> p (a k) n")).then_inc(loaded[z][j], 16)

            @block.vector
            def _(dve):
                nc.vector.memset(hm[:], 0.0).then_inc(hmz, 1)
                with dve.Fori(0, NT) as t:
                    normalise(Y[:, ds(t, 1), :].rearrange("p a d -> p (a d)"), t).then_inc(xn_done, 1)
                dve.wait_ge(xn_done, NT)
                with dve.Fori(0, NT // 2) as t:
                    two = lambda v: v[:, ds(2 * t, 2), :].rearrange("p a d -> p (a d)")
                    nc.vector.tensor_tensor(two(X), two(X), two(Y), op=ALU.add).then_inc(x_steps, 1)
                dve.wait_ge(hmz, 1)
                with dve.Fori(0, NB) as b:
                    for p in range(PAIRS):
                        u = PAIRS * b + p
                        dve.wait_ge(g_done, u + 1)
                        if p > 0:
                            dve.wait_ge(hs_ready, PAIRS * (NS + 1) * b + p)
                        for j in of(p):
                            nc.vector.tensor_tensor(gm[:, j % 2], slot(G_BANK, j).rearrange("p (c t) -> p c t", c=GC),
                                                    mask[:].unsqueeze(2).broadcast_to([P, GC, NT]), op=ALU.mult).then_inc(g_steps, 1)
                        dve.wait_ge(g_steps, 2 * u + 2)
                        nc.vector.reduce_sum(hs[:, 2 * p:2 * p + 2], gm[:].rearrange("p s c t -> p s t c"), AX).then_inc(hs_ready, 1)
                    for k, d in enumerate(STEPS):
                        for p in range(PAIRS):
                            dve.wait_ge(ks_done, PAIRS * (NS * b + k) + p + 1)
                            dve.wait_ge(hs_ready, PAIRS * ((NS + 1) * b + k) + p + 1)
                            v = hs[:, 2 * p:2 * p + 2].rearrange("p s (b c) -> p s b c", b=BATCH)[:, :, :, d:TPB - 1]
                            nc.vector.tensor_tensor(v, scan(p, d).rearrange("p s (b c) -> p s b c", b=BATCH), v, op=ALU.add).then_inc(hs_ready, 1)
                    for p in range(PAIRS):
                        dve.wait_ge(hs_ready, PAIRS * ((NS + 1) * b + NS) + p + 1)
                        dve.wait_ge(y_done, PAIRS * b + p + PAIRS + 1)
                        for j in of(p):
                            before = hs[:, j].rearrange("p (b c) -> p b c", b=BATCH)[:, :, 0:TPB - 1]
                            nc.vector.tensor_tensor(hm[:, j, :, :, 1:TPB], before.unsqueeze(1).broadcast_to([P, GC, BATCH, TPB - 1]),
                                                    mask[:].unsqueeze(2).unsqueeze(3).broadcast_to([P, GC, BATCH, TPB - 1]), op=ALU.mult).then_inc(hm_ready, 1)

            @block.gpsimd
            def _(pool):
                pool.wait_ge(x_steps, NT // 2)
                with pool.Fori(0, NB) as b:
                    for j in range(SLOT):
                        pool.wait_ge(y_done, PAIRS * b + j // 2 + PAIRS + 1)
                        nc.gpsimd.tensor_copy(xs[:, j], Y[:, :, ds(GC * (SLOT * b + j), GC)].rearrange("p t c -> p c t")).then_inc(xs_ready, 1)
                    tiles = ds(NT // NB * b, NT // NB)
                    nc.gpsimd.tensor_tensor(X[:, tiles, :], X[:, tiles, :], bout[:].unsqueeze(1).broadcast_to([P, NT // NB, D]), op=ALU.add)

            @block.scalar
            def _(act):
                with act.Fori(0, NB) as b:
                    for p in range(PAIRS):
                        act.wait_ge(T_done, PAIRS * b + p + 1)
                        act.wait_ge(y_done, PAIRS * b + p + PAIRS + 1)
                        nc.scalar.copy(yl[:, 2 * p:2 * p + 2].rearrange("p s q n -> p (s q n)"), ps[:, T_BANK + p]).then_inc(T_kept, 1)
                    for p in range(PAIRS):
                        act.wait_ge(y_done, PAIRS * b + p + 2 * PAIRS + 1)
                        nc.scalar.copy(Y[:, :, ds(GC * (SLOT * b + 2 * p), 2 * GC)], ps[:, Y_BANK + p].rearrange("p (c t) -> p t c", t=NT)).then_inc(y_kept, 1)

            @block.tensor
            def _(pe):
                pe.sem_inc(y_kept, PAIRS)
                with pe.Fori(0, NB // 2) as i:
                    for z in range(2):
                        b = 2 * i + z
                        for p in range(PAIRS):
                            for j in of(p):
                                pe.wait_ge(xs_ready, SLOT * b + j + 1)
                                pe.wait_ge(loaded[z][j], 64 * i + 64)
                                last = nc.tensor.matmul(slot(G_BANK, j), SG[:, j, GT_], xs[:, j].rearrange("p c t -> p (c t)"), start=True, stop=True, skip_group_check=True)
                            last.then_inc(g_done, 1)
                        for p in range(PAIRS):
                            for j in of(p):
                                for q in range(2):
                                    for c in range(4):
                                        last = nc.tensor.matmul(slot(T_BANK, j)[NT * c:NT * (c + 1), q * P:(q + 1) * P],
                                                                xs[:, j, 4 * q + c], TB[:, z, j, 4 * q + c], start=True, stop=True, skip_group_check=True)
                            last.then_inc(T_done, 1)
                        for k, d in enumerate(STEPS):
                            for p in range(PAIRS):
                                pe.wait_ge(hs_ready, PAIRS * ((NS + 1) * b + k) + p + 1)
                                for j in of(p):
                                    last = nc.tensor.matmul(scan(p, d)[:, j % 2], SG[:, j, PT1_ + k],
                                                            hs[:, j].rearrange("p (b c) -> p b c", b=BATCH)[:, :, 0:TPB - 1 - d], start=True, stop=True, skip_group_check=True)
                                last.then_inc(ks_done, 1)
                        for p in range(PAIRS):
                            pe.wait_ge(T_kept, PAIRS * b + p + 1)
                            pe.wait_ge(y_kept, PAIRS * b + p + 1)
                            for j in of(p):
                                pe.wait_ge(hm_ready, SLOT * b + j + 1)
                                nc.tensor.matmul(slot(Y_BANK, j), SG[:, j, OB_], hm[:, j].rearrange("p c b t -> p (c b t)"), start=True, stop=False, skip_group_check=True)
                                for q in range(2):
                                    last = nc.tensor.matmul(slot(Y_BANK, j)[:, q * P:(q + 1) * P], yl[:, j, q], ident[:], start=False, stop=(q == 1), skip_group_check=True)
                            last.then_inc(y_done, 1)


def toeplitz(line):
    a = line.rearrange("a c n -> (a c) n")
    return bass.AP(tensor=a.tensor, offset=a.offset, ap=[[1, P], *a.ap])


def ssm_output(nc, sem, sbuf, ps, X, Y, bn, ident, normalise, add_chunk, layernorm_root_act, layernorm_scale_dve, xs_steps, woT, lnwb, turned):
    with ExitStack() as st:
        yn = sbuf(st, "yn", [P, 2, CT, D])
        gT = sbuf(st, "gT", [P, 2, DK, CW])
        y_steps, n_ready, n_tr, g_ready, o_done, o_added = (sem("so_" + n) for n in ("y_steps", "n_ready", "n_tr", "g_ready", "done", "added"))
        with nc.Block() as block:
            @block.vector
            def _(dve):
                with dve.Fori(0, NT) as t:
                    nc.vector.bn_stats(bn[:, ds(t, 1), :].rearrange("p a s -> p (a s)"), Y[:, ds(t, 1), :].rearrange("p a d -> p (a d)")).then_inc(y_steps, 1)
                dve.wait_ge(y_steps, NT)
                layernorm_scale_dve(dve, 4)

                def norm(c, h):
                    for k in range(CT):
                        last = normalise(yn[:, h, k, :], CT * c + k, Y)
                    last.then_inc(n_ready, 1)
                dve.sem_inc(o_added, 2)
                norm(0, 0)
                with dve.Fori(0, NC // 2) as i:
                    for h in range(2):
                        c = 2 * i + h
                        norm((c + 1) % NC, 1 - h)
                        add_chunk(dve, c, 4 + 2 * h, o_done, o_added, 2, xs_steps[2])
                dve.wait_ge(xs_steps[2], NT)
                layernorm_scale_dve(dve, 3)

            @block.scalar
            def _(act):
                layernorm_root_act(act, 4)
                with act.Fori(0, NC // 2) as i:
                    for h in range(2):
                        c = 2 * i + h
                        act.wait_ge(n_tr, c + 1)
                        act.wait_ge(o_added, c + 1)
                        for dk in range(DK):
                            nc.scalar.activation(gT[:, h, dk], ps[:, 2 * h + dk], ACT.Gelu, bias=lnwb[:, 1, dk:dk + 1], scale=lnwb[:, 0, dk:dk + 1]).then_inc(g_ready, 1)
                layernorm_root_act(act, 3)

            @block.tensor
            def _(pe):
                def turn(c, h):
                    pe.wait_ge(n_ready, c + 1)
                    for dk in range(DK):
                        for k in range(CT):
                            last = nc.tensor.matmul(ps[:, 2 * h + dk, k * P:(k + 1) * P], yn[:, h, k, dk * P:(dk + 1) * P], turned[:],
                                                    start=True, stop=True, skip_group_check=True)
                    last.then_inc(n_tr, 1)
                turn(0, 0)
                with pe.Fori(0, NC // 2) as i:
                    for h in range(2):
                        c = 2 * i + h
                        turn(c + 1, 1 - h)
                        pe.wait_ge(g_ready, DK * (c + 1))
                        pe.wait_ge(o_added, c + 1)
                        for k in range(CT):
                            for dk in range(DK):
                                last = nc.tensor.matmul(ps[:, 4 + 2 * h + k // 2, (k % 2) * D:(k % 2 + 1) * D], gT[:, h, dk, k * P:(k + 1) * P], woT[:, dk],
                                                        start=(dk == 0 and k % 2 == 0), stop=(dk == DK - 1), skip_group_check=True)
                        last.then_inc(o_done, 1)


def moe(nc, sem, sbuf, ps, X, ident, normalise, xsort, x_zeroed, out_tiles, wg_in, bg_in, bias_in, w1_in, b1_in, w2_in, b2_in):
    ysort = nc.dram_tensor("outputs_by_expert", [MT * P, D], F32, kind="Internal").ap()
    with ExitStack() as st:
        W1 = sbuf(st, "eW1", [P, E, DK, EH])
        W2 = sbuf(st, "eW2", [P, E, EK, D])
        b1T = sbuf(st, "b1T", [P, E * EK])
        slot = sbuf(st, "slot", [P, 2, NT], U32)
        weight = sbuf(st, "weight", [P, 2, NT])
        owner = sbuf(st, "owner", [P, MT], I32)
        w_loaded = [sem(f"e_w_loaded{q}") for q in range(2)]
        placed = sem("e_placed")
        with ExitStack() as s0:
            xc = sbuf(s0, "e_xn", [P, 2, CT, D])
            xT = sbuf(s0, "e_xT", [P, 2, DK, CW])
            wg = sbuf(s0, "wg", [P, DK, E])
            bgb = sbuf(s0, "bgb", [P, 2, E])
            b1r = sbuf(s0, "b1r", [E * EK, P])
            L, hot1, hot2, tmp, S, C, C2 = (sbuf(s0, "r_" + n, [P, NT, E]) for n in ("logits", "hot1", "hot2", "tmp", "slots", "sums", "sums2"))
            top, at = (sbuf(s0, "r_" + n, [P, 2, NT]) for n in ("top", "at"))
            ex = sbuf(s0, "r_exp", [P, 3, NT])
            place = sbuf(s0, "r_place", [P, 2, 2, CT], U32)
            held = sbuf(s0, "r_held", [P, MT, E])
            ended = sbuf(s0, "r_ended", [P, MT])
            ne = sbuf(s0, "r_ne", [P, 4, E])
            ni = sbuf(s0, "r_ni", [P, 2, E], I32)
            ei, ti = sbuf(s0, "r_ei", [P, E], I32), sbuf(s0, "r_ti", [P, MT], I32)
            ef, tf = sbuf(s0, "r_ef", [P, E]), sbuf(s0, "r_tf", [P, MT])
            before, ones = sbuf(s0, "r_before", [P, P]), sbuf(s0, "r_ones", [P, P])
            small, xc_ready, x_tr, xT_ready, lg_done, b1_tr, b1_kept, r_steps, r_exp, c_ready, c_done, iotas = (
                sem("r_" + n) for n in ("small_loaded", "xn_ready", "x_tr", "xT_ready", "logits_done", "b1_tr", "b1_kept", "steps", "exp", "consts", "counted", "iotas"))
            hot_ready, gap_ready, slots_ready, row_ready, scatter_turn = (sem("r_" + n) for n in ("hot_ready", "gap_ready", "slots_ready", "row_ready", "scatter_turn"))
            scattered = [sem(f"r_scattered{h}") for h in range(2)]
            with nc.Block() as block:
                @block.sync
                def _(sp):
                    sp.dma_start(wg[:], wg_in.rearrange("(k p) e -> p k e", p=P)).then_inc(small, 16)
                    sp.dma_start(bgb[:, 0], bg_in.partition_broadcast(P)).then_inc(small, 16)
                    sp.dma_start(bgb[:, 1], bias_in.partition_broadcast(P)).then_inc(small, 16)
                    sp.dma_start(b1r[:], b1_in.rearrange("e (k p) -> (e k) p", p=P)).then_inc(small, 16)
                    for q in range(4):
                        es = slice(q * E // 4, (q + 1) * E // 4)
                        sp.dma_start(W1[:, es], w1_in[es].rearrange("e (k p) h -> p e k h", p=P)).then_inc(w_loaded[0], 16)
                        sp.dma_start(W2[:, es], w2_in[es].rearrange("e (k p) d -> p e k d", p=P)).then_inc(w_loaded[1], 16)

                @block.gpsimd
                def _(pool):
                    nc.gpsimd.memset(ones[:], 1.0).then_inc(c_ready, 1)
                    pool.wait_ge(c_ready, 1)
                    nc.gpsimd.affine_select(out=before[:], in_=ones[:], compare_op=ALU.is_ge, fill=0.0, base=-1,
                                            pattern=[[1, P]], channel_multiplier=-1).then_inc(c_ready, 1)
                    nc.gpsimd.iota(ei[:], pattern=[[1, E]], base=-E, channel_multiplier=0).then_inc(iotas, 1)
                    nc.gpsimd.iota(ti[:], pattern=[[1, MT]], base=0, channel_multiplier=0).then_inc(iotas, 1)
                    pool.wait_ge(x_zeroed, 16)
                    pool.wait_ge(slots_ready, 2)
                    with pool.Fori(0, NC // 2) as i:
                        for h in range(2):
                            c = 2 * i + h
                            pool.wait_ge(row_ready, c + 1)
                            pool.sem_inc(scatter_turn, 1)
                            for k in range(CT):
                                for s in range(2):
                                    nc.gpsimd.indirect_dma_start(xsort, bass.IndirectOffsetOnAxis(ap=place[:, h, s, k:k + 1], axis=0),
                                                                 xc[:, h, k], None).then_inc(scattered[h], 16)
                    for h in range(2):
                        pool.wait_ge(scattered[h], 16 * 2 * CT * (NC // 2))

                @block.vector
                def _(dve):
                    def norm(c, h, ready):
                        for k in range(CT):
                            last = normalise(xc[:, h, k], CT * c + k)
                        last.then_inc(ready, 1)
                    norm(0, 0, xc_ready)
                    with dve.Fori(0, NC // 2) as i:
                        for h in range(2):
                            c = 2 * i + h
                            dve.wait_ge(x_tr, c + 1)
                            norm((c + 1) % NC, 1 - h, xc_ready)
                    dve.wait_ge(b1_tr, 1)
                    nc.vector.tensor_copy(b1T[:], ps[:, 7, 0:E * EK]).then_inc(b1_kept, 1)
                    steps = Count(r_steps)

                    def step(ins):
                        steps.mark(ins)
                        steps.wait(dve)
                    of_e = lambda v: v.unsqueeze(1).broadcast_to([P, NT, E])
                    of_t = lambda v: v.unsqueeze(2).broadcast_to([P, NT, E])
                    dve.wait_ge(iotas, 2)
                    steps.mark(nc.vector.tensor_copy(ef[:], ei[:]))
                    step(nc.vector.tensor_copy(tf[:], ti[:]))
                    dve.wait_ge(small, 64)
                    dve.wait_ge(lg_done, NC)
                    step(nc.vector.tensor_tensor(L[:], ps[:, 4].rearrange("p (t e) -> p t e", e=E), of_e(bgb[:, 0]), op=ALU.add))
                    step(nc.vector.tensor_tensor(L[:], L[:], of_e(bgb[:, 1]), op=ALU.add))
                    for s, hot in enumerate((hot1, hot2)):
                        step(nc.vector.reduce_max(top[:, s], L[:], AX))
                        step(nc.vector.tensor_tensor(tmp[:], L[:], of_t(top[:, s]), op=ALU.is_equal))
                        step(nc.vector.tensor_tensor(tmp[:], tmp[:], of_e(ef[:]), op=ALU.mult))
                        step(nc.vector.tensor_reduce(at[:, s], tmp[:], AX, ALU.min))
                        step(nc.vector.tensor_tensor(hot[:], of_t(at[:, s]), of_e(ef[:]), op=ALU.is_equal))
                        if s == 0:
                            step(nc.vector.scalar_tensor_tensor(L[:], hot[:], -3e38, L[:], op0=ALU.mult, op1=ALU.add))
                    nc.vector.tensor_tensor(tmp[:], hot1[:], hot2[:], op=ALU.add).then_inc(hot_ready, 1)
                    nc.vector.tensor_tensor(ex[:, 0], top[:, 1], top[:, 0], op=ALU.subtract).then_inc(gap_ready, 1)
                    dve.wait_ge(c_done, 1)
                    tot = ps[:, 6].rearrange("p (t e) -> p t e", e=E)
                    pre = ps[:, 5].rearrange("p (t e) -> p t e", e=E)
                    step(nc.vector.tensor_copy(C[:], tot))
                    a, b, d = C, C2, 1
                    while d < NT:
                        steps.mark(nc.vector.tensor_tensor(b[:, d:NT], a[:, d:NT], a[:, 0:NT - d], op=ALU.add))
                        step(nc.vector.tensor_copy(b[:, 0:d], a[:, 0:d]))
                        a, b, d = b, a, 2 * d
                    step(nc.vector.tensor_scalar(ni[:, 0], a[:, NT - 1], float(P - 1), None, ALU.add))
                    step(nc.vector.tensor_scalar(ni[:, 1], ni[:, 0], P.bit_length() - 1, None, ALU.arith_shift_right))
                    step(nc.vector.tensor_copy(ne[:, 0], ni[:, 1]))
                    step(nc.vector.tensor_copy(ne[:, 1], ne[:, 0]))
                    x, y, d = 1, 2, 1
                    while d < E:
                        steps.mark(nc.vector.tensor_tensor(ne[:, y, d:E], ne[:, x, d:E], ne[:, x, 0:E - d], op=ALU.add))
                        step(nc.vector.tensor_copy(ne[:, y, 0:d], ne[:, x, 0:d]))
                        x, y, d = y, x, 2 * d
                    step(nc.vector.tensor_tensor(ne[:, 3], ne[:, x], ne[:, 0], op=ALU.subtract))
                    step(nc.vector.tensor_scalar_mul(ne[:, 3], ne[:, 3], float(P)))
                    step(nc.vector.tensor_tensor(S[:], a[:], tot, op=ALU.subtract))
                    step(nc.vector.tensor_tensor(S[:], S[:], pre, op=ALU.add))
                    step(nc.vector.tensor_tensor(S[:], S[:], of_e(ne[:, 3]), op=ALU.add))
                    for s, hot in enumerate((hot1, hot2)):
                        step(nc.vector.tensor_tensor(tmp[:], hot[:], S[:], op=ALU.mult))
                        step(nc.vector.reduce_sum(at[:, s], tmp[:], AX))
                        nc.vector.tensor_copy(slot[:, s], at[:, s]).then_inc(slots_ready, 1)
                    dve.wait_ge(x_tr, NC + 2)
                    dve.wait_ge(slots_ready, 2)

                    def rows(c, h):
                        nc.vector.tensor_copy(place[:, h], slot[:, :, ds(CT * c, CT)])
                        norm(c, h, row_ready)
                    rows(0, 0)
                    rows(1, 1)
                    with dve.Fori(1, NC // 2) as i:
                        for h in range(2):
                            dve.wait_ge(scattered[h], 16 * 2 * CT * i)
                            rows(2 * i + h, h)
                    step(nc.vector.tensor_tensor(held[:], ne[:, x].unsqueeze(1).broadcast_to([P, MT, E]), tf[:].unsqueeze(2).broadcast_to([P, MT, E]), op=ALU.is_le))
                    step(nc.vector.reduce_sum(ended[:], held[:], AX))
                    step(nc.vector.tensor_scalar(owner[:], ended[:], float(E - 1), None, ALU.min))
                    dve.wait_ge(r_exp, 1)
                    step(nc.vector.tensor_scalar(ex[:, 2], ex[:, 1], 1.0, None, ALU.add))
                    step(nc.vector.reciprocal(weight[:, 0], ex[:, 2]))
                    step(nc.vector.tensor_tensor(weight[:, 1], ex[:, 1], weight[:, 0], op=ALU.mult))

                @block.scalar
                def _(act):
                    with act.Fori(0, NC // 2) as i:
                        for h in range(2):
                            c = 2 * i + h
                            act.wait_ge(x_tr, c + 2)
                            nc.scalar.copy(xT[:, h].rearrange("p k n -> p (k n)"), ps[:, 2 * h:2 * h + 2].rearrange("p a n -> p (a n)")).then_inc(xT_ready, 1)
                    act.wait_ge(gap_ready, 1)
                    nc.scalar.activation(ex[:, 1], ex[:, 0], ACT.Exp).then_inc(r_exp, 1)

                @block.tensor
                def _(pe):
                    pe.wait_ge(small, 64)
                    nc.tensor.transpose(ps[:, 7, 0:E * EK], b1r[:], ident[0:E * EK, 0:E * EK]).then_inc(b1_tr, 1)

                    pe.sem_inc(x_tr, 1)

                    def turn(c, h):
                        pe.wait_ge(xc_ready, c + 1)
                        for dk in range(DK):
                            for k in range(CT):
                                last = nc.tensor.transpose(ps[:, 2 * h + dk, k * P:(k + 1) * P], xc[:, h, k, dk * P:(dk + 1) * P], ident[:])
                        last.then_inc(x_tr, 1)
                    turn(0, 0)
                    with pe.Fori(0, NC // 2) as i:
                        for h in range(2):
                            c = 2 * i + h
                            turn(c + 1, 1 - h)
                            pe.wait_ge(xT_ready, c + 1)
                            for k in range(CT):
                                for dk in range(DK):
                                    last = nc.tensor.matmul(ps[:, 4, ds(E * (CT * c + k), E)], xT[:, h, dk, k * P:(k + 1) * P], wg[:, dk],
                                                            start=(dk == 0), stop=(dk == DK - 1), skip_group_check=True)
                            last.then_inc(lg_done, 1)
                    pe.wait_ge(c_ready, 2)
                    pe.wait_ge(hot_ready, 1)
                    chosen = tmp[:].rearrange("p t e -> p (t e)")
                    nc.tensor.matmul(ps[:, 5], before[:], chosen, start=True, stop=True)
                    nc.tensor.matmul(ps[:, 6], ones[:], chosen, start=True, stop=True).then_inc(c_done, 1)

        with ExitStack() as s1:
            AHEAD = 4
            xin = sbuf(s1, "e_xin", [P, AHEAD, D])
            xT = sbuf(s1, "e_xinT", [P, 2, DK, P])
            hid = sbuf(s1, "e_hidden", [P, 2, EH])
            hT = sbuf(s1, "e_hiddenT", [P, 2, EK, P])
            y = sbuf(s1, "e_y", [P, 2, D])
            b2b = sbuf(s1, "b2b", [P, E, D])
            x_loaded = [sem(f"e_x_loaded{r}") for r in range(AHEAD)]
            stored = [sem(f"e_y_stored{z}") for z in range(2)]
            b2_loaded, xt_done, xt_kept, m1_done, h_kept, ht_done, hta_kept, htb_kept, m2_done, y_kept, y_turn = (
                sem("e_" + n) for n in ("b2_loaded", "xt_done", "xt_kept", "m1_done", "h_kept", "ht_done", "hta_kept", "htb_kept", "m2_done", "y_kept", "y_turn"))
            assert AHEAD % 2 == 0 and MT % AHEAD == 0
            XT_BANK, H_BANK, HT_BANK, Y_BANK = (0, 7), (1, 2), (3, 4), (5, 6)
            HK = EK // 2
            of_tile = lambda eng, k: eng.value_load(owner[0:1, ds(k, 1)] if not isinstance(k, int) else owner[0:1, k:k + 1], min_val=0, max_val=E - 1)

            def tiles(eng, body):
                body(0, 0)
                with eng.Fori(0, MT // AHEAD - 1) as i:
                    for r in range(1, AHEAD + 1):
                        body(AHEAD * i + r, r % AHEAD)
                for r in range(1, AHEAD):
                    body(MT - AHEAD + r, r)
            with nc.Block() as block:
                @block.sync
                def _(sp):
                    def load(k, r):
                        sp.dma_start(xin[:, r], xsort[ds(P * k, P), :]).then_inc(x_loaded[r], 16)

                    def store(k, r):
                        sp.wait_ge(y_kept, k + 3)
                        sp.sem_inc(y_turn, 1)
                        sp.dma_start(ysort[ds(P * k, P), :], y[:, r % 2]).then_inc(stored[r % 2], 16)
                    for r in range(AHEAD):
                        load(r, r)
                    sp.dma_start(b2b[:], b2_in.partition_broadcast(P)).then_inc(b2_loaded, 16)
                    for z in range(2):
                        sp.sem_inc(stored[z], 16)
                    with sp.Fori(0, MT // AHEAD - 1) as i:
                        for r in range(AHEAD):
                            store(AHEAD * i + r, r)
                            load(AHEAD * i + r + AHEAD, r)
                    for r in range(AHEAD):
                        store(MT - AHEAD + r, r)
                    for z in range(2):
                        sp.wait_ge(stored[z], 16 * (MT // 2 + 1))

                @block.scalar
                def _(act):
                    def body(k, r):
                        z = r % 2
                        act.wait_ge(xt_done, k + 1)
                        nc.scalar.copy(xT[:, z].rearrange("p k n -> p (k n)"), ps[:, XT_BANK[z], 0:D]).then_inc(xt_kept, 1)
                        if isinstance(k, int) and k == 0:
                            return
                        half(k - 1, 1 - z)

                    def half(k, z):
                        e = of_tile(act, k)
                        act.wait_ge(ht_done, k + 1)
                        for j in range(HK):
                            nc.scalar.activation(hT[:, z, j], ps[:, HT_BANK[0], j * P:(j + 1) * P], ACT.Relu, bias=b1T[:, ds(EK * e + j, 1)]).then_inc(hta_kept, 1)
                    tiles(act, body)
                    half(MT - 1, 1)

                @block.vector
                def _(dve):
                    dve.wait_ge(b2_loaded, 16)

                    def outputs(k, r):
                        z = r % 2
                        e = of_tile(dve, k)
                        dve.wait_ge(m2_done, k + 1)
                        dve.wait_ge(stored[z], 16 * (k // 2) + 16)
                        nc.vector.tensor_tensor(y[:, z], ps[:, Y_BANK[z], 0:D], b2b[:, ds(e, 1), :].rearrange("p a d -> p (a d)"), op=ALU.add).then_inc(y_kept, 1)

                    def body(k, r):
                        z = r % 2
                        dve.wait_ge(m1_done, k + 1)
                        nc.vector.tensor_copy(hid[:, z], ps[:, H_BANK[z]]).then_inc(h_kept, 1)
                        if not (isinstance(k, int) and k == 0):
                            outputs(k - 1, r - 1)
                        e = of_tile(dve, k)
                        dve.wait_ge(ht_done, k + 1)
                        for j in range(HK, EK):
                            nc.vector.tensor_scalar(hT[:, z, j], ps[:, HT_BANK[1], (j - HK) * P:(j - HK + 1) * P], b1T[:, ds(EK * e + j, 1)], 0.0, ALU.add, ALU.max).then_inc(htb_kept, 1)
                    tiles(dve, body)
                    outputs(MT - 1, AHEAD - 1)

                @block.tensor
                def _(pe):
                    def turn_x(k, r):
                        z = r % 2
                        pe.wait_ge(x_loaded[r], 16 * (k // AHEAD) + 16)
                        for dk in range(DK):
                            last = nc.tensor.transpose(ps[:, XT_BANK[z], dk * P:(dk + 1) * P], xin[:, r, dk * P:(dk + 1) * P], ident[:])
                        last.then_inc(xt_done, 1)

                    def second(k, z):
                        e = of_tile(pe, k)
                        pe.wait_ge(y_kept, k + 1)
                        pe.wait_ge(hta_kept, HK * (k + 1))
                        pe.wait_ge(htb_kept, HK * (k + 1))
                        for j in range(EK):
                            last = nc.tensor.matmul(ps[:, Y_BANK[z], 0:D], hT[:, z, j], W2[:, ds(e, 1), j, :].rearrange("p a d -> p (a d)"), start=(j == 0), stop=(j == EK - 1))
                        last.then_inc(m2_done, 1)

                    def body(k, r):
                        z = r % 2
                        e = of_tile(pe, k)
                        pe.wait_ge(xt_kept, k + 1)
                        for dk in range(DK):
                            last = nc.tensor.matmul(ps[:, H_BANK[z]], xT[:, z, dk], W1[:, ds(e, 1), dk, :].rearrange("p a d -> p (a d)"), start=(dk == 0), stop=(dk == DK - 1))
                        last.then_inc(m1_done, 1)
                        if not (isinstance(k, int) and k == MT - 1):
                            turn_x(k + 1, (r + 1) % AHEAD)
                        if not (isinstance(k, int) and k == 0):
                            second(k - 1, 1 - z)
                        pe.wait_ge(h_kept, k + 1)
                        for j in range(EK):
                            last = nc.tensor.transpose(ps[:, HT_BANK[j // HK], (j % HK) * P:(j % HK + 1) * P], hid[:, z, j * P:(j + 1) * P], ident[:])
                        last.then_inc(ht_done, 1)
                    pe.sem_inc(y_kept, 2)
                    for w in w_loaded:
                        pe.wait_ge(w, 64)
                    turn_x(0, 0)
                    tiles(pe, body)
                    second(MT - 1, 1)

        with ExitStack() as s2:
            RING = 4
            got = sbuf(s2, "e_got", [P, RING, 2, D])
            place = sbuf(s2, "e_place", [P, 2, 2, RING], U32)
            place_ready, fetch_turn = sem("e_place_ready"), sem("e_fetch_turn")
            fetched = [sem(f"e_fetched{r}") for r in range(RING)]
            added, out_turn, out_stored = sem("e_added"), sem("out_turn"), sem("out_stored")
            with nc.Block() as block:
                @block.gpsimd
                def _(pool):
                    pool.sem_inc(added, 2 * RING)
                    with pool.Fori(0, NT // RING // 2) as i2:
                        for h in range(2):
                            i = 2 * i2 + h
                            pool.wait_ge(added, 2 * RING * i + 2)
                            nc.gpsimd.tensor_copy(place[:, h], slot[:, :, ds(RING * i, RING)]).then_inc(place_ready, 1)
                            pool.wait_ge(place_ready, i + 1)
                            for r in range(RING):
                                pool.wait_ge(added, 2 * (RING * i + r) + 2)
                                pool.sem_inc(fetch_turn, 1)
                                for s in range(2):
                                    nc.gpsimd.indirect_dma_start(got[:, r, s], None, ysort, bass.IndirectOffsetOnAxis(ap=place[:, h, s, r:r + 1], axis=0)).then_inc(fetched[r], 16)

                @block.vector
                def _(dve):
                    with dve.Fori(0, NT // RING) as i:
                        for r in range(RING):
                            t = RING * i + r
                            dve.wait_ge(fetched[r], 32 * i + 32)
                            row = X[:, ds(t, 1), :].rearrange("p a d -> p (a d)")
                            for s in range(2):
                                nc.vector.scalar_tensor_tensor(row, got[:, r, s], weight[:, s, ds(t, 1)], row, op0=ALU.mult, op1=ALU.add).then_inc(added, 1)
                                if s == 0:
                                    dve.wait_ge(added, 2 * t + 2 * RING + 1)

                @block.sync
                def _(sp):
                    with sp.Fori(0, NT // RING) as i:
                        sp.wait_ge(added, 2 * RING * (i + 2))
                        sp.sem_inc(out_turn, 1)
                        sp.dma_start(out_tiles[:, ds(RING * i, RING), :], X[:, ds(RING * i, RING), :]).then_inc(out_stored, 16)
                    sp.wait_ge(out_stored, 16 * (NT // RING))


def attention(nc, sem, stack, sbuf, ps, ident, identb, pqk, V, ATT):
    KQ = sbuf(stack, "KQ", [P, RING, 2, HG, SEQ], BF16)
    PR = sbuf(stack, "PR", [P, 2, HG, SEQ])
    VO = sbuf(stack, "VO", [P, KT, HG, 2 * HD])
    OT = sbuf(stack, "OT", [P, SEQ])
    mx = sbuf(stack, "mx", [P, QC, HG, QT])
    mm = sbuf(stack, "mm", [P, HG * QT])
    rest = sbuf(stack, "nm_rest", [P, HG * QT])
    nmp = sbuf(stack, "nmp", [P, PARTS, HG * QT], BF16)
    nrow = sbuf(stack, "nrow", [PARTS * HG * QT, P], BF16)
    rec = sbuf(stack, "rec", [P, 2, QT // 2, HG])
    SLOTS = 3
    MAX_BANK, ST_BANK, OT_BANK = 0, SLOTS, 2 * SLOTS

    ready, freed = sem("att_ready"), sem("kq_first")
    kq_loaded = [sem(f"kq_loaded{r}") for r in range(RING)]
    row_loaded = [sem(f"row_loaded{r}") for r in range(RING)]
    st_done, exp_done, pv_done = sem("st_done"), sem("exp_done"), sem("pv_done")
    max_done, red_done = sem("max_done"), sem("red_done")
    nm_steps, nm_tr, nm_kept = sem("nm_steps"), sem("nm_tr"), sem("nm_kept")
    vo_ready, ot_kept, ot_tr, att_steps = sem("vo_ready"), sem("ot_kept"), sem("ot_tr"), sem("att_steps")
    BLOCKS, MAXES, NM = KT * HG * QC, HG * QT * QC, 5
    order = [(h, q, k) for h in range(HG) for q in range(QT) for k in range(QC)]
    LOADS = 2 * len(PAIR_Q)
    EARLY = 12
    TURN = EARLY + 8
    LATE = 5
    events = ([("max", t) for t in range(LATE)] + [("nm", 0)] + [("max", t) for t in range(LATE, TURN)]
              + [("heads", 0), ("heads", 1)] + [("max", t) for t in range(TURN, MAXES)])
    place = {event: e for e, event in enumerate(events)}
    assert RING == SLOTS and BLOCKS % SLOTS == 1 and len(events) % SLOTS == 1
    bank = lambda r, event: MAX_BANK + (r + place[event]) % SLOTS
    st_bank = lambda r, s: ST_BANK + (r + s) % SLOTS

    def unit_loop(eng, unit):
        known = lambda u: lambda k: (u + k, (u + k) // RING, (u + k) % RING) if u + k < UNITS else None
        unit(known(0))
        with eng.Fori(0, (UNITS - 4) // RING) as i:
            for j in range(1, RING + 1):
                unit(lambda k, j=j: (RING * i + j + k, i + (j + k) // RING, (j + k) % RING))
        for u in range(UNITS - 3, UNITS):
            unit(known(u))
    assert (UNITS - 4) % RING == 0
    is0 = lambda u: isinstance(u, int) and u == 0

    with nc.Block() as block:
        @block.vector
        def _(dve):
            nc.vector.memset(KQ[KROWS:AROWS, :, 0].rearrange("p r h n -> p r (h n)"), 1.0).then_inc(ready, 1)
            nc.vector.memset(VO[:], 1.0).then_inc(ready, 1)

            def reduce(u, r, t):
                h, q, k = order[t]
                dve.wait_ge(max_done, MAXES * u + t + 1)
                nc.vector.reduce_max(mx[:, k, h, q:q + 1], ps[:, bank(r, ("max", t))], AX).then_inc(red_done, 1)

            def negate(u):
                dve.wait_ge(red_done, MAXES * u + MAXES)
                if not is0(u):
                    dve.wait_ge(nm_tr, u)
                m0, m1 = (mx[:, k].rearrange("p h q -> p (h q)") for k in range(QC))
                step = lambda ins: ins.then_inc(nm_steps, 1)
                step(nc.vector.tensor_tensor(mm[:], m0, m1, op=ALU.max))
                dve.wait_ge(nm_steps, NM * u + 1)
                step(nc.vector.tensor_scalar_mul(nmp[:, 0], mm[:], -1.0))
                dve.wait_ge(nm_steps, NM * u + 2)
                step(nc.vector.scalar_tensor_tensor(rest[:], mm[:], -1.0, nmp[:, 0], op0=ALU.mult, op1=ALU.subtract))
                dve.wait_ge(nm_steps, NM * u + 3)
                step(nc.vector.tensor_copy(nmp[:, 1], rest[:]))
                dve.wait_ge(nm_steps, NM * u + 4)
                step(nc.vector.tensor_tensor(nmp[:, 2], rest[:], nmp[:, 1], op=ALU.subtract))

            def heads_out(u, r):
                for k in range(2):
                    o = ps[:, bank(r, ("heads", k))].rearrange("p (q h c) -> p q h c", q=QT // 2, h=HG)
                    dve.wait_ge(ot_tr, 2 * u + k + 1)
                    nc.vector.reciprocal(rec[:, k], o[:, :, :, HD]).then_inc(att_steps, 1)
                    dve.wait_ge(att_steps, 4 * u + 2 * k + 1)
                    b, g = u // UPB, u % UPB
                    nc.vector.tensor_tensor(
                        ATT[:, ds(QT * b + QT // 2 * k, QT // 2), ds(HG * HD * g, HG * HD)].rearrange("p q (h c) -> p q h c", h=HG),
                        o[:, :, :, 0:HD], rec[:, k].unsqueeze(3).broadcast_to([P, QT // 2, HG, HD]), op=ALU.mult).then_inc(att_steps, 1)

            for t in range(MAXES):
                reduce(0, 0, t)
            negate(0)
            for t in range(EARLY):
                reduce(1, 1, t)

            def unit(at):
                (u, n, r), nxt, after = at(0), at(1), at(2)
                if nxt is not None:
                    for t in range(EARLY, TURN):
                        reduce(nxt[0], nxt[2], t)
                if not is0(u):
                    heads_out(u - 1, (r + 1) % RING)
                if nxt is not None:
                    for t in range(TURN, MAXES):
                        reduce(nxt[0], nxt[2], t)
                    negate(nxt[0])
                if after is not None:
                    for t in range(EARLY):
                        reduce(after[0], after[2], t)
            unit_loop(dve, unit)
            heads_out(UNITS - 1, (UNITS + 1) % RING)

        @block.scalar
        def _(act):
            def keep_rows(u, r):
                act.wait_ge(nm_tr, u + 1)
                if not is0(u):
                    act.wait_ge(freed, u)
                nc.scalar.copy(nrow[:], ps[0:PARTS * HG * QT, bank(r, ("nm", 0)), 0:P // 2].bitcast(BF16)).then_inc(nm_kept, 1)

            keep_rows(0, 1)

            def unit(at):
                (u, n, r), nxt = at(0), at(1)
                for s in range(BLOCKS):
                    kt, h, qc = s // (HG * QC), s // QC % HG, s % QC
                    act.wait_ge(st_done, BLOCKS * u + s + 1)
                    if h == 0 and qc == 0 and not (is0(u) and kt < 2):
                        act.wait_ge(pv_done, KT * u + kt - 1)
                    nc.scalar.activation(PR[:, kt % 2, h, qc * BANK:(qc + 1) * BANK], ps[:, st_bank(r, s)], ACT.Exp).then_inc(exp_done, 1)
                    if nxt is not None and s == (BLOCKS - 8 if at(2) is not None else BLOCKS - 1):
                        keep_rows(nxt[0], (nxt[2] + 1) % RING)
                act.wait_ge(pv_done, KT * u + KT)
                if not is0(u):
                    act.wait_ge(ot_tr, 2 * u)
                nc.scalar.copy(OT[:], ps[:, OT_BANK:OT_BANK + 2].rearrange("p a n -> p (a n)")).then_inc(ot_kept, 1)
            unit_loop(act, unit)

        @block.gpsimd
        def _(pool):
            pool.wait_ge(ready, 2)

            def unit(at):
                u = at(0)[0]
                if not is0(u):
                    pool.wait_ge(pv_done, KT * u)
                b, g = u // UPB, u % UPB
                nc.gpsimd.tensor_copy(VO[:, :, :, 0:HD], V[:, ds(KT * b, KT), ds(HG * HD * g, HG * HD)].rearrange("p k (h c) -> p k h c", h=HG)).then_inc(vo_ready, 1)
            unit_loop(pool, unit)

        @block.sync
        def _(sp):
            def load(u, r):
                b, g = u // UPB, u % UPB
                for side, pairs in ((1, PAIR_Q), (0, PAIR_K)):
                    for j, part in enumerate(pairs):
                        src = pqk.rearrange("s a k p t -> s a (k p) t").rearrange("s a (g h c) t -> s a g c h t", h=HG, c=HD)
                        sp.dma_start(KQ[j * HD:(j + 1) * HD, r, side],
                                     src[1 - side, part, ds(g, 1), :, :, ds(SEQ * b, SEQ)].rearrange("g c h t -> (g c) h t")).then_inc(kq_loaded[r], 16)

            def rows(u, r):
                sp.wait_ge(nm_kept, u + 1)
                for a in range(PARTS):
                    n = HG * QT
                    sp.dma_start(KQ[KROWS + a:KROWS + a + 1, r, 1].rearrange("p h (q n) -> p (h q) n", n=P),
                                 nrow[a * n:(a + 1) * n, :]).then_inc(row_loaded[r], 16)

            load(0, 0)
            load(1, 1)
            rows(0, 0)

            def unit(at):
                (u, n, r), nxt, after = at(0), at(1), at(2)
                sp.wait_ge(row_loaded[r], 16 * PARTS * (n + 1))
                if after is not None and not is0(u):
                    sp.wait_ge(st_done, BLOCKS * u)
                sp.sem_inc(freed, 1)
                if after is not None:
                    load(after[0], after[2])
                if nxt is not None:
                    rows(nxt[0], nxt[2])
            unit_loop(sp, unit)

        @block.tensor
        def _(pe):
            def bank_read(u, e):
                while True:
                    u, e = (u, e - SLOTS) if e >= SLOTS else (u - 1, e - SLOTS + len(events))
                    if isinstance(u, int) and u < 0:
                        return
                    kind, t = events[e]
                    if isinstance(u, int) and (kind == "max" and u >= UNITS or kind == "nm" and u > UNITS):
                        continue
                    if kind == "max":
                        return pe.wait_ge(red_done, MAXES * u + t + 1)
                    if kind == "nm" and not is0(u):
                        return pe.wait_ge(nm_kept, u)
                    if kind == "heads" and (not isinstance(u, int) or u >= 2):
                        return pe.wait_ge(att_steps, 4 * (u - 2) + 2 * t + 2)

            def first_pass(u, n, r, t):
                h, q, k = order[t]
                if t == 0:
                    pe.wait_ge(kq_loaded[r], 16 * LOADS * (n + 1))
                bank_read(u, place["max", t])
                nc.tensor.matmul(ps[:, bank(r, ("max", t))], KQ[0:KROWS, r, 1, h, q * P:(q + 1) * P], KQ[0:KROWS, r, 0, h, k * BANK:(k + 1) * BANK],
                                 start=True, stop=True).then_inc(max_done, 1)

            def turn_max(u, r):
                pe.wait_ge(nm_steps, NM * u + NM)
                bank_read(u + 1, place["nm", 0])
                nc.tensor.transpose(ps[0:PARTS * HG * QT, bank(r, ("nm", 0)), 0:P // 2].bitcast(BF16), nmp[:].rearrange("p a n -> p (a n)"), identb[:]).then_inc(nm_tr, 1)

            def turn_heads(u, r, k):
                pe.wait_ge(ot_kept, u + 1)
                bank_read(u + 2, place["heads", k])
                for q in range(QT // 2):
                    last = nc.tensor.transpose(ps[:, bank(r, ("heads", k)), q * P:(q + 1) * P], OT[:, (k * QT // 2 + q) * P:(k * QT // 2 + q + 1) * P], ident[:])
                last.then_inc(ot_tr, 1)

            def weigh(u, kt, qc):
                if qc == 0:
                    pe.wait_ge(exp_done, BLOCKS * u + HG * QC * (kt + 1))
                if kt == 0 and qc == 0:
                    pe.wait_ge(vo_ready, u + 1)
                    if not is0(u):
                        pe.wait_ge(ot_kept, u)
                for h in range(HG):
                    last = nc.tensor.matmul(ps[2 * HD * h:2 * HD * (h + 1), OT_BANK + qc], VO[:, kt, h], PR[:, kt % 2, h, qc * BANK:(qc + 1) * BANK],
                                            start=(kt == 0), stop=(kt == KT - 1))
                if qc == QC - 1:
                    last.then_inc(pv_done, 1)

            pe.wait_ge(ready, 2)
            for t in range(MAXES):
                first_pass(0, 0, 0, t)
            for t in range(LATE):
                first_pass(1, 0, 1, t)
            turn_max(0, 1)
            for t in range(LATE, EARLY):
                first_pass(1, 0, 1, t)

            def unit(at):
                (u, n, r), nxt, after = at(0), at(1), at(2)
                beside = [(first_pass, (*nxt, t)) for t in range(EARLY, TURN)] if nxt is not None else []
                if not is0(u):
                    beside += [(turn_heads, (u - 1, (r + 1) % RING, k)) for k in range(2)]
                if nxt is not None:
                    beside += [(first_pass, (*nxt, t)) for t in range(TURN, MAXES)]
                if after is not None:
                    beside += [(first_pass, (*after, t)) for t in range(LATE)]
                if nxt is not None:
                    beside += [(turn_max, (nxt[0], (nxt[2] + 1) % RING))]
                if after is not None:
                    beside += [(first_pass, (*after, t)) for t in range(LATE, EARLY)]
                pe.wait_ge(row_loaded[r], 16 * PARTS * (n + 1))
                done = 0
                for s in range(BLOCKS):
                    kt, h, qc = s // (HG * QC), s // QC % HG, s % QC
                    if not (is0(u) and s < SLOTS):
                        pe.wait_ge(exp_done, BLOCKS * u + s - SLOTS + 1)
                    nc.tensor.matmul(ps[:, st_bank(r, s)], KQ[0:AROWS, r, 0, h, kt * P:(kt + 1) * P],
                                     KQ[0:AROWS, r, 1, h, qc * BANK:(qc + 1) * BANK], start=True, stop=True).then_inc(st_done, 1)
                    if kt > 0 and h in (1, 3) and qc == 1:
                        weigh(u, kt - 1, h // 2)
                    while done < (s + 1) * len(beside) // BLOCKS:
                        what, given = beside[done]
                        what(*given)
                        done += 1
                for qc in range(QC):
                    weigh(u, KT - 1, qc)
            unit_loop(pe, unit)
            for k in range(2):
                turn_heads(UNITS - 1, (UNITS + 1) % RING, k)


_INS = ['L0_attn_x', 'L0_attn_Wq', 'L0_attn_Wk', 'L0_attn_Wv', 'L0_attn_Wo', 'L0_attn_quadrant_weights',
        'L0_ffn_fast_b', 'L0_ffn_w_fc', 'L0_ffn_w_proj', 'L0_ffn_u', 'L0_ffn_v', 'L0_ffn_gate',
        'L1_attn_A', 'L1_attn_Bm', 'L1_attn_Cm', 'L1_attn_Dm', 'L1_attn_ln_w', 'L1_attn_ln_b', 'L1_attn_W_out', 'L1_attn_b_out',
        'L1_ffn_Wg', 'L1_ffn_bg', 'L1_ffn_bias', 'L1_ffn_W1', 'L1_ffn_b1', 'L1_ffn_W2', 'L1_ffn_b2']


def kernel(**inputs):
    import numpy as np
    import concourse.bacc as bacc
    from concourse.bass_utils import run_bass_kernel_spmd

    nc = bacc.Bacc("TRN2", target_bir_lowering=False, num_devices=1)
    nc.disable_value_cache = True
    arrays, args = {}, []
    for name in _INS:
        a = np.ascontiguousarray(inputs[name])
        if a.ndim == 0:
            a = a.reshape(1)
        arrays[f"in_{name}"] = a
        args.append(nc.dram_tensor(f"in_{name}", a.shape, mybir.dt.from_np(a.dtype), kind="ExternalInput").ap())
    out = nc.dram_tensor("out", (BATCH, SEQ, D), F32, kind="ExternalOutput").ap()
    transformer_kernel(nc, args, out)
    r = run_bass_kernel_spmd(nc, [arrays], core_ids=[0])
    return r.results[0]["out"]
```

```python
from contextlib import ExitStack

import concourse.bass as bass
from concourse import mybir

F32 = mybir.dt.float32
BF16 = mybir.dt.bfloat16
F32R = mybir.dt.float32r
I32 = mybir.dt.int32
U32 = mybir.dt.uint32
ALU = mybir.AluOpType
ACT = mybir.ActivationFunctionType
AX = mybir.AxisListType.X
ds = bass.ds

P = 128
BATCH, SEQ, D = 4, 1024, 256
T = BATCH * SEQ
NT = T // P
DK = D // P
CT = 4
CW = CT * P
NC = T // CW
BANK = 512
EPS = 1e-5

H, HD = 16, 16
HH = HD // 2
HG = 4
UNITS = BATCH * H // HG
UPB = H // HG
KT = SEQ // P
QT = SEQ // P
QC = SEQ // BANK
PARTS = 3
PAIR_Q = [0, 0, 1, 0, 2, 1]
PAIR_K = [0, 1, 0, 2, 0, 1]
KROWS = len(PAIR_Q) * HD
AROWS = KROWS + PARTS
RING = 3


E = 16
EH = 512
EK = EH // P
MT = 2 * NT + E


class ChunkNorm:

    def __init__(self, nc, sem, sbuf, stack, name, src):
        self.nc, self.src = nc, src
        self.bn = sbuf(stack, name + "_bn", [P, 2, CT, 6])
        self.mv = sbuf(stack, name + "_mv", [P, 2, CT, 2])
        self.ve = sbuf(stack, name + "_ve", [P, 2, CT])
        self.power = sbuf(stack, name + "_power", [P, CT])
        self.mean, self.rstd = (sbuf(stack, name + n, [P, NT]) for n in ("_mean", "_rstd"))
        self.taken, self.known, self.set, self.eps, self.rooted, self.ready, self.turn = (
            sem(name + n) for n in ("_taken", "_known", "_set", "_eps", "_rooted", "_ready", "_turn"))

    def stats(self, dve, c, h):
        tile = lambda k: self.src[:, ds(CT * c + k, 1), :].rearrange("p a d -> p (a d)")
        for k in range(CT):
            self.nc.vector.bn_stats(self.bn[:, h, k], tile(k)).then_inc(self.taken, 1)
        dve.wait_ge(self.taken, CT * c + CT)
        dve.sem_inc(self.turn, 1)
        for k in range(CT):
            self.nc.vector.bn_aggr(self.mv[:, h, k], self.bn[:, h, k]).then_inc(self.known, 1)

    def start(self, pool):
        self.nc.gpsimd.memset(self.power[:], -0.5).then_inc(self.set, 1)
        pool.wait_ge(self.set, 1)

    def root(self, pool, c, h):
        pool.wait_ge(self.known, CT * c + CT)
        pool.sem_inc(self.turn, 1)
        self.nc.gpsimd.tensor_scalar(self.ve[:, h], self.mv[:, h, :, 1], EPS, None, ALU.add).then_inc(self.eps, 1)
        self.nc.gpsimd.tensor_copy(self.mean[:, ds(CT * c, CT)], self.mv[:, h, :, 0])
        pool.wait_ge(self.eps, c + 1)
        self.nc.gpsimd.tensor_tensor(self.rstd[:, ds(CT * c, CT)], self.ve[:, h], self.power[:], op=ALU.pow).then_inc(self.rooted, 1)

    def apply(self, dve, c, dst, ready=None):
        dve.wait_ge(self.rooted, c + 1)
        for k in range(CT):
            t = ds(CT * c + k, 1)
            last = self.nc.vector.tensor_scalar(dst(k), self.src[:, t, :].rearrange("p a d -> p (a d)"),
                                                self.mean[:, t], self.rstd[:, t], ALU.subtract, ALU.mult)
        last.then_inc(ready or self.ready, 1)


def chunks(eng, body, first=False):
    if first:
        body(0, 0)
        body(1, 1)
    with eng.Fori(1 if first else 0, NC // 2 - 1) as i:
        body(2 * i, 0)
        body(2 * i + 1, 1)
    body(NC - 2, 0)
    body(NC - 1, 1)


def split_products(a, b):
    return ((a[0], b[0]), (a[1], b[0]), (a[0], b[1]))


is_first = lambda c: isinstance(c, int) and c == 0
more = lambda c, k: not isinstance(c, int) or c + k < NC


class Count:

    def __init__(self, sem):
        self.sem, self.n = sem, 0

    def mark(self, ins):
        ins.then_inc(self.sem, 1)
        self.n += 1

    def wait(self, eng):
        eng.wait_ge(self.sem, self.n)


def transformer_kernel(nc, ins, out):
    (x_in, wq_in, wk_in, wv_in, wo_in, quad_in, fastb_in, wfc_in, wproj_in, u_in, v_in, gate_in,
     a_in, bm_in, cm_in, dm_in, lnw_in, lnb_in, wout_in, bout_in,
     wg_in, bg_in, bias_in, w1_in, b1_in, w2_in, b2_in) = ins
    x_rows = x_in.rearrange("b s d -> (b s) d")
    out_rows = out.rearrange("b s d -> (b s) d")
    x_tiles = x_rows.rearrange("(t p) d -> p t d", p=P)
    out_tiles = out_rows.rearrange("(t p) d -> p t d", p=P)
    by_k = lambda w: w.rearrange("(k p) n -> p k n", p=P)

    outer = ExitStack()
    phase_sems = []

    def sem(name):
        phase_sems.append(nc.alloc_semaphore(name))
        return phase_sems[-1]

    def reuse_sems(kept=()):
        with nc.Block() as block:
            @block.gpsimd
            def _(pool):
                nc.clear_and_free_semaphores([s for s in phase_sems if s not in kept])
        phase_sems.clear()

    def sbuf(stack, name, shape, dt=F32):
        return stack.enter_context(nc.sbuf_tensor(name, shape, dt))

    with outer:
        ps = outer.enter_context(nc.psum_tensor("ps", [P, 8, BANK], F32))
        X = sbuf(outer, "X", [P, NT, D])
        ident = sbuf(outer, "ident", [P, P])
        identb = sbuf(outer, "identb", [P, P], BF16)
        xsort = nc.dram_tensor("tokens_by_expert", [MT * P, D], F32, kind="Internal").ap()
        zero = sbuf(outer, "zero", [P, D])
        x_zeroed = sem("tokens_zeroed")
        lasting = [x_zeroed]
        pqk = nc.dram_tensor("qk_parts", [2, PARTS, DK, P, T], BF16, kind="Internal").ap()

        mid = ExitStack()
        with mid:
            V = sbuf(mid, "V", [P, NT, D])
            wo = [sbuf(mid, f"wo{a}", [P, DK, D], F32R) for a in range(2)]
            with ExitStack() as st:
                KQ = sbuf(st, "KQ", [P, RING, 2, HG, SEQ], BF16)
                kq_loaded = [sem(f"kq_loaded{r}") for r in range(RING)]

                def load_qk(sp, u, r):
                    b, g = u // UPB, u % UPB
                    for side, pairs in ((1, PAIR_Q), (0, PAIR_K)):
                        for j, part in enumerate(pairs):
                            src = pqk.rearrange("s a k p t -> s a (k p) t").rearrange("s a (g h c) t -> s a g c h t", h=HG, c=HD)
                            sp.dma_start(KQ[j * HD:(j + 1) * HD, r, side],
                                         src[1 - side, part, ds(g, 1), :, :, ds(SEQ * b, SEQ)].rearrange("g c h t -> (g c) h t")).then_inc(kq_loaded[r], 16)

                with ExitStack() as s1:
                    W = sbuf(s1, "w_raw", [P, 4, DK, D])
                    Wq, Wk, Wv, Wo = range(4)
                    wsplit = [sbuf(s1, f"w_part{a}", [P, 3, DK, D], F32R) for a in range(2)]
                    wk = sbuf(s1, "wk", [P, DK, H, 2, HH])
                    wkt = sbuf(s1, "wkt", [P, DK, H, 2, HH])
                    quad = sbuf(s1, "quad", [P, 4])
                    qs = sbuf(s1, "qs", [P, 8])
                    xn = sbuf(s1, "xn", [P, 2, CT, D])
                    xT = [sbuf(s1, f"xT{a}", [P, 2, DK, CW], F32R) for a in range(2)]
                    parts = sbuf(s1, "parts", [P, 2, 2, PARTS, DK, CW], BF16)
                    part = lambda h, m, a: parts[:, h, m // DK, a, m % DK]
                    rest = sbuf(s1, "rest", [P, 2 * DK, CW])
                    norm = ChunkNorm(nc, sem, sbuf, s1, "ln1", X)
                    x_loaded = [sem(f"x_loaded{h}") for h in range(2)]
                    w_loaded = [sem(f"w{n}_loaded") for n in "qkvo"]
                    quad_loaded, quad_steps, quad_max, quad_exp, k_mixed, w_hi, w_lo, idz, id_ready = (
                        sem(n) for n in ("quad_loaded", "quad_steps", "quad_max", "quad_exp", "k_mixed", "w_hi", "w_lo", "idz", "id_ready"))
                    xn_tr, xh_ready, xl_ready = sem("xn_tr"), sem("xh_ready"), sem("xl_ready")
                    qk_done, hi_ready, rest_ready, mid_ready, lo_ready = (sem(n) for n in ("qk_done", "hi_ready", "rest_ready", "mid_ready", "lo_ready"))
                    v_done, v_kept, parts_turn = sem("v_done"), sem("v_kept"), sem("parts_turn")
                    stored = [sem(f"parts_stored{h}") for h in range(2)]
                    with nc.Block() as block:
                        @block.sync
                        def _(sp):
                            for c in range(NC):
                                if c >= 2:
                                    sp.wait_ge(x_loaded[c % 2], 16 * (c // 2))
                                sp.dma_start(X[:, CT * c:CT * c + CT, :], x_tiles[:, CT * c:CT * c + CT, :]).then_inc(x_loaded[c % 2], 16)
                            for h in range(2):
                                sp.sem_inc(stored[h], 16)

                            def body(c, h):
                                if isinstance(c, int) and c == NC - 2:
                                    for h2 in range(2):
                                        sp.wait_ge(stored[h2], 16 * (NC // 2))
                                    for u in range(2):
                                        load_qk(sp, u, u)
                                sp.wait_ge(lo_ready, 2 * DK * (c + 2))
                                sp.sem_inc(parts_turn, 1)
                                sp.dma_start(pqk[:, :, :, :, ds(CW * c, CW)].rearrange("s a k p n -> p (s a k) n"),
                                             parts[:, h].rearrange("p s a k n -> p (s a k) n")).then_inc(stored[h], 16)
                            chunks(sp, body)
                            for h in range(2):
                                sp.wait_ge(stored[h], 16 * (NC // 2 + 1))

                        @block.gpsimd
                        def _(pool):
                            nc.gpsimd.memset(zero[:], 0.0)
                            nc.gpsimd.memset(ident[:], 0.0).then_inc(idz, 1)
                            nc.gpsimd.memset(identb[:], 0.0).then_inc(idz, 1)
                            pool.wait_ge(idz, 2)
                            for m in (ident, identb):
                                nc.gpsimd.affine_select(out=m[:], in_=m[:], compare_op=ALU.not_equal, fill=1.0, base=0,
                                                        pattern=[[-1, P]], channel_multiplier=1).then_inc(id_ready, 1)
                            norm.start(pool)
                            for c in range(2):
                                norm.root(pool, c, c)
                            pool.sem_inc(lo_ready, 2 * DK)

                            def body(c, h):
                                if more(c, 2):
                                    norm.root(pool, c + 2, h)
                                for m in range(2 * DK):
                                    pool.wait_ge(mid_ready, 2 * DK * c + m + 1)
                                    nc.gpsimd.tensor_tensor(part(h, m, 2), rest[:, m], part(h, m, 1), op=ALU.subtract).then_inc(lo_ready, 1)
                            chunks(pool, body)

                        @block.vector
                        def _(dve):
                            def stats(c, h):
                                dve.wait_ge(x_loaded[h], 16 * (c // 2) + 16)
                                norm.stats(dve, c, h)
                            stats(0, 0)
                            dve.wait_ge(quad_loaded, 16)
                            steps = Count(quad_steps)
                            steps.mark(nc.vector.reduce_max(qs[:, 0:1], quad[:], AX))
                            steps.wait(dve)
                            nc.vector.tensor_scalar_mul(qs[:, 1:2], qs[:, 0:1], -1.0).then_inc(quad_max, 1)
                            dve.wait_ge(quad_exp, 1)
                            steps.mark(nc.vector.reduce_sum(qs[:, 2:3], qs[:, 4:8], AX))
                            steps.wait(dve)
                            steps.mark(nc.vector.reciprocal(qs[:, 3:4], qs[:, 2:3]))
                            steps.wait(dve)
                            steps.mark(nc.vector.tensor_scalar(quad[:], qs[:, 4:8], qs[:, 3:4], float(HH) ** -0.5, ALU.mult, ALU.mult))
                            steps.wait(dve)
                            dve.wait_ge(w_loaded[Wk], 16)
                            half = W[:, Wk].rearrange("p k (h a c) -> p k h a c", h=H, a=2)
                            for a in range(2):
                                for k in range(DK):
                                    steps.mark(nc.vector.tensor_scalar(wkt[:, k, :, a, :], wk[:, k, :, 1, :], quad[:, 2 * a + 1:2 * a + 2], None, ALU.mult))
                            steps.wait(dve)
                            for a in range(2):
                                for k in range(DK):
                                    nc.vector.scalar_tensor_tensor(half[:, k, :, a, :], wk[:, k, :, 0, :], quad[:, 2 * a:2 * a + 1],
                                                                   wkt[:, k, :, a, :], op0=ALU.mult, op1=ALU.add).then_inc(k_mixed, 1)
                            stats(1, 1)
                            norm.apply(dve, 0, lambda k: xn[:, 0, k])
                            dve.wait_ge(k_mixed, 2 * DK)

                            def low_weights(n, dst):
                                dve.wait_ge(w_hi, n + 1)
                                nc.vector.tensor_tensor(dst[1], W[:, n], dst[0].bitcast(F32), op=ALU.subtract).then_inc(w_lo, 1)
                            for n in (Wq, Wk, Wv):
                                low_weights(n, [w[:, n] for w in wsplit])

                            def low(c, h):
                                dve.wait_ge(xh_ready, c + 1)
                                nc.vector.tensor_tensor(xT[1][:, h].rearrange("p k n -> p (k n)"), ps[:, 0:2].rearrange("p a n -> p (a n)"),
                                                        xT[0][:, h].rearrange("p k n -> p (k n)").bitcast(F32), op=ALU.subtract).then_inc(xl_ready, 1)
                            low(0, 0)

                            def body(c, h):
                                if more(c, 1):
                                    norm.apply(dve, c + 1, lambda k: xn[:, 1 - h, k])
                                if more(c, 2):
                                    stats(c + 2, h)
                                for m in range(2 * DK):
                                    dve.wait_ge(hi_ready, 2 * DK * c + m + 1)
                                    dve.wait_ge(lo_ready, 2 * DK * c + m + 1)
                                    nc.vector.tensor_tensor(rest[:, m], ps[:, 2 + m], part(h, m, 0), op=ALU.subtract).then_inc(rest_ready, 1)
                                if more(c, 1):
                                    low(c + 1, 1 - h)
                            chunks(dve, body)
                            low_weights(Wo, [w[:] for w in wo])

                        @block.scalar
                        def _(act):
                            act.dma_start(quad[:], quad_in.partition_broadcast(P)).then_inc(quad_loaded, 16)
                            act.dma_start(wk[:].rearrange("p k h a c -> p k (h a c)"), by_k(wk_in)).then_inc(w_loaded[Wk], 16)
                            for n, w in ((Wq, wq_in), (Wv, wv_in), (Wo, wo_in)):
                                act.dma_start(W[:, n], by_k(w)).then_inc(w_loaded[n], 16)
                            act.wait_ge(quad_max, 1)
                            nc.scalar.activation(qs[:, 4:8], quad[:], ACT.Exp, bias=qs[:, 1:2]).then_inc(quad_exp, 1)

                            def high(c, h):
                                act.wait_ge(xn_tr, c + 1)
                                nc.scalar.copy(xT[0][:, h].rearrange("p k n -> p (k n)"), ps[:, 0:2].rearrange("p a n -> p (a n)")).then_inc(xh_ready, 1)
                            for n in (Wq, Wk, Wv, Wo):
                                act.wait_ge(w_loaded[n], 16)
                                if n == Wk:
                                    act.wait_ge(k_mixed, 2 * DK)
                                nc.scalar.copy(wsplit[0][:, n] if n != Wo else wo[0][:], W[:, n]).then_inc(w_hi, 1)
                            high(0, 0)

                            def body(c, h):
                                act.wait_ge(stored[h], 16 * (c // 2) + 16)
                                for m in range(2 * DK):
                                    act.wait_ge(qk_done, 2 * DK * c + m + 1)
                                    nc.scalar.copy(part(h, m, 0), ps[:, 2 + m]).then_inc(hi_ready, 1)
                                if more(c, 1):
                                    high(c + 1, 1 - h)
                                for m in range(2 * DK):
                                    act.wait_ge(rest_ready, 2 * DK * c + m + 1)
                                    nc.scalar.copy(part(h, m, 1), rest[:, m]).then_inc(mid_ready, 1)
                                act.wait_ge(v_done, c + 1)
                                nc.scalar.copy(V[:, ds(CT * c, CT), :].rearrange("p t n -> p (t n)"), ps[:, 6:8].rearrange("p a n -> p (a n)")).then_inc(v_kept, 1)
                            chunks(act, body)

                        @block.tensor
                        def _(pe):
                            pe.sem_inc(v_kept, 1)
                            pe.wait_ge(id_ready, 2)

                            def turn(c, h):
                                pe.wait_ge(norm.ready, c + 1)
                                for dk in range(DK):
                                    for k in range(CT):
                                        last = nc.tensor.transpose(ps[:, dk, k * P:(k + 1) * P], xn[:, h, k, dk * P:(dk + 1) * P], ident[:])
                                last.then_inc(xn_tr, 1)
                            turn(0, 0)
                            pe.wait_ge(w_lo, 3)

                            def body(c, h):
                                pe.wait_ge(xl_ready, c + 1)
                                for m in range(2 * DK):
                                    pe.wait_ge(lo_ready, 2 * DK * c + m + 1)
                                    n, cols = m // DK, slice(m % DK * P, (m % DK + 1) * P)
                                    todo = [p for dk in range(DK) for p in split_products([w[:, n, dk, cols] for w in wsplit], [x[:, h, dk] for x in xT])]
                                    for j, (w, x) in enumerate(todo):
                                        last = nc.tensor.matmul(ps[:, 2 + m], w, x, start=(j == 0), stop=(j == len(todo) - 1))
                                    last.then_inc(qk_done, 1)
                                if more(c, 1):
                                    turn(c + 1, 1 - h)
                                pe.wait_ge(v_kept, c + 1)
                                for k in range(CT):
                                    todo = [p for dk in range(DK) for p in split_products([x[:, h, dk, k * P:(k + 1) * P] for x in xT], [w[:, Wv, dk] for w in wsplit])]
                                    for j, (x, w) in enumerate(todo):
                                        last = nc.tensor.matmul(ps[:, 6 + k // 2, (k % 2) * D:(k % 2 + 1) * D], x, w,
                                                                start=(j == 0 and k % 2 == 0), stop=(j == len(todo) - 1), skip_group_check=True)
                                last.then_inc(v_done, 1)
                            chunks(pe, body)

                with ExitStack() as s2:
                    attention(nc, sem, s2, sbuf, ps, ident, identb, KQ, kq_loaded, load_qk, V, xsort, zero, x_zeroed)

            reuse_sems(kept=lasting)

            feed_forward(nc, sem, sbuf, ps, X, V, wo, ident, fastb_in, wfc_in, wproj_in, u_in, v_in, gate_in, by_k)
        ssm(nc, sem, sbuf, ps, X, ident, a_in, bm_in, cm_in, dm_in, lnw_in, lnb_in, wout_in, bout_in, by_k)
        reuse_sems()
        moe(nc, sem, sbuf, ps, X, ident, xsort, x_zeroed, out_tiles, wg_in, bg_in, bias_in, w1_in, b1_in, w2_in, b2_in)


FH = 1024
FK = FH // P
RANK = 16


def feed_forward(nc, sem, sbuf, ps, X, ATT, wo, ident, fastb_in, wfc_in, wproj_in, u_in, v_in, gate_in, by_k):
    with ExitStack() as st:
        wfT = [sbuf(st, f"wfT{a}", [P, DK, FH], F32R) for a in range(2)]
        wpT = sbuf(st, "wpT", [P, FK, D], F32R)
        pscale = sbuf(st, "pscale", [P, D])
        with ExitStack() as s0:
            stage = sbuf(s0, "stage", [P, 2, CT, D])
            aT = [sbuf(s0, f"aT{a}", [P, 2, DK, CW], F32R) for a in range(2)]
            staged, at_tr, ah_ready, al_ready, o_done, o_added = (sem("a_" + n) for n in ("staged", "tr", "hi", "lo", "done", "added"))
            wf = sbuf(s0, "wf", [P, FK, D])
            wp = sbuf(s0, "wp", [P, DK, FH])
            u = sbuf(s0, "u", [P, FK, RANK])
            uT = sbuf(s0, "uT", [RANK, FH])
            fb = sbuf(s0, "fb", [RANK, RANK])
            fbT = sbuf(s0, "fbT", [RANK, RANK])
            v = sbuf(s0, "v", [RANK, D])
            fv = sbuf(s0, "fv", [RANK, D])
            gate = sbuf(s0, "gate", [P, 1])
            NR = FK + DK
            sc = sbuf(s0, "sc", [P, 5, NR])
            spread = sbuf(s0, "spread", [P, DK, P])
            above = sbuf(s0, "above", [P, FK * D + DK * FH])
            f_loaded, p_loaded, small_loaded = sem("wf_loaded"), sem("wp_loaded"), sem("lowrank_loaded")
            mags, f_steps, f_rows, f_tr, f_lr, f_kept, t_done, t_hi, t_lo = (
                sem(n) for n in ("ffn_mags", "ffn_steps", "ffn_rows", "lowrank_tr", "lowrank_done", "lowrank_kept", "ffn_w_tr", "ffn_w_hi", "ffn_w_lo"))
            rows = ([(wf, k, slice(k * D, (k + 1) * D)) for k in range(FK)]
                    + [(wp, k, slice(FK * D + k * FH, FK * D + (k + 1) * FH)) for k in range(DK)])
            QSTEPS = 2 + 3 + DK + 3 * NR
            two = lambda bank: ps[:, bank:bank + 2].rearrange("p a n -> p (a n)")
            flat = lambda v: v.rearrange("p k n -> p (k n)")
            HALF = NC // 2

            def halves(eng, body, between):
                for a in range(2):
                    with eng.Fori(a * HALF // 2, (a + 1) * HALF // 2) as i:
                        for h in range(2):
                            body(2 * i + h, h)
                    if a == 0:
                        between()

            with nc.Block() as block:
                @block.sync
                def _(sp):
                    sp.dma_start(wf[:], by_k(wfc_in)).then_inc(f_loaded, 16)
                    sp.dma_start(wp[:], by_k(wproj_in)).then_inc(p_loaded, 16)
                    sp.dma_start(u[:], by_k(u_in)).then_inc(small_loaded, 16)
                    sp.dma_start(fb[:], fastb_in).then_inc(small_loaded, 16)
                    sp.dma_start(v[:], v_in).then_inc(small_loaded, 16)
                    sp.dma_start(gate[:], gate_in.partition_broadcast(P)).then_inc(small_loaded, 16)

                @block.gpsimd
                def _(pool):
                    with pool.Fori(0, NC // 2) as i:
                        for h in range(2):
                            c = 2 * i + h
                            pool.wait_ge(at_tr, c + 1)
                            nc.gpsimd.tensor_copy(flat(stage[:, h]), flat(ATT[:, ds(CT * c, CT), :])).then_inc(staged, 1)

                @block.scalar
                def _(act):
                    def body(c, h):
                        act.wait_ge(at_tr, c + 3)
                        nc.scalar.copy(flat(aT[0][:, h]), two(0)).then_inc(ah_ready, 1)

                    def magnitudes():
                        act.wait_ge(f_loaded, 16)
                        act.wait_ge(p_loaded, 16)
                        for r, (w, k, n) in enumerate(rows):
                            nc.scalar.activation(above[:, n], w[:, k], ACT.Abs, accum_out=sc[:, 0, r:r + 1]).then_inc(mags, 1)
                    halves(act, body, magnitudes)
                    act.wait_ge(f_tr, 1)
                    nc.scalar.copy(uT[:], two(6)[0:RANK]).then_inc(f_kept, 1)
                    nc.scalar.copy(fbT[:], ps[0:RANK, 0, 0:RANK]).then_inc(f_kept, 1)
                    act.wait_ge(f_lr, 1)
                    nc.scalar.copy(fv[:], ps[0:RANK, 1, 0:D]).then_inc(f_kept, 1)
                    for half, bank in enumerate((2, 4)):
                        act.wait_ge(t_done, half + 1)
                        nc.scalar.copy(flat(wpT[:])[:, half * FH:(half + 1) * FH], two(bank)).then_inc(t_hi, 1)
                    for half, bank in enumerate((0, 6)):
                        act.wait_ge(t_done, half + 3)
                        nc.scalar.copy(wfT[0][:, half], two(bank)).then_inc(t_hi, 1)
                    act.wait_ge(t_done, 5)
                    nc.scalar.copy(pscale[:], ps[:, 2, 0:D]).then_inc(t_hi, 1)

                @block.vector
                def _(dve):
                    dve.sem_inc(o_added, 2)
                    steps = Count(f_steps)

                    def body(c, h):
                        dve.wait_ge(ah_ready, c + 1)
                        nc.vector.tensor_tensor(flat(aT[1][:, h]), two(0), flat(aT[0][:, h]).bitcast(F32), op=ALU.subtract).then_inc(al_ready, 1)
                        dve.wait_ge(o_done, c + 1)
                        chunk = flat(X[:, ds(CT * c, CT), :])
                        nc.vector.tensor_tensor(chunk, two(2 + 2 * h), chunk, op=ALU.add).then_inc(o_added, 1)

                    def quantise():
                        dve.wait_ge(mags, NR)
                        for a, b, n in ((0, FK, D), (FK, NR, FH)):
                            steps.mark(nc.vector.tensor_scalar(sc[:, 1, a:b], sc[:, 0, a:b], 1.0 / n, 1e-5, ALU.mult, ALU.max))
                        steps.wait(dve)
                        for k, f in ((2, 0.5), (3, -0.5), (4, -1.0)):
                            steps.mark(nc.vector.tensor_scalar_mul(sc[:, k], sc[:, 1], f))
                        for k in range(DK):
                            steps.mark(nc.vector.tensor_scalar(spread[:, k], ident[:], 0.0, sc[:, 1, FK + k:FK + k + 1], ALU.mult, ALU.add))
                        steps.wait(dve)
                        for r, (w, k, n) in enumerate(rows):
                            steps.mark(nc.vector.tensor_scalar(above[:, n], w[:, k], sc[:, 2, r:r + 1], None, ALU.is_gt))
                        steps.wait(dve)
                        for r, (w, k, n) in enumerate(rows):
                            steps.mark(nc.vector.scalar_tensor_tensor(above[:, n], w[:, k], sc[:, 3, r:r + 1], above[:, n], op0=ALU.is_lt, op1=ALU.subtract))
                        steps.wait(dve)
                        for r, (w, k, n) in enumerate(rows):
                            steps.mark(nc.vector.tensor_scalar(w[:, k], above[:, n], sc[:, 4, r:r + 1] if r < FK else -1.0, None, ALU.mult))
                        steps.wait(dve)
                    halves(dve, body, quantise)
                    dve.wait_ge(f_lr, 2)
                    for k in range(FK):
                        nc.vector.scalar_tensor_tensor(wf[:, k], ps[:, (6, 7, 0, 1)[k // 2], (k % 2) * D:(k % 2 + 1) * D], gate[:], wf[:, k],
                                                       op0=ALU.mult, op1=ALU.add).then_inc(f_rows, 1)
                    for half, bank in enumerate((0, 6)):
                        dve.wait_ge(t_hi, half + 3)
                        nc.vector.tensor_tensor(wfT[1][:, half], two(bank), wfT[0][:, half].bitcast(F32), op=ALU.subtract).then_inc(t_lo, 1)

                @block.tensor
                def _(pe):
                    pe.sem_inc(at_tr, 2)

                    def turn(c, h):
                        pe.wait_ge(staged, c + 1)
                        for dk in range(DK):
                            for k in range(CT):
                                last = nc.tensor.transpose(ps[:, dk, k * P:(k + 1) * P], stage[:, h, k, dk * P:(dk + 1) * P], ident[:])
                        last.then_inc(at_tr, 1)

                    def body(c, h):
                        turn(c, h)
                        pe.wait_ge(al_ready, c + 1)
                        pe.wait_ge(o_added, c + 1)
                        for k in range(CT):
                            todo = [p for dk in range(DK) for p in split_products([x[:, h, dk, k * P:(k + 1) * P] for x in aT], [w[:, dk] for w in wo])]
                            for j, (x, w) in enumerate(todo):
                                last = nc.tensor.matmul(ps[:, 2 + 2 * h + k // 2, (k % 2) * D:(k % 2 + 1) * D], x, w,
                                                        start=(j == 0 and k % 2 == 0), stop=(j == len(todo) - 1), skip_group_check=True)
                        last.then_inc(o_done, 1)
                    halves(pe, body, lambda: None)
                    pe.wait_ge(small_loaded, 64)
                    for k in range(FK):
                        nc.tensor.transpose(ps[0:RANK, 6 + k // 4, (k % 4) * P:(k % 4 + 1) * P], u[:, k], ident[:])
                    nc.tensor.transpose(ps[0:RANK, 0, 0:RANK], fb[:], ident[0:RANK, 0:RANK]).then_inc(f_tr, 1)
                    pe.wait_ge(f_kept, 2)
                    nc.tensor.matmul(ps[0:RANK, 1, 0:D], fbT[:], v[:], start=True, stop=True).then_inc(f_lr, 1)
                    pe.wait_ge(f_steps, QSTEPS)
                    pe.wait_ge(o_added, NC + 2)
                    for half, bank in enumerate((2, 4)):
                        for k in range(FK):
                            kk, o = divmod(k + half * FK, DK)
                            last = nc.tensor.transpose(ps[:, bank + k // 4, (k % 4) * P:(k % 4 + 1) * P], wp[:, o, kk * P:(kk + 1) * P], ident[:])
                        last.then_inc(t_done, 1)
                    pe.wait_ge(f_kept, 3)
                    for k in range(FK):
                        last = nc.tensor.matmul(ps[:, (6, 7, 0, 1)[k // 2], (k % 2) * D:(k % 2 + 1) * D], uT[:, k * P:(k + 1) * P], fv[:],
                                                start=(k % 2 == 0), stop=True, skip_group_check=True)
                    last.then_inc(f_lr, 1)
                    pe.wait_ge(f_rows, FK)
                    for half, bank in enumerate((0, 6)):
                        for k in range(FK):
                            last = nc.tensor.transpose(ps[:, bank + k // 4, (k % 4) * P:(k % 4 + 1) * P], wf[:, k, half * P:(half + 1) * P], ident[:])
                        last.then_inc(t_done, 1)
                    pe.wait_ge(t_hi, 1)
                    for k in range(DK):
                        last = nc.tensor.matmul(ps[:, 2, k * P:(k + 1) * P], spread[:, k], ident[:], start=True, stop=True, skip_group_check=True)
                    last.then_inc(t_done, 1)

        with ExitStack() as s1:
            xn = sbuf(s1, "f_xn", [P, 2, CT, D])
            xT = [sbuf(s1, f"f_xT{a}", [P, 2, DK, CW], F32R) for a in range(2)]
            relu = sbuf(s1, "relu", [P, 2, CW])
            square = sbuf(s1, "square", [P, 2, CW])
            sq = [sbuf(s1, f"sq{a}", [P, FK, CW], F32R) for a in range(2)]
            scaled = sbuf(s1, "scaled", [P, CT, D])
            norm = ChunkNorm(nc, sem, sbuf, s1, "ln2", X)
            n_tr, xh_ready, xl_ready, h_done, relu_ready, s_ready, hi_ready, lo_ready, o_done, o_scaled, o_added = (
                sem("f_" + n) for n in ("n_tr", "xh_ready", "xl_ready", "h_done", "relu_ready", "s_ready", "hi_ready", "lo_ready", "o_done", "o_scaled", "o_added"))
            HB = 4
            flat = lambda v: v.rearrange("p k n -> p (k n)")
            two = lambda bank: ps[:, bank:bank + 2].rearrange("p a n -> p (a n)")
            with nc.Block() as block:
                @block.gpsimd
                def _(pool):
                    norm.start(pool)
                    for c in range(2):
                        norm.root(pool, c, c)
                    pool.sem_inc(o_added, 1)

                    def add(c):
                        pool.wait_ge(o_scaled, c + 2)
                        chunk = flat(X[:, ds(CT * c, CT), :])
                        nc.gpsimd.tensor_tensor(chunk, flat(scaled[:]), chunk, op=ALU.add).then_inc(o_added, 1)

                    def body(c, h):
                        if not is_first(c):
                            add(c - 1)
                        if more(c, 2):
                            norm.root(pool, c + 2, h)
                    chunks(pool, body, first=True)
                    add(NC - 1)

                @block.vector
                def _(dve):
                    norm.stats(dve, 0, 0)
                    norm.stats(dve, 1, 1)
                    norm.apply(dve, 0, lambda k: xn[:, 0, k])

                    def low(c, h):
                        dve.wait_ge(xh_ready, c + 1)
                        nc.vector.tensor_tensor(flat(xT[1][:, h]), two(0), flat(xT[0][:, h]).bitcast(F32), op=ALU.subtract).then_inc(xl_ready, 1)
                    low(0, 0)
                    dve.sem_inc(o_scaled, 1)
                    dve.sem_inc(lo_ready, 2)

                    def sq_full(c, m):
                        dve.wait_ge(relu_ready, FK * c + m + HB + 1)
                        dve.wait_ge(lo_ready, FK * c + m + 1)
                        nc.vector.tensor_tensor(square[:, m % 2], relu[:, m % 2], relu[:, m % 2], op=ALU.mult).then_inc(s_ready, 1)

                    def sq_low(c, m):
                        dve.wait_ge(hi_ready, FK * c + m + 1)
                        nc.vector.tensor_tensor(sq[1][:, m], square[:, m % 2], sq[0][:, m].bitcast(F32), op=ALU.subtract).then_inc(lo_ready, 1)

                    def scale(c):
                        dve.wait_ge(o_done, c + 1)
                        dve.wait_ge(o_added, c + 1)
                        nc.vector.tensor_tensor(scaled[:], two(6).rearrange("p (k d) -> p k d", d=D),
                                                pscale[:].unsqueeze(1).broadcast_to([P, CT, D]), op=ALU.mult).then_inc(o_scaled, 1)

                    def body(c, h):
                        for m in range(FK):
                            sq_full(c, m)
                            if m > 0:
                                sq_low(c, m - 1)
                            if m == 1 and not is_first(c):
                                scale(c - 1)
                            if m == 2 and more(c, 1):
                                norm.apply(dve, c + 1, lambda k: xn[:, 1 - h, k])
                            if m == 4 and more(c, 2):
                                norm.stats(dve, c + 2, h)
                        sq_low(c, FK - 1)
                        if more(c, 1):
                            low(c + 1, 1 - h)
                    chunks(dve, body, first=True)
                    scale(NC - 1)

                @block.scalar
                def _(act):
                    def high(c, h):
                        act.wait_ge(n_tr, c + 1)
                        nc.scalar.copy(flat(xT[0][:, h]), two(0)).then_inc(xh_ready, 1)
                    high(0, 0)
                    act.sem_inc(s_ready, 2)

                    def sq_high(c, m):
                        act.wait_ge(s_ready, FK * c + m + 3)
                        nc.scalar.copy(sq[0][:, m], square[:, m % 2]).then_inc(hi_ready, 1)

                    def body(c, h):
                        for m in range(FK):
                            act.wait_ge(h_done, FK * c + m + 1)
                            act.wait_ge(s_ready, FK * c + m + 1)
                            nc.scalar.activation(relu[:, m % 2], ps[:, 2 + m % HB], ACT.Relu).then_inc(relu_ready, 1)
                            if m > 0:
                                sq_high(c, m - 1)
                        sq_high(c, FK - 1)
                        if more(c, 1):
                            high(c + 1, 1 - h)
                    chunks(act, body)

                @block.tensor
                def _(pe):
                    def turn(c, h):
                        pe.wait_ge(norm.ready, c + 1)
                        for dk in range(DK):
                            for k in range(CT):
                                last = nc.tensor.transpose(ps[:, dk, k * P:(k + 1) * P], xn[:, h, k, dk * P:(dk + 1) * P], ident[:])
                        last.then_inc(n_tr, 1)
                    turn(0, 0)
                    pe.sem_inc(relu_ready, HB)

                    def body(c, h):
                        pe.wait_ge(xl_ready, c + 1)
                        for m in range(FK):
                            pe.wait_ge(relu_ready, FK * c + m + 1)
                            todo = [p for dk in range(DK) for p in split_products([w[:, dk, m * P:(m + 1) * P] for w in wfT], [x[:, h, dk] for x in xT])]
                            for j, (w, x) in enumerate(todo):
                                last = nc.tensor.matmul(ps[:, 2 + m % HB], w, x, start=(j == 0), stop=(j == len(todo) - 1))
                            last.then_inc(h_done, 1)
                        if more(c, 1):
                            turn(c + 1, 1 - h)
                        pe.wait_ge(o_scaled, c + 1)
                        pe.wait_ge(lo_ready, FK * (c + 1) + 2)
                        for k in range(CT):
                            todo = [(a[:, m, k * P:(k + 1) * P], wpT[:, m]) for m in range(FK) for a in sq]
                            for j, (x, w) in enumerate(todo):
                                last = nc.tensor.matmul(ps[:, 6 + k // 2, (k % 2) * D:(k % 2 + 1) * D], x, w,
                                                        start=(j == 0 and k % 2 == 0), stop=(j == len(todo) - 1), skip_group_check=True)
                        last.then_inc(o_done, 1)
                    chunks(pe, body)


N = 16
GC = P // N
NG = D // GC
SLOT = 4
LEVELS = 7
TPB = SEQ // P
REACH = [1, 2, 4]
GT_, OB_, PT1_ = range(3)
KEPT = PT1_ + len(REACH)


def ssm(nc, sem, sbuf, ps, X, ident, a_in, bm_in, cm_in, dm_in, lnw_in, lnb_in, wout_in, bout_in, by_k):
    zline = nc.dram_tensor("toeplitz_lines", [D, 2 * P], F32, kind="Internal").ap()
    NB = NG // SLOT
    HS = SLOT // 2
    W = GC * NT
    with ExitStack() as st:
        woT = sbuf(st, "woT", [P, DK, D])
        lnwb = sbuf(st, "lnwb", [P, 2, DK])
        turned = sbuf(st, "turned", [P, P])
        Y = sbuf(st, "Y", [P, NT, D])
        with ExitStack() as s0:
            mask = sbuf(s0, "mask", [P, GC])
            bout = sbuf(s0, "bout", [P, D])
            vA = sbuf(s0, "vA", [P, NG, N])
            bB = sbuf(s0, "bB", [P, NG, N])
            ab = sbuf(s0, "ab", [P, NG])
            abt = sbuf(s0, "abt", [P, NG, N])
            rowsB = sbuf(s0, "rowsB", [NG, 2, P])
            rowsD = sbuf(s0, "rowsD", [NG, GC])
            rowsL = sbuf(s0, "rowsL", [DK, 2, P])
            vBC = sbuf(s0, "vBC", [P, 2, NG])
            dcol = sbuf(s0, "dcol", [GC, NG])
            rowBC = sbuf(s0, "rowBC", [GC, 2, NG, N])
            cb = sbuf(s0, "cb", [GC, NG, N])
            k0 = sbuf(s0, "k0", [GC, NG])
            wo = sbuf(s0, "wo_rows", [P, DK, D])
            W1 = sbuf(s0, "W1", [P, SLOT, 2 * P])
            W2 = sbuf(s0, "W2", [P, SLOT, 2 * P])
            Cbd = sbuf(s0, "Cbd", [P, SLOT, GC])
            zk = sbuf(s0, "zk", [GC, 2, SLOT, P])
            zero = sbuf(s0, "zeros", [P, DK, P])
            KM = sbuf(s0, "KM", [P, 2, SLOT, KEPT, P])
            TB = sbuf(s0, "TB", [P, 2, SLOT, GC, P])
            xs = sbuf(s0, "xs", [P, 2, SLOT, GC, NT])
            yl = sbuf(s0, "yl", [P, SLOT, 2, P])
            gm = sbuf(s0, "gm", [P, HS, GC, NT])
            hs = sbuf(s0, "hs", [P, SLOT, NT])
            hm = sbuf(s0, "hm", [P, SLOT, GC, BATCH, TPB])
            c_loaded, small_kept, a_loaded, bc_loaded, z_zeroed, z_turn, t_steps, mz, mask_ready, zero_ready = (
                sem("s_" + n) for n in ("consts_loaded", "small_kept", "a_loaded", "bc_loaded", "z_zeroed", "z_turn", "turned_steps", "mask_steps", "mask_ready", "zero_ready"))
            bc_tr, wo_tr, ab_steps, built, o_copied, k_done, k_kept, gt_done, gt_kept = (
                sem("s_" + n) for n in ("bc_tr", "wo_tr", "ab_steps", "built", "o_copied", "k_done", "k_kept", "gt_done", "gt_kept"))
            xn_done, x_steps, hmz, xs_ready, g_done, g_steps, T_done, T_kept, ks_done, hs_ready, hm_ready, y_done, y_kept = (
                sem("s_" + n) for n in ("xn_done", "x_steps", "hm_zeroed", "xs_ready", "g_done", "g_steps", "T_done", "T_kept", "ks_done", "hs_ready", "hm_ready", "y_done", "y_kept"))
            bb_loaded, pool_turn = sem("s_bb_loaded"), sem("s_pool_turn")
            norm = ChunkNorm(nc, sem, sbuf, s0, "ln3", X)
            assert NC <= LEVELS + 1
            stored = [sem(f"z_stored{z}") for z in range(2)]
            loaded = [[sem(f"t_loaded{z}{j}") for j in range(SLOT)] for z in range(2)]
            lv, w1r, w2r = ([sem(f"s_{n}{h}") for h in range(2)] for n in ("level", "w1_ready", "w2_ready"))
            LV, W1N, W2N = LEVELS + 3, LEVELS + 1, LEVELS + 3
            NS = len(REACH)
            HSN = 2 + NS
            SMALL = 4
            G_BANK, T_BANK, Y_BANK = (5, 6), (7, 5), (6, 7)
            slots = lambda h: range(HS * h, HS * h + HS)
            of_pair = lambda t, h: t[:, HS * h:HS * h + HS]

            def pair(side, h):
                return ps[:, 2 * h + side].rearrange("p (s n) -> p s n", s=HS)
            in_bank = lambda bank, j: ps[:, bank, (j % HS) * W:(j % HS + 1) * W]
            scan = lambda d: ps[:, SMALL, 0:SLOT * NT].rearrange("p (s n) -> p s n", s=SLOT)[:, :, 0:BATCH * (TPB - 1 - d)]
            by_batch = lambda v: v.rearrange("p s (b c) -> p s b c", b=BATCH)

            def batches(eng, body):
                body((0, 0), None)
                with eng.Fori(0, (NB - 2) // 2) as i:
                    body((2 * i + 1, 1), (2 * i, 0))
                    body((2 * i + 2, 0), (2 * i + 1, 1))
                body((NB - 1, 1), (NB - 2, 0))
                body(None, (NB - 1, 1))
            assert NB % 2 == 0

            with nc.Block() as block:
                @block.sync
                def _(sp):
                    sp.dma_start(rowsB[:, 0], bm_in.rearrange("(g c) n -> g (c n)", c=GC)).then_inc(bc_loaded, 16)
                    sp.dma_start(rowsB[:, 1], cm_in.rearrange("(g c) n -> g (c n)", c=GC)).then_inc(bc_loaded, 16)
                    sp.dma_start(rowsD[:], dm_in.rearrange("(g c) -> g c", c=GC)).then_inc(bc_loaded, 16)
                    sp.dma_start(rowsL[:, 0], lnw_in.rearrange("(k p) -> k p", p=P)).then_inc(bc_loaded, 16)
                    sp.dma_start(rowsL[:, 1], lnb_in.rearrange("(k p) -> k p", p=P)).then_inc(bc_loaded, 16)
                    sp.dma_start(vA[:], a_in.rearrange("(g c) n m -> (c n) g m", c=GC)).then_inc(a_loaded, 16)
                    sp.dma_start(rowBC[:, 0], bm_in.rearrange("(g c) n -> c g n", c=GC)).then_inc(a_loaded, 16)
                    sp.dma_start(rowBC[:, 1], cm_in.rearrange("(g c) n -> c g n", c=GC)).then_inc(a_loaded, 16)
                    sp.dma_start(wo[:], by_k(wout_in)).then_inc(c_loaded, 16)
                    sp.dma_start(bout[:], bout_in.partition_broadcast(P)).then_inc(c_loaded, 16)
                    sp.wait_ge(zero_ready, 1)
                    sp.dma_start(zline.rearrange("(k p) n -> p k n", p=P)[:, :, P:2 * P], zero[:]).then_inc(z_zeroed, 16)
                    for z in range(2):
                        sp.sem_inc(stored[z], 16)
                    sp.sem_inc(T_done, 2)
                    sp.wait_ge(z_zeroed, 16)

                    def body(made, used):
                        if made is None:
                            return
                        b, z = made
                        sp.wait_ge(k_kept, 2 * b + 2)
                        sp.sem_inc(z_turn, 1)
                        sp.dma_start(zline.rearrange("(g c) n -> c g n", c=GC)[:, ds(SLOT * b, SLOT), 0:P], zk[:, z]).then_inc(stored[z], 16)
                        sp.wait_ge(stored[z], 16 * (b // 2) + 32)
                        if used is not None:
                            sp.wait_ge(T_done, 2 * b)
                        sp.sem_inc(z_turn, 1)
                        for j in range(SLOT):
                            line = zline.rearrange("(g c) n -> g c n", c=GC)[ds(SLOT * b + j, 1), :, 0:P]
                            sp.dma_start(TB[:, z, j], toeplitz(line)).then_inc(loaded[z][j], 16)
                    batches(sp, body)

                @block.gpsimd
                def _(pool):
                    nc.gpsimd.memset(zero[:], 0.0).then_inc(zero_ready, 1)
                    nc.gpsimd.memset(mask[:], 1.0).then_inc(mz, 1)
                    nc.gpsimd.memset(turned[:], 0.0).then_inc(t_steps, 1)
                    nc.gpsimd.memset(hm[:], 0.0).then_inc(hmz, 1)
                    for c in range(GC):
                        pool.dma_start(bB[c * N:(c + 1) * N], bm_in.rearrange("(g c) m -> c g m", c=GC)[c].partition_broadcast(N)).then_inc(bb_loaded, 16)
                    pool.wait_ge(mz, 1)
                    nc.gpsimd.affine_select(out=mask[:], in_=mask[:], compare_op=ALU.is_ge, fill=0.0, base=0,
                                            pattern=[[-N, GC]], channel_multiplier=1).then_inc(mz, 1)
                    pool.wait_ge(mz, 2)
                    nc.gpsimd.affine_select(out=mask[:], in_=mask[:], compare_op=ALU.is_ge, fill=0.0, base=N - 1,
                                            pattern=[[N, GC]], channel_multiplier=-1).then_inc(mask_ready, 1)
                    pool.wait_ge(t_steps, 1)
                    nc.gpsimd.affine_select(out=turned[:], in_=turned[:], compare_op=ALU.not_equal, fill=1.0, base=1 - P,
                                            pattern=[[1, P]], channel_multiplier=1).then_inc(t_steps, 1)

                    norm.start(pool)
                    for c in range(NC):
                        norm.root(pool, c, c % 2)

                    def body(made, used):
                        if made is None:
                            return
                        b, z = made
                        for h in range(2):
                            pool.wait_ge(w2r[h], W2N * b + LEVELS + 2)
                            pool.sem_inc(pool_turn, 1)
                            nc.gpsimd.tensor_copy(of_pair(KM[:, z], h)[:, :, OB_], of_pair(W2, h)[:, :, 0:P]).then_inc(o_copied, 1)
                        if used is None:
                            pool.wait_ge(xn_done, NC)
                            pool.wait_ge(x_steps, NT // 2)
                        else:
                            pool.wait_ge(T_done, 2 * b)
                        pool.sem_inc(pool_turn, 1)
                        for j in range(SLOT):
                            nc.gpsimd.tensor_copy(xs[:, z, j], Y[:, :, ds(GC * (SLOT * b + j), GC)].rearrange("p t c -> p c t")).then_inc(xs_ready, 1)
                        tiles = ds(NT // NB * b, NT // NB)
                        nc.gpsimd.tensor_tensor(X[:, tiles, :], X[:, tiles, :], bout[:].unsqueeze(1).broadcast_to([P, NT // NB, D]), op=ALU.add)
                    batches(pool, body)

                @block.vector
                def _(dve):
                    dve.wait_ge(a_loaded, 48)
                    dve.wait_ge(bb_loaded, 16 * GC)
                    nc.vector.tensor_tensor(abt[:], vA[:], bB[:], op=ALU.mult).then_inc(ab_steps, 1)
                    nc.vector.tensor_tensor(cb[:], rowBC[:, 0], rowBC[:, 1], op=ALU.mult).then_inc(ab_steps, 1)
                    dve.wait_ge(ab_steps, 2)
                    nc.vector.reduce_sum(ab[:], abt[:], AX).then_inc(ab_steps, 1)
                    nc.vector.reduce_sum(k0[:], cb[:], AX).then_inc(ab_steps, 1)
                    dve.wait_ge(bc_tr, 1)
                    nc.vector.tensor_copy(vBC[:].rearrange("p s g -> p (s g)"), ps[:, 7, 0:2 * NG]).then_inc(ab_steps, 1)
                    nc.vector.tensor_copy(dcol[:], ps[0:GC, 7, 2 * NG:3 * NG]).then_inc(ab_steps, 1)
                    nc.vector.tensor_copy(lnwb[:].rearrange("p s k -> p (s k)"), ps[:, 7, 3 * NG:3 * NG + 2 * DK]).then_inc(ab_steps, 1)
                    dve.wait_ge(ab_steps, 7)
                    nc.vector.tensor_tensor(k0[:], k0[:], dcol[:], op=ALU.add).then_inc(ab_steps, 1)
                    dve.wait_ge(ab_steps, 8)
                    dve.wait_ge(mask_ready, 1)
                    dve.wait_ge(hmz, 1)

                    def build(b):
                        these = ds(SLOT * b, SLOT)
                        for h in range(2):
                            dve.wait_ge(w2r[h], W2N * b + 1)
                        dve.wait_ge(o_copied, 2 * b + 2)
                        spread = mask[:].unsqueeze(1).broadcast_to([P, SLOT, GC])
                        nc.vector.tensor_tensor(W1[:, :, P:2 * P].rearrange("p s (c n) -> p s c n", n=N),
                                                vA[:, these, :].unsqueeze(2).broadcast_to([P, SLOT, GC, N]),
                                                spread.unsqueeze(3).broadcast_to([P, SLOT, GC, N]), op=ALU.mult)
                        nc.vector.tensor_copy(W1[:, :, P - 1], ab[:, these])
                        nc.vector.tensor_copy(W2[:, :, P - 1], vBC[:, 1, these])
                        nc.vector.tensor_tensor(Cbd[:], vBC[:, 1, these].unsqueeze(2).broadcast_to([P, SLOT, GC]), spread, op=ALU.mult).then_inc(built, 1)

                    def keep_level(b, z, l):
                        m = 1 << l
                        for h in range(2):
                            if l <= LEVELS:
                                dve.wait_ge(lv[h], LV * b + l + 2)
                                src, dst = pair(0, h), of_pair(W1, h)
                                if l < LEVELS:
                                    nc.vector.tensor_copy(dst[:, :, P - 2 * m:P - m], src[:, :, 0:m])
                                o = m if l < LEVELS else 0
                                nc.vector.tensor_copy(dst[:, :, P:2 * P], src[:, :, o:o + P]).then_inc(w1r[h], 1)
                        small = ps[:, SMALL].rearrange("p (s n) -> p s n", n=P)
                        if l == LEVELS:
                            dve.wait_ge(k_done, b + 1)
                            dve.wait_ge(stored[z], 16 * (b // 2) + 16)
                            nc.vector.tensor_copy(zk[:, z, :, 0:P - 1], small[0:GC, :, 1:P]).then_inc(k_kept, 1)
                            nc.vector.tensor_copy(zk[:, z, :, P - 1:P], k0[:, ds(SLOT * b, SLOT)].unsqueeze(2)).then_inc(k_kept, 1)
                        if l == LEVELS + 1:
                            dve.wait_ge(gt_done, b + 1)
                            nc.vector.tensor_copy(KM[:, z, :, GT_], small).then_inc(gt_kept, 1)

                    def beside_first(l):
                        if l < NC:
                            norm.stats(dve, l, l % 2)
                        if 0 < l <= NC:
                            tiles = slice(CT * (l - 1), CT * l)
                            norm.apply(dve, l - 1, lambda k: Y[:, tiles.start + k], ready=xn_done)
                            dve.wait_ge(xn_done, l)
                            for t in range(tiles.start, tiles.stop, 2):
                                two = lambda v: v[:, t:t + 2, :].rearrange("p a d -> p (a d)")
                                nc.vector.tensor_tensor(two(X), two(X), two(Y), op=ALU.add).then_inc(x_steps, 1)

                    def recur(b, l):
                        if l < 2:
                            p = l
                            dve.wait_ge(g_done, 2 * b + p + 1)
                            if p > 0:
                                dve.wait_ge(hs_ready, HSN * b + p)
                            for j in slots(p):
                                nc.vector.tensor_tensor(gm[:, j % HS], in_bank(G_BANK[p], j).rearrange("p (c t) -> p c t", c=GC),
                                                        mask[:].unsqueeze(2).broadcast_to([P, GC, NT]), op=ALU.mult).then_inc(g_steps, 1)
                            dve.wait_ge(g_steps, HS * (2 * b + p + 1))
                            nc.vector.reduce_sum(of_pair(hs, p), gm[:].rearrange("p s c t -> p s t c"), AX).then_inc(hs_ready, 1)
                        elif l < 2 + NS:
                            d = REACH[l - 2]
                            dve.wait_ge(ks_done, NS * b + l - 1)
                            dve.wait_ge(hs_ready, HSN * b + l)
                            for j in range(SLOT):
                                v = by_batch(hs[:, j:j + 1])[:, 0, :, d:TPB - 1]
                                last = nc.vector.tensor_tensor(v, by_batch(scan(d)[:, j:j + 1])[:, 0], v, op=ALU.add)
                            last.then_inc(hs_ready, 1)
                        elif l < 4 + NS:
                            dve.wait_ge(hs_ready, HSN * b + HSN)
                            for j in slots(l - 2 - NS):
                                before = by_batch(hs[:, j:j + 1])[:, 0, :, 0:TPB - 1]
                                nc.vector.tensor_tensor(hm[:, j, :, :, 1:TPB], before.unsqueeze(1).broadcast_to([P, GC, BATCH, TPB - 1]),
                                                        mask[:].unsqueeze(2).unsqueeze(3).broadcast_to([P, GC, BATCH, TPB - 1]), op=ALU.mult).then_inc(hm_ready, 1)

                    def body(made, used):
                        if made is not None:
                            build(made[0])
                        for l in range(LEVELS + 2):
                            if made is not None:
                                keep_level(*made, l)
                            if used is not None:
                                recur(used[0], l)
                            else:
                                beside_first(l)
                    batches(dve, body)

                @block.scalar
                def _(act):
                    act.wait_ge(wo_tr, 1)
                    nc.scalar.copy(woT[:].rearrange("p k n -> p (k n)"), ps[:, 5]).then_inc(small_kept, 1)
                    act.sem_inc(o_copied, 2)
                    for h in range(2):
                        act.sem_inc(w2r[h], 1)
                    act.sem_inc(T_kept, 2)
                    act.sem_inc(y_kept, 2)

                    def keep_level(b, z, l):
                        m = 1 << l
                        for h in range(2):
                            act.wait_ge(lv[h], LV * b + l + 2)
                            src, dst = pair(1, h), of_pair(W2, h)
                            o = m if l < LEVELS else 0
                            if l < LEVELS:
                                nc.scalar.copy(dst[:, :, P - 2 * m:P - m], src[:, :, 0:m])
                            if l >= LEVELS - 1:
                                last = nc.scalar.copy(of_pair(KM[:, z], h)[:, :, PT1_ + l - LEVELS + 1], src[:, :, o:o + P])
                            if l <= LEVELS:
                                last = nc.scalar.copy(dst[:, :, P:2 * P], src[:, :, o:o + P])
                            last.then_inc(w2r[h], 1)

                    def recur(b, l):
                        first = 2 + NS
                        if first <= l < first + 2:
                            p = l - first
                            act.wait_ge(T_done, 2 * b + p + 3)
                            nc.scalar.copy(of_pair(yl, p).rearrange("p s q n -> p (s q n)"), ps[:, T_BANK[p]]).then_inc(T_kept, 1)
                        elif first + 2 <= l:
                            p = l - first - 2
                            act.wait_ge(y_done, 2 * b + p + 1)
                            nc.scalar.copy(Y[:, :, ds(GC * (SLOT * b + HS * p), HS * GC)], ps[:, Y_BANK[p]].rearrange("p (c t) -> p t c", t=NT)).then_inc(y_kept, 1)

                    def body(made, used):
                        if made is not None:
                            b = made[0]
                            for h in range(2):
                                act.wait_ge(lv[h], LV * b + 1)
                                nc.scalar.copy(of_pair(W2, h)[:, :, P:2 * P], pair(1, h)[:, :, 0:P]).then_inc(w2r[h], 1)
                        for l in range(LEVELS + 2):
                            if made is not None:
                                keep_level(*made, l)
                            if used is not None:
                                recur(used[0], l)
                    batches(act, body)

                @block.tensor
                def _(pe):
                    pe.wait_ge(bc_loaded, 80)
                    for s in range(2):
                        nc.tensor.transpose(ps[:, 7, s * NG:(s + 1) * NG], rowsB[:, s], ident[0:NG, 0:NG])
                    nc.tensor.transpose(ps[0:GC, 7, 2 * NG:3 * NG], rowsD[:], ident[0:NG, 0:NG])
                    for s in range(2):
                        last = nc.tensor.transpose(ps[:, 7, 3 * NG + s * DK:3 * NG + (s + 1) * DK], rowsL[:, s], ident[0:DK, 0:DK])
                    last.then_inc(bc_tr, 1)
                    pe.wait_ge(c_loaded, 32)
                    for dk in range(DK):
                        for o in range(DK):
                            last = nc.tensor.transpose(ps[:, 5, dk * D + o * P:dk * D + (o + 1) * P], wo[:, o, dk * P:(dk + 1) * P], ident[:])
                    last.then_inc(wo_tr, 1)
                    pe.wait_ge(small_kept, 1)

                    def inputs(b, z, p):
                        if p == 0:
                            pe.wait_ge(gt_kept, b + 1)
                            pe.wait_ge(T_kept, 2 * b + 2)
                        else:
                            pe.wait_ge(y_kept, 2 * b + 1)
                        for j in slots(p):
                            pe.wait_ge(xs_ready, SLOT * b + j + 1)
                            last = nc.tensor.matmul(in_bank(G_BANK[p], j), KM[:, z, j, GT_], xs[:, z, j].rearrange("p c t -> p (c t)"), start=True, stop=True, skip_group_check=True)
                        last.then_inc(g_done, 1)

                    def recur(b, z, l):
                        if 2 <= l < 2 + NS:
                            k, d = l - 2, REACH[l - 2]
                            if k == 0:
                                for h in range(2):
                                    pe.wait_ge(w2r[h], W2N * b + W2N + 1)
                            pe.wait_ge(hs_ready, HSN * b + l)
                            for j in range(SLOT):
                                last = nc.tensor.matmul(scan(d)[:, j], KM[:, z, j, PT1_ + k], by_batch(hs[:, j:j + 1])[:, 0, :, 0:TPB - 1 - d],
                                                        start=True, stop=True, skip_group_check=True)
                            last.then_inc(ks_done, 1)
                        elif 2 + NS <= l < 4 + NS:
                            p = l - 2 - NS
                            if p == 0:
                                pe.wait_ge(y_kept, 2 * b + 2)
                            for j in slots(p):
                                pe.wait_ge(loaded[z][j], 16 * (b // 2) + 16)
                                for q in range(2):
                                    for c in range(4):
                                        last = nc.tensor.matmul(in_bank(T_BANK[p], j)[NT * c:NT * (c + 1), q * P:(q + 1) * P],
                                                                xs[:, z, j, 4 * q + c], TB[:, z, j, 4 * q + c], start=True, stop=True, skip_group_check=True)
                            last.then_inc(T_done, 1)
                        elif 4 + NS <= l:
                            p = l - 4 - NS
                            pe.wait_ge(o_copied, 2 * b + 4)
                            pe.wait_ge(T_kept, 2 * b + p + 3)
                            for j in slots(p):
                                pe.wait_ge(hm_ready, SLOT * b + j + 1)
                                nc.tensor.matmul(in_bank(Y_BANK[p], j), KM[:, z, j, OB_], hm[:, j].rearrange("p c b t -> p (c b t)"), start=True, stop=False, skip_group_check=True)
                                for q in range(2):
                                    last = nc.tensor.matmul(in_bank(Y_BANK[p], j)[:, q * P:(q + 1) * P], yl[:, j, q], ident[:], start=False, stop=(q == 1), skip_group_check=True)
                            last.then_inc(y_done, 1)

                    def level(b, l):
                        m = 1 << l
                        for h in range(2):
                            if l > 0:
                                pe.wait_ge(w1r[h], W1N * b + l)
                            pe.wait_ge(w2r[h], W2N * b + l + 2)
                            c = m if l < LEVELS else 0
                            for s in slots(h):
                                if l <= LEVELS:
                                    nc.tensor.matmul(pair(0, h)[:, s % HS, 0:c + P], W2[:, s, P:2 * P], W1[:, s, P - c:2 * P], start=True, stop=True, skip_group_check=True)
                                last = nc.tensor.matmul(pair(1, h)[:, s % HS, 0:c + P], W1[:, s, P:2 * P], W2[:, s, P - c:2 * P], start=True, stop=True, skip_group_check=True)
                            last.then_inc(lv[h], 1)

                    def body(made, used):
                        if used is not None:
                            for p in range(2):
                                inputs(*used, p)
                        if made is not None:
                            b = made[0]
                            pe.wait_ge(built, b + 1)
                            for h in range(2):
                                for s in slots(h):
                                    last = nc.tensor.transpose(pair(1, h)[:, s % HS, 0:P], W1[:, s, P:2 * P], ident[:])
                                last.then_inc(lv[h], 1)
                        for l in range(LEVELS + 2):
                            if made is not None:
                                if l == LEVELS:
                                    if used is not None:
                                        pe.wait_ge(hs_ready, HSN * b)
                                    for h in range(2):
                                        pe.wait_ge(w1r[h], W1N * b + l)
                                    for s in range(SLOT):
                                        last = nc.tensor.matmul(ps[0:GC, SMALL, s * P:(s + 1) * P], Cbd[:, s], W1[:, s, 0:P], start=True, stop=True, skip_group_check=True)
                                    last.then_inc(k_done, 1)
                                if l == LEVELS + 1:
                                    pe.wait_ge(k_kept, 2 * b + 1)
                                    for s in range(SLOT):
                                        last = nc.tensor.transpose(ps[:, SMALL, s * P:(s + 1) * P], W1[:, s, 0:P], ident[:])
                                    last.then_inc(gt_done, 1)
                                level(b, l)
                            if used is not None:
                                recur(*used, l)
                    batches(pe, body)

        ssm_output(nc, sem, sbuf, ps, X, Y, ident, woT, lnwb, turned)


def toeplitz(line):
    a = line.rearrange("a c n -> (a c) n")
    return bass.AP(tensor=a.tensor, offset=a.offset, ap=[[1, P], *a.ap])


def ssm_output(nc, sem, sbuf, ps, X, Y, ident, woT, lnwb, turned):
    with ExitStack() as st:
        yn = sbuf(st, "yn", [P, 2, CT, D])
        gT = sbuf(st, "gT", [P, 2, DK, CW])
        norm = ChunkNorm(nc, sem, sbuf, st, "lny", Y)
        n_tr, g_ready, o_done, o_added = (sem("so_" + n) for n in ("n_tr", "g_ready", "done", "added"))
        with nc.Block() as block:
            @block.gpsimd
            def _(pool):
                norm.start(pool)
                for c in range(2):
                    norm.root(pool, c, c)

                def body(c, h):
                    if more(c, 2):
                        norm.root(pool, c + 2, h)
                chunks(pool, body)

            @block.vector
            def _(dve):
                dve.sem_inc(o_added, 2)
                norm.stats(dve, 0, 0)
                norm.stats(dve, 1, 1)
                norm.apply(dve, 0, lambda k: yn[:, 0, k])

                def body(c, h):
                    if more(c, 1):
                        norm.apply(dve, c + 1, lambda k: yn[:, 1 - h, k])
                    if more(c, 2):
                        norm.stats(dve, c + 2, h)
                    dve.wait_ge(o_done, c + 1)
                    chunk = X[:, ds(CT * c, CT), :].rearrange("p k d -> p (k d)")
                    nc.vector.tensor_tensor(chunk, ps[:, 4 + 2 * h:6 + 2 * h].rearrange("p a n -> p (a n)"), chunk, op=ALU.add).then_inc(o_added, 1)
                chunks(dve, body)

            @block.scalar
            def _(act):
                def body(c, h):
                    act.wait_ge(n_tr, c + 1)
                    act.wait_ge(o_added, c + 1)
                    for dk in range(DK):
                        nc.scalar.activation(gT[:, h, dk], ps[:, 2 * h + dk], ACT.Gelu, bias=lnwb[:, 1, dk:dk + 1], scale=lnwb[:, 0, dk:dk + 1]).then_inc(g_ready, 1)
                chunks(act, body)

            @block.tensor
            def _(pe):
                def turn(c, h):
                    pe.wait_ge(norm.ready, c + 1)
                    for dk in range(DK):
                        for k in range(CT):
                            last = nc.tensor.matmul(ps[:, 2 * h + dk, k * P:(k + 1) * P], yn[:, h, k, dk * P:(dk + 1) * P], turned[:],
                                                    start=True, stop=True, skip_group_check=True)
                    last.then_inc(n_tr, 1)
                turn(0, 0)

                def body(c, h):
                    if more(c, 1):
                        turn(c + 1, 1 - h)
                    pe.wait_ge(g_ready, DK * (c + 1))
                    pe.wait_ge(o_added, c + 1)
                    for k in range(CT):
                        for dk in range(DK):
                            last = nc.tensor.matmul(ps[:, 4 + 2 * h + k // 2, (k % 2) * D:(k % 2 + 1) * D], gT[:, h, dk, k * P:(k + 1) * P], woT[:, dk],
                                                    start=(dk == 0 and k % 2 == 0), stop=(dk == DK - 1), skip_group_check=True)
                    last.then_inc(o_done, 1)
                chunks(pe, body)


def moe(nc, sem, sbuf, ps, X, ident, xsort, x_zeroed, out_tiles, wg_in, bg_in, bias_in, w1_in, b1_in, w2_in, b2_in):
    ysort = nc.dram_tensor("outputs_by_expert", [MT * P, D], F32, kind="Internal").ap()
    with ExitStack() as st:
        W1 = sbuf(st, "eW1", [P, E, DK, EH])
        W2 = sbuf(st, "eW2", [P, E, EK, D])
        b1T = sbuf(st, "b1T", [P, E * EK])
        slot = sbuf(st, "slot", [P, 2, NT], U32)
        weight = sbuf(st, "weight", [P, 2, NT])
        owner = sbuf(st, "owner", [P, MT], I32)
        w_loaded = [sem(f"e_w_loaded{q}") for q in range(2)]
        placed = sem("e_placed")
        with ExitStack() as s0:
            xc = sbuf(s0, "e_xn", [P, 2, CT, D])
            xT = sbuf(s0, "e_xT", [P, 2, DK, CW])
            wg = sbuf(s0, "wg", [P, DK, E])
            bgb = sbuf(s0, "bgb", [P, 2, E])
            b1r = sbuf(s0, "b1r", [E * EK, P])
            L, hot1, hot2, tmp, S, C, C2 = (sbuf(s0, "r_" + n, [P, NT, E]) for n in ("logits", "hot1", "hot2", "tmp", "slots", "sums", "sums2"))
            top, at = (sbuf(s0, "r_" + n, [P, 2, NT]) for n in ("top", "at"))
            ex = sbuf(s0, "r_exp", [P, 3, NT])
            place = sbuf(s0, "r_place", [P, 2, 2, CT], U32)
            held = sbuf(s0, "r_held", [P, MT, E])
            ended = sbuf(s0, "r_ended", [P, MT])
            ne = sbuf(s0, "r_ne", [P, 4, E])
            ni = sbuf(s0, "r_ni", [P, 2, E], I32)
            ei, ti = sbuf(s0, "r_ei", [P, E], I32), sbuf(s0, "r_ti", [P, MT], I32)
            ef, tf = sbuf(s0, "r_ef", [P, E]), sbuf(s0, "r_tf", [P, MT])
            before, ones = sbuf(s0, "r_before", [P, P]), sbuf(s0, "r_ones", [P, P])
            norm = ChunkNorm(nc, sem, sbuf, s0, "ln4", X)
            small, x_tr, xT_ready, lg_done, b1_tr, b1_kept, r_steps, r_exp, c_ready, c_done, iotas = (
                sem("r_" + n) for n in ("small_loaded", "x_tr", "xT_ready", "logits_done", "b1_tr", "b1_kept", "steps", "exp", "consts", "counted", "iotas"))
            hot_ready, gap_ready, slots_ready, row_ready, scatter_turn = (sem("r_" + n) for n in ("hot_ready", "gap_ready", "slots_ready", "row_ready", "scatter_turn"))
            scattered = [sem(f"r_scattered{h}") for h in range(2)]
            with nc.Block() as block:
                @block.sync
                def _(sp):
                    sp.dma_start(wg[:], wg_in.rearrange("(k p) e -> p k e", p=P)).then_inc(small, 16)
                    sp.dma_start(bgb[:, 0], bg_in.partition_broadcast(P)).then_inc(small, 16)
                    sp.dma_start(bgb[:, 1], bias_in.partition_broadcast(P)).then_inc(small, 16)
                    sp.dma_start(b1r[:], b1_in.rearrange("e (k p) -> (e k) p", p=P)).then_inc(small, 16)
                    for q in range(4):
                        es = slice(q * E // 4, (q + 1) * E // 4)
                        sp.dma_start(W1[:, es], w1_in[es].rearrange("e (k p) h -> p e k h", p=P)).then_inc(w_loaded[0], 16)
                        sp.dma_start(W2[:, es], w2_in[es].rearrange("e (k p) d -> p e k d", p=P)).then_inc(w_loaded[1], 16)

                @block.gpsimd
                def _(pool):
                    nc.gpsimd.memset(ones[:], 1.0).then_inc(c_ready, 1)
                    pool.wait_ge(c_ready, 1)
                    nc.gpsimd.affine_select(out=before[:], in_=ones[:], compare_op=ALU.is_ge, fill=0.0, base=-1,
                                            pattern=[[1, P]], channel_multiplier=-1).then_inc(c_ready, 1)
                    nc.gpsimd.iota(ei[:], pattern=[[1, E]], base=-E, channel_multiplier=0).then_inc(iotas, 1)
                    nc.gpsimd.iota(ti[:], pattern=[[1, MT]], base=0, channel_multiplier=0).then_inc(iotas, 1)
                    norm.start(pool)
                    for c in range(2):
                        norm.root(pool, c, c)

                    def body(c, h):
                        if more(c, 2):
                            norm.root(pool, c + 2, h)
                    chunks(pool, body)
                    pool.wait_ge(x_zeroed, 16 * UNITS)
                    pool.wait_ge(slots_ready, 2)
                    with pool.Fori(0, NC // 2) as i:
                        for h in range(2):
                            c = 2 * i + h
                            pool.wait_ge(row_ready, c + 1)
                            pool.sem_inc(scatter_turn, 1)
                            for k in range(CT):
                                for s in range(2):
                                    nc.gpsimd.indirect_dma_start(xsort, bass.IndirectOffsetOnAxis(ap=place[:, h, s, k:k + 1], axis=0),
                                                                 xc[:, h, k], None).then_inc(scattered[h], 16)
                    for h in range(2):
                        pool.wait_ge(scattered[h], 16 * 2 * CT * (NC // 2))

                @block.vector
                def _(dve):
                    norm.stats(dve, 0, 0)
                    norm.stats(dve, 1, 1)
                    norm.apply(dve, 0, lambda k: xc[:, 0, k])

                    def body(c, h):
                        if more(c, 1):
                            dve.wait_ge(x_tr, c + 1)
                            norm.apply(dve, c + 1, lambda k: xc[:, 1 - h, k])
                        if more(c, 2):
                            norm.stats(dve, c + 2, h)
                    chunks(dve, body)
                    dve.wait_ge(b1_tr, 1)
                    nc.vector.tensor_copy(b1T[:], ps[:, 7, 0:E * EK]).then_inc(b1_kept, 1)
                    steps = Count(r_steps)

                    def step(ins):
                        steps.mark(ins)
                        steps.wait(dve)
                    of_e = lambda v: v.unsqueeze(1).broadcast_to([P, NT, E])
                    of_t = lambda v: v.unsqueeze(2).broadcast_to([P, NT, E])
                    dve.wait_ge(iotas, 2)
                    steps.mark(nc.vector.tensor_copy(ef[:], ei[:]))
                    step(nc.vector.tensor_copy(tf[:], ti[:]))
                    dve.wait_ge(small, 64)
                    dve.wait_ge(lg_done, NC)
                    step(nc.vector.tensor_tensor(L[:], ps[:, 4].rearrange("p (t e) -> p t e", e=E), of_e(bgb[:, 0]), op=ALU.add))
                    step(nc.vector.tensor_tensor(L[:], L[:], of_e(bgb[:, 1]), op=ALU.add))
                    for s, hot in enumerate((hot1, hot2)):
                        step(nc.vector.reduce_max(top[:, s], L[:], AX))
                        step(nc.vector.tensor_tensor(tmp[:], L[:], of_t(top[:, s]), op=ALU.is_equal))
                        step(nc.vector.tensor_tensor(tmp[:], tmp[:], of_e(ef[:]), op=ALU.mult))
                        step(nc.vector.tensor_reduce(at[:, s], tmp[:], AX, ALU.min))
                        step(nc.vector.tensor_tensor(hot[:], of_t(at[:, s]), of_e(ef[:]), op=ALU.is_equal))
                        if s == 0:
                            step(nc.vector.scalar_tensor_tensor(L[:], hot[:], -3e38, L[:], op0=ALU.mult, op1=ALU.add))
                    nc.vector.tensor_tensor(tmp[:], hot1[:], hot2[:], op=ALU.add).then_inc(hot_ready, 1)
                    nc.vector.tensor_tensor(ex[:, 0], top[:, 1], top[:, 0], op=ALU.subtract).then_inc(gap_ready, 1)
                    dve.wait_ge(c_done, 1)
                    tot = ps[:, 6].rearrange("p (t e) -> p t e", e=E)
                    pre = ps[:, 5].rearrange("p (t e) -> p t e", e=E)
                    step(nc.vector.tensor_copy(C[:], tot))
                    a, b, d = C, C2, 1
                    while d < NT:
                        steps.mark(nc.vector.tensor_tensor(b[:, d:NT], a[:, d:NT], a[:, 0:NT - d], op=ALU.add))
                        step(nc.vector.tensor_copy(b[:, 0:d], a[:, 0:d]))
                        a, b, d = b, a, 2 * d
                    step(nc.vector.tensor_scalar(ni[:, 0], a[:, NT - 1], float(P - 1), None, ALU.add))
                    step(nc.vector.tensor_scalar(ni[:, 1], ni[:, 0], P.bit_length() - 1, None, ALU.arith_shift_right))
                    step(nc.vector.tensor_copy(ne[:, 0], ni[:, 1]))
                    step(nc.vector.tensor_copy(ne[:, 1], ne[:, 0]))
                    x, y, d = 1, 2, 1
                    while d < E:
                        steps.mark(nc.vector.tensor_tensor(ne[:, y, d:E], ne[:, x, d:E], ne[:, x, 0:E - d], op=ALU.add))
                        step(nc.vector.tensor_copy(ne[:, y, 0:d], ne[:, x, 0:d]))
                        x, y, d = y, x, 2 * d
                    step(nc.vector.tensor_tensor(ne[:, 3], ne[:, x], ne[:, 0], op=ALU.subtract))
                    step(nc.vector.tensor_scalar_mul(ne[:, 3], ne[:, 3], float(P)))
                    step(nc.vector.tensor_tensor(S[:], a[:], tot, op=ALU.subtract))
                    step(nc.vector.tensor_tensor(S[:], S[:], pre, op=ALU.add))
                    step(nc.vector.tensor_tensor(S[:], S[:], of_e(ne[:, 3]), op=ALU.add))
                    for s, hot in enumerate((hot1, hot2)):
                        step(nc.vector.tensor_tensor(tmp[:], hot[:], S[:], op=ALU.mult))
                        step(nc.vector.reduce_sum(at[:, s], tmp[:], AX))
                        nc.vector.tensor_copy(slot[:, s], at[:, s]).then_inc(slots_ready, 1)
                    dve.wait_ge(x_tr, NC + 1)
                    dve.wait_ge(slots_ready, 2)

                    def rows(c, h):
                        nc.vector.tensor_copy(place[:, h], slot[:, :, ds(CT * c, CT)])
                        norm.apply(dve, c, lambda k: xc[:, h, k], ready=row_ready)
                    rows(0, 0)
                    rows(1, 1)
                    with dve.Fori(1, NC // 2) as i:
                        for h in range(2):
                            dve.wait_ge(scattered[h], 16 * 2 * CT * i)
                            rows(2 * i + h, h)
                    step(nc.vector.tensor_tensor(held[:], ne[:, x].unsqueeze(1).broadcast_to([P, MT, E]), tf[:].unsqueeze(2).broadcast_to([P, MT, E]), op=ALU.is_le))
                    step(nc.vector.reduce_sum(ended[:], held[:], AX))
                    step(nc.vector.tensor_scalar(owner[:], ended[:], float(E - 1), None, ALU.min))
                    dve.wait_ge(r_exp, 1)
                    step(nc.vector.tensor_scalar(ex[:, 2], ex[:, 1], 1.0, None, ALU.add))
                    step(nc.vector.reciprocal(weight[:, 0], ex[:, 2]))
                    step(nc.vector.tensor_tensor(weight[:, 1], ex[:, 1], weight[:, 0], op=ALU.mult))

                @block.scalar
                def _(act):
                    def body(c, h):
                        act.wait_ge(x_tr, c + 2)
                        nc.scalar.copy(xT[:, h].rearrange("p k n -> p (k n)"), ps[:, 2 * h:2 * h + 2].rearrange("p a n -> p (a n)")).then_inc(xT_ready, 1)
                    chunks(act, body)
                    act.wait_ge(gap_ready, 1)
                    nc.scalar.activation(ex[:, 1], ex[:, 0], ACT.Exp).then_inc(r_exp, 1)

                @block.tensor
                def _(pe):
                    pe.wait_ge(small, 64)
                    nc.tensor.transpose(ps[:, 7, 0:E * EK], b1r[:], ident[0:E * EK, 0:E * EK]).then_inc(b1_tr, 1)

                    pe.sem_inc(x_tr, 1)

                    def turn(c, h):
                        pe.wait_ge(norm.ready, c + 1)
                        for dk in range(DK):
                            for k in range(CT):
                                last = nc.tensor.transpose(ps[:, 2 * h + dk, k * P:(k + 1) * P], xc[:, h, k, dk * P:(dk + 1) * P], ident[:])
                        last.then_inc(x_tr, 1)
                    turn(0, 0)

                    def body(c, h):
                        if more(c, 1):
                            turn(c + 1, 1 - h)
                        pe.wait_ge(xT_ready, c + 1)
                        for k in range(CT):
                            for dk in range(DK):
                                last = nc.tensor.matmul(ps[:, 4, ds(E * (CT * c + k), E)], xT[:, h, dk, k * P:(k + 1) * P], wg[:, dk],
                                                        start=(dk == 0), stop=(dk == DK - 1), skip_group_check=True)
                        last.then_inc(lg_done, 1)
                    chunks(pe, body)
                    pe.wait_ge(c_ready, 2)
                    pe.wait_ge(hot_ready, 1)
                    chosen = tmp[:].rearrange("p t e -> p (t e)")
                    nc.tensor.matmul(ps[:, 5], before[:], chosen, start=True, stop=True)
                    nc.tensor.matmul(ps[:, 6], ones[:], chosen, start=True, stop=True).then_inc(c_done, 1)

        with ExitStack() as s1:
            AHEAD = 4
            xin = sbuf(s1, "e_xin", [P, AHEAD, D])
            xT = sbuf(s1, "e_xinT", [P, 2, DK, P])
            hid = sbuf(s1, "e_hidden", [P, 2, EH])
            hT = sbuf(s1, "e_hiddenT", [P, 2, EK, P])
            y = sbuf(s1, "e_y", [P, 2, D])
            b2b = sbuf(s1, "b2b", [P, E, D])
            x_loaded = [sem(f"e_x_loaded{r}") for r in range(AHEAD)]
            stored = [sem(f"e_y_stored{z}") for z in range(2)]
            b2_loaded, xt_done, xt_kept, m1_done, h_kept, ht_done, hta_kept, htb_kept, m2_done, y_kept, y_turn = (
                sem("e_" + n) for n in ("b2_loaded", "xt_done", "xt_kept", "m1_done", "h_kept", "ht_done", "hta_kept", "htb_kept", "m2_done", "y_kept", "y_turn"))
            assert AHEAD % 2 == 0 and MT % AHEAD == 0
            XT_BANK, H_BANK, HT_BANK, Y_BANK = (0, 7), (1, 2), (3, 4), (5, 6)
            HK = EK // 2
            of_tile = lambda eng, k: eng.value_load(owner[0:1, ds(k, 1)] if not isinstance(k, int) else owner[0:1, k:k + 1], min_val=0, max_val=E - 1)

            def tiles(eng, body):
                body(0, 0)
                with eng.Fori(0, MT // AHEAD - 1) as i:
                    for r in range(1, AHEAD + 1):
                        body(AHEAD * i + r, r % AHEAD)
                for r in range(1, AHEAD):
                    body(MT - AHEAD + r, r)
            with nc.Block() as block:
                @block.sync
                def _(sp):
                    def load(k, r):
                        sp.dma_start(xin[:, r], xsort[ds(P * k, P), :]).then_inc(x_loaded[r], 16)

                    def store(k, r):
                        sp.wait_ge(y_kept, k + 3)
                        sp.sem_inc(y_turn, 1)
                        sp.dma_start(ysort[ds(P * k, P), :], y[:, r % 2]).then_inc(stored[r % 2], 16)
                    for r in range(AHEAD):
                        load(r, r)
                    sp.dma_start(b2b[:], b2_in.partition_broadcast(P)).then_inc(b2_loaded, 16)
                    for z in range(2):
                        sp.sem_inc(stored[z], 16)
                    with sp.Fori(0, MT // AHEAD - 1) as i:
                        for r in range(AHEAD):
                            store(AHEAD * i + r, r)
                            load(AHEAD * i + r + AHEAD, r)
                    for r in range(AHEAD):
                        store(MT - AHEAD + r, r)
                    for z in range(2):
                        sp.wait_ge(stored[z], 16 * (MT // 2 + 1))

                @block.scalar
                def _(act):
                    def body(k, r):
                        z = r % 2
                        act.wait_ge(xt_done, k + 1)
                        nc.scalar.copy(xT[:, z].rearrange("p k n -> p (k n)"), ps[:, XT_BANK[z], 0:D]).then_inc(xt_kept, 1)
                        if isinstance(k, int) and k == 0:
                            return
                        half(k - 1, 1 - z)

                    def half(k, z):
                        e = of_tile(act, k)
                        act.wait_ge(ht_done, k + 1)
                        for j in range(HK):
                            nc.scalar.activation(hT[:, z, j], ps[:, HT_BANK[0], j * P:(j + 1) * P], ACT.Relu, bias=b1T[:, ds(EK * e + j, 1)]).then_inc(hta_kept, 1)
                    tiles(act, body)
                    half(MT - 1, 1)

                @block.vector
                def _(dve):
                    dve.wait_ge(b2_loaded, 16)

                    def outputs(k, r):
                        z = r % 2
                        e = of_tile(dve, k)
                        dve.wait_ge(m2_done, k + 1)
                        dve.wait_ge(stored[z], 16 * (k // 2) + 16)
                        nc.vector.tensor_tensor(y[:, z], ps[:, Y_BANK[z], 0:D], b2b[:, ds(e, 1), :].rearrange("p a d -> p (a d)"), op=ALU.add).then_inc(y_kept, 1)

                    def body(k, r):
                        z = r % 2
                        dve.wait_ge(m1_done, k + 1)
                        nc.vector.tensor_copy(hid[:, z], ps[:, H_BANK[z]]).then_inc(h_kept, 1)
                        if not (isinstance(k, int) and k == 0):
                            outputs(k - 1, r - 1)
                        e = of_tile(dve, k)
                        dve.wait_ge(ht_done, k + 1)
                        for j in range(HK, EK):
                            nc.vector.tensor_scalar(hT[:, z, j], ps[:, HT_BANK[1], (j - HK) * P:(j - HK + 1) * P], b1T[:, ds(EK * e + j, 1)], 0.0, ALU.add, ALU.max).then_inc(htb_kept, 1)
                    tiles(dve, body)
                    outputs(MT - 1, AHEAD - 1)

                @block.tensor
                def _(pe):
                    def turn_x(k, r):
                        z = r % 2
                        pe.wait_ge(x_loaded[r], 16 * (k // AHEAD) + 16)
                        for dk in range(DK):
                            last = nc.tensor.transpose(ps[:, XT_BANK[z], dk * P:(dk + 1) * P], xin[:, r, dk * P:(dk + 1) * P], ident[:])
                        last.then_inc(xt_done, 1)

                    def second(k, z):
                        e = of_tile(pe, k)
                        pe.wait_ge(y_kept, k + 1)
                        pe.wait_ge(hta_kept, HK * (k + 1))
                        pe.wait_ge(htb_kept, HK * (k + 1))
                        for j in range(EK):
                            last = nc.tensor.matmul(ps[:, Y_BANK[z], 0:D], hT[:, z, j], W2[:, ds(e, 1), j, :].rearrange("p a d -> p (a d)"), start=(j == 0), stop=(j == EK - 1))
                        last.then_inc(m2_done, 1)

                    def body(k, r):
                        z = r % 2
                        e = of_tile(pe, k)
                        pe.wait_ge(xt_kept, k + 1)
                        for dk in range(DK):
                            last = nc.tensor.matmul(ps[:, H_BANK[z]], xT[:, z, dk], W1[:, ds(e, 1), dk, :].rearrange("p a d -> p (a d)"), start=(dk == 0), stop=(dk == DK - 1))
                        last.then_inc(m1_done, 1)
                        if not (isinstance(k, int) and k == MT - 1):
                            turn_x(k + 1, (r + 1) % AHEAD)
                        if not (isinstance(k, int) and k == 0):
                            second(k - 1, 1 - z)
                        pe.wait_ge(h_kept, k + 1)
                        for j in range(EK):
                            last = nc.tensor.transpose(ps[:, HT_BANK[j // HK], (j % HK) * P:(j % HK + 1) * P], hid[:, z, j * P:(j + 1) * P], ident[:])
                        last.then_inc(ht_done, 1)
                    pe.sem_inc(y_kept, 2)
                    for w in w_loaded:
                        pe.wait_ge(w, 64)
                    turn_x(0, 0)
                    tiles(pe, body)
                    second(MT - 1, 1)

        with ExitStack() as s2:
            RING = 4
            got = sbuf(s2, "e_got", [P, RING, 2, D])
            place = sbuf(s2, "e_place", [P, 2, 2, RING], U32)
            place_ready, fetch_turn = sem("e_place_ready"), sem("e_fetch_turn")
            fetched = [sem(f"e_fetched{r}") for r in range(RING)]
            added, out_turn, out_stored = sem("e_added"), sem("out_turn"), sem("out_stored")
            with nc.Block() as block:
                @block.gpsimd
                def _(pool):
                    pool.sem_inc(added, 2 * RING)
                    with pool.Fori(0, NT // RING // 2) as i2:
                        for h in range(2):
                            i = 2 * i2 + h
                            pool.wait_ge(added, 2 * RING * i + 2)
                            nc.gpsimd.tensor_copy(place[:, h], slot[:, :, ds(RING * i, RING)]).then_inc(place_ready, 1)
                            pool.wait_ge(place_ready, i + 1)
                            for r in range(RING):
                                pool.wait_ge(added, 2 * (RING * i + r) + 2)
                                pool.sem_inc(fetch_turn, 1)
                                for s in range(2):
                                    nc.gpsimd.indirect_dma_start(got[:, r, s], None, ysort, bass.IndirectOffsetOnAxis(ap=place[:, h, s, r:r + 1], axis=0)).then_inc(fetched[r], 16)

                @block.vector
                def _(dve):
                    with dve.Fori(0, NT // RING) as i:
                        for r in range(RING):
                            t = RING * i + r
                            dve.wait_ge(fetched[r], 32 * i + 32)
                            row = X[:, ds(t, 1), :].rearrange("p a d -> p (a d)")
                            for s in range(2):
                                nc.vector.scalar_tensor_tensor(row, got[:, r, s], weight[:, s, ds(t, 1)], row, op0=ALU.mult, op1=ALU.add).then_inc(added, 1)
                                if s == 0:
                                    dve.wait_ge(added, 2 * t + 2 * RING + 1)

                @block.sync
                def _(sp):
                    with sp.Fori(0, NT // RING) as i:
                        sp.wait_ge(added, 2 * RING * (i + 2))
                        sp.sem_inc(out_turn, 1)
                        sp.dma_start(out_tiles[:, ds(RING * i, RING), :], X[:, ds(RING * i, RING), :]).then_inc(out_stored, 16)
                    sp.wait_ge(out_stored, 16 * (NT // RING))


def attention(nc, sem, stack, sbuf, ps, ident, identb, KQ, kq_loaded, load_qk, V, xsort, zero, x_zeroed):
    PR = sbuf(stack, "PR", [P, 2, HG, SEQ])
    VO = sbuf(stack, "VO", [P, KT, HG, 2 * HD])
    OT = sbuf(stack, "OT", [P, SEQ])
    mx = sbuf(stack, "mx", [P, QC, HG, QT])
    mm = sbuf(stack, "mm", [P, HG * QT])
    rest = sbuf(stack, "nm_rest", [P, HG * QT])
    nmp = sbuf(stack, "nmp", [P, PARTS, HG * QT], BF16)
    nrow = sbuf(stack, "nrow", [PARTS * HG * QT, P], BF16)
    rec = sbuf(stack, "rec", [P, 2, QT // 2, HG])
    SLOTS = 3
    MAX_BANK, ST_BANK, OT_BANK = 0, SLOTS, 2 * SLOTS

    ready, freed, vo_turn = sem("att_ready"), sem("kq_first"), sem("vo_turn")
    assert MT % UNITS == 0
    row_loaded = [sem(f"row_loaded{r}") for r in range(RING)]
    st_done, exp_done, pv_done = sem("st_done"), sem("exp_done"), sem("pv_done")
    max_done, red_done = sem("max_done"), sem("red_done")
    nm_steps, nm_tr, nm_kept = sem("nm_steps"), sem("nm_tr"), sem("nm_kept")
    vo_ready, ot_kept, ot_tr, att_steps = sem("vo_ready"), sem("ot_kept"), sem("ot_tr"), sem("att_steps")
    BLOCKS, MAXES, NM = KT * HG * QC, HG * QT * QC, 5
    order = [(h, q, k) for h in range(HG) for q in range(QT) for k in range(QC)]
    LOADS = 2 * len(PAIR_Q)
    EARLY = 12
    TURN = EARLY + 8
    LATE = 5
    events = ([("max", t) for t in range(LATE)] + [("nm", 0)] + [("max", t) for t in range(LATE, TURN)]
              + [("heads", 0), ("heads", 1)] + [("max", t) for t in range(TURN, MAXES)])
    place = {event: e for e, event in enumerate(events)}
    assert RING == SLOTS and BLOCKS % SLOTS == 1 and len(events) % SLOTS == 1
    bank = lambda r, event: MAX_BANK + (r + place[event]) % SLOTS
    st_bank = lambda r, s: ST_BANK + (r + s) % SLOTS

    def unit_loop(eng, unit):
        known = lambda u: lambda k: (u + k, (u + k) // RING, (u + k) % RING) if u + k < UNITS else None
        unit(known(0))
        with eng.Fori(0, (UNITS - 4) // RING) as i:
            for j in range(1, RING + 1):
                unit(lambda k, j=j: (RING * i + j + k, i + (j + k) // RING, (j + k) % RING))
        for u in range(UNITS - 3, UNITS):
            unit(known(u))
    assert (UNITS - 4) % RING == 0
    is0 = lambda u: isinstance(u, int) and u == 0

    with nc.Block() as block:
        @block.vector
        def _(dve):
            nc.vector.memset(KQ[KROWS:AROWS, :, 0].rearrange("p r h n -> p r (h n)"), 1.0).then_inc(ready, 1)
            nc.vector.memset(VO[:], 1.0).then_inc(ready, 1)

            def reduce(u, r, t):
                h, q, k = order[t]
                dve.wait_ge(max_done, MAXES * u + t + 1)
                nc.vector.reduce_max(mx[:, k, h, q:q + 1], ps[:, bank(r, ("max", t))], AX).then_inc(red_done, 1)

            def negate(u):
                dve.wait_ge(red_done, MAXES * u + MAXES)
                if not is0(u):
                    dve.wait_ge(nm_tr, u)
                m0, m1 = (mx[:, k].rearrange("p h q -> p (h q)") for k in range(QC))
                step = lambda ins: ins.then_inc(nm_steps, 1)
                step(nc.vector.tensor_tensor(mm[:], m0, m1, op=ALU.max))
                dve.wait_ge(nm_steps, NM * u + 1)
                step(nc.vector.tensor_scalar_mul(nmp[:, 0], mm[:], -1.0))
                dve.wait_ge(nm_steps, NM * u + 2)
                step(nc.vector.scalar_tensor_tensor(rest[:], mm[:], -1.0, nmp[:, 0], op0=ALU.mult, op1=ALU.subtract))
                dve.wait_ge(nm_steps, NM * u + 3)
                step(nc.vector.tensor_copy(nmp[:, 1], rest[:]))
                dve.wait_ge(nm_steps, NM * u + 4)
                step(nc.vector.tensor_tensor(nmp[:, 2], rest[:], nmp[:, 1], op=ALU.subtract))

            def heads_out(u, r):
                for k in range(2):
                    o = ps[:, bank(r, ("heads", k))].rearrange("p (q h c) -> p q h c", q=QT // 2, h=HG)
                    dve.wait_ge(ot_tr, 2 * u + k + 1)
                    nc.vector.reciprocal(rec[:, k], o[:, :, :, HD]).then_inc(att_steps, 1)
                    dve.wait_ge(att_steps, 4 * u + 2 * k + 1)
                    b, g = u // UPB, u % UPB
                    nc.vector.tensor_tensor(
                        V[:, ds(QT * b + QT // 2 * k, QT // 2), ds(HG * HD * g, HG * HD)].rearrange("p q (h c) -> p q h c", h=HG),
                        o[:, :, :, 0:HD], rec[:, k].unsqueeze(3).broadcast_to([P, QT // 2, HG, HD]), op=ALU.mult).then_inc(att_steps, 1)

            for t in range(MAXES):
                reduce(0, 0, t)
            negate(0)
            for t in range(EARLY):
                reduce(1, 1, t)

            def unit(at):
                (u, n, r), nxt, after = at(0), at(1), at(2)
                if nxt is not None:
                    for t in range(EARLY, TURN):
                        reduce(nxt[0], nxt[2], t)
                if not is0(u):
                    heads_out(u - 1, (r + 1) % RING)
                if nxt is not None:
                    for t in range(TURN, MAXES):
                        reduce(nxt[0], nxt[2], t)
                    negate(nxt[0])
                if after is not None:
                    for t in range(EARLY):
                        reduce(after[0], after[2], t)
            unit_loop(dve, unit)
            heads_out(UNITS - 1, (UNITS + 1) % RING)

        @block.scalar
        def _(act):
            def keep_rows(u, r):
                act.wait_ge(nm_tr, u + 1)
                if not is0(u):
                    act.wait_ge(freed, u)
                nc.scalar.copy(nrow[:], ps[0:PARTS * HG * QT, bank(r, ("nm", 0)), 0:P // 2].bitcast(BF16)).then_inc(nm_kept, 1)

            keep_rows(0, 1)

            def unit(at):
                (u, n, r), nxt = at(0), at(1)
                for s in range(BLOCKS):
                    kt, h, qc = s // (HG * QC), s // QC % HG, s % QC
                    act.wait_ge(st_done, BLOCKS * u + s + 1)
                    if h == 0 and qc == 0 and not (is0(u) and kt < 2):
                        act.wait_ge(pv_done, KT * u + kt - 1)
                    nc.scalar.activation(PR[:, kt % 2, h, qc * BANK:(qc + 1) * BANK], ps[:, st_bank(r, s)], ACT.Exp).then_inc(exp_done, 1)
                    if nxt is not None and s == (BLOCKS - 8 if at(2) is not None else BLOCKS - 1):
                        keep_rows(nxt[0], (nxt[2] + 1) % RING)
                act.wait_ge(pv_done, KT * u + KT)
                if not is0(u):
                    act.wait_ge(ot_tr, 2 * u)
                nc.scalar.copy(OT[:], ps[:, OT_BANK:OT_BANK + 2].rearrange("p a n -> p (a n)")).then_inc(ot_kept, 1)
            unit_loop(act, unit)

        @block.gpsimd
        def _(pool):
            pool.wait_ge(ready, 2)

            def unit(at):
                u = at(0)[0]
                if not is0(u):
                    pool.wait_ge(pv_done, KT * u)
                pool.sem_inc(vo_turn, 1)
                b, g = u // UPB, u % UPB
                share = MT // UNITS
                pool.dma_start(xsort.rearrange("(a p) d -> p a d", p=P)[:, ds(share * u, share), :], zero[:].unsqueeze(1).broadcast_to([P, share, D])).then_inc(x_zeroed, 16)
                nc.gpsimd.tensor_copy(VO[:, :, :, 0:HD], V[:, ds(KT * b, KT), ds(HG * HD * g, HG * HD)].rearrange("p k (h c) -> p k h c", h=HG)).then_inc(vo_ready, 1)
            unit_loop(pool, unit)

        @block.sync
        def _(sp):
            def rows(u, r):
                sp.wait_ge(nm_kept, u + 1)
                for a in range(PARTS):
                    n = HG * QT
                    sp.dma_start(KQ[KROWS + a:KROWS + a + 1, r, 1].rearrange("p h (q n) -> p (h q) n", n=P),
                                 nrow[a * n:(a + 1) * n, :]).then_inc(row_loaded[r], 16)

            rows(0, 0)

            def unit(at):
                (u, n, r), nxt, after = at(0), at(1), at(2)
                sp.wait_ge(row_loaded[r], 16 * PARTS * (n + 1))
                if after is not None and not is0(u):
                    sp.wait_ge(st_done, BLOCKS * u)
                sp.sem_inc(freed, 1)
                if after is not None:
                    load_qk(sp, after[0], after[2])
                if nxt is not None:
                    rows(nxt[0], nxt[2])
            unit_loop(sp, unit)

        @block.tensor
        def _(pe):
            def bank_read(u, e):
                while True:
                    u, e = (u, e - SLOTS) if e >= SLOTS else (u - 1, e - SLOTS + len(events))
                    if isinstance(u, int) and u < 0:
                        return
                    kind, t = events[e]
                    if isinstance(u, int) and (kind == "max" and u >= UNITS or kind == "nm" and u > UNITS):
                        continue
                    if kind == "max":
                        return pe.wait_ge(red_done, MAXES * u + t + 1)
                    if kind == "nm" and not is0(u):
                        return pe.wait_ge(nm_kept, u)
                    if kind == "heads" and (not isinstance(u, int) or u >= 2):
                        return pe.wait_ge(att_steps, 4 * (u - 2) + 2 * t + 2)

            def first_pass(u, n, r, t):
                h, q, k = order[t]
                if t == 0:
                    pe.wait_ge(kq_loaded[r], 16 * LOADS * (n + 1))
                bank_read(u, place["max", t])
                nc.tensor.matmul(ps[:, bank(r, ("max", t))], KQ[0:KROWS, r, 1, h, q * P:(q + 1) * P], KQ[0:KROWS, r, 0, h, k * BANK:(k + 1) * BANK],
                                 start=True, stop=True).then_inc(max_done, 1)

            def turn_max(u, r):
                pe.wait_ge(nm_steps, NM * u + NM)
                bank_read(u + 1, place["nm", 0])
                nc.tensor.transpose(ps[0:PARTS * HG * QT, bank(r, ("nm", 0)), 0:P // 2].bitcast(BF16), nmp[:].rearrange("p a n -> p (a n)"), identb[:]).then_inc(nm_tr, 1)

            def turn_heads(u, r, k):
                pe.wait_ge(ot_kept, u + 1)
                bank_read(u + 2, place["heads", k])
                for q in range(QT // 2):
                    last = nc.tensor.transpose(ps[:, bank(r, ("heads", k)), q * P:(q + 1) * P], OT[:, (k * QT // 2 + q) * P:(k * QT // 2 + q + 1) * P], ident[:])
                last.then_inc(ot_tr, 1)

            def weigh(u, kt, qc):
                if qc == 0:
                    pe.wait_ge(exp_done, BLOCKS * u + HG * QC * (kt + 1))
                if kt == 0 and qc == 0:
                    pe.wait_ge(vo_ready, u + 1)
                    if not is0(u):
                        pe.wait_ge(ot_kept, u)
                for h in range(HG):
                    last = nc.tensor.matmul(ps[2 * HD * h:2 * HD * (h + 1), OT_BANK + qc], VO[:, kt, h], PR[:, kt % 2, h, qc * BANK:(qc + 1) * BANK],
                                            start=(kt == 0), stop=(kt == KT - 1))
                if qc == QC - 1:
                    last.then_inc(pv_done, 1)

            pe.wait_ge(ready, 2)
            for t in range(MAXES):
                first_pass(0, 0, 0, t)
            for t in range(LATE):
                first_pass(1, 0, 1, t)
            turn_max(0, 1)
            for t in range(LATE, EARLY):
                first_pass(1, 0, 1, t)

            def unit(at):
                (u, n, r), nxt, after = at(0), at(1), at(2)
                beside = [(first_pass, (*nxt, t)) for t in range(EARLY, TURN)] if nxt is not None else []
                if not is0(u):
                    beside += [(turn_heads, (u - 1, (r + 1) % RING, k)) for k in range(2)]
                if nxt is not None:
                    beside += [(first_pass, (*nxt, t)) for t in range(TURN, MAXES)]
                if after is not None:
                    beside += [(first_pass, (*after, t)) for t in range(LATE)]
                if nxt is not None:
                    beside += [(turn_max, (nxt[0], (nxt[2] + 1) % RING))]
                if after is not None:
                    beside += [(first_pass, (*after, t)) for t in range(LATE, EARLY)]
                pe.wait_ge(row_loaded[r], 16 * PARTS * (n + 1))
                done = 0
                for s in range(BLOCKS):
                    kt, h, qc = s // (HG * QC), s // QC % HG, s % QC
                    if not (is0(u) and s < SLOTS):
                        pe.wait_ge(exp_done, BLOCKS * u + s - SLOTS + 1)
                    nc.tensor.matmul(ps[:, st_bank(r, s)], KQ[0:AROWS, r, 0, h, kt * P:(kt + 1) * P],
                                     KQ[0:AROWS, r, 1, h, qc * BANK:(qc + 1) * BANK], start=True, stop=True).then_inc(st_done, 1)
                    if kt > 0 and h in (1, 3) and qc == 1:
                        weigh(u, kt - 1, h // 2)
                    while done < (s + 1) * len(beside) // BLOCKS:
                        what, given = beside[done]
                        what(*given)
                        done += 1
                for qc in range(QC):
                    weigh(u, KT - 1, qc)
            unit_loop(pe, unit)
            for k in range(2):
                turn_heads(UNITS - 1, (UNITS + 1) % RING, k)


_INS = ['L0_attn_x', 'L0_attn_Wq', 'L0_attn_Wk', 'L0_attn_Wv', 'L0_attn_Wo', 'L0_attn_quadrant_weights',
        'L0_ffn_fast_b', 'L0_ffn_w_fc', 'L0_ffn_w_proj', 'L0_ffn_u', 'L0_ffn_v', 'L0_ffn_gate',
        'L1_attn_A', 'L1_attn_Bm', 'L1_attn_Cm', 'L1_attn_Dm', 'L1_attn_ln_w', 'L1_attn_ln_b', 'L1_attn_W_out', 'L1_attn_b_out',
        'L1_ffn_Wg', 'L1_ffn_bg', 'L1_ffn_bias', 'L1_ffn_W1', 'L1_ffn_b1', 'L1_ffn_W2', 'L1_ffn_b2']


def kernel(**inputs):
    import numpy as np
    import concourse.bacc as bacc
    from concourse.bass_utils import run_bass_kernel_spmd

    nc = bacc.Bacc("TRN2", target_bir_lowering=False, num_devices=1)
    nc.disable_value_cache = True
    arrays, args = {}, []
    for name in _INS:
        a = np.ascontiguousarray(inputs[name])
        if a.ndim == 0:
            a = a.reshape(1)
        arrays[f"in_{name}"] = a
        args.append(nc.dram_tensor(f"in_{name}", a.shape, mybir.dt.from_np(a.dtype), kind="ExternalInput").ap())
    out = nc.dram_tensor("out", (BATCH, SEQ, D), F32, kind="ExternalOutput").ap()
    transformer_kernel(nc, args, out)
    r = run_bass_kernel_spmd(nc, [arrays], core_ids=[0])
    return r.results[0]["out"]
```

```python
from contextlib import ExitStack

import concourse.bass as bass
from concourse import mybir

F32 = mybir.dt.float32
BF16 = mybir.dt.bfloat16
F32R = mybir.dt.float32r
I32 = mybir.dt.int32
U32 = mybir.dt.uint32
ALU = mybir.AluOpType
ACT = mybir.ActivationFunctionType
AX = mybir.AxisListType.X
ds = bass.ds

P = 128
BATCH, SEQ, D = 4, 1024, 256
T = BATCH * SEQ
NT = T // P
DK = D // P
CT = 4
CW = CT * P
NC = T // CW
BANK = 512
EPS = 1e-5

H, HD = 16, 16
HH = HD // 2
HG = 4
UNITS = BATCH * H // HG
UPB = H // HG
KT = SEQ // P
QT = SEQ // P
QC = SEQ // BANK
PARTS = 3
PAIR_Q = [0, 0, 1, 0, 2, 1]
PAIR_K = [0, 1, 0, 2, 0, 1]
KROWS = len(PAIR_Q) * HD
AROWS = KROWS + PARTS
RING = 3

E = 16
EH = 512
EK = EH // P
MT = (2 * T + E * (P - 1)) // P


class ChunkNorm:

    def __init__(self, nc, sem, sbuf, stack, name, src):
        self.nc, self.src = nc, src
        self.bn = sbuf(stack, name + "_bn", [P, 2, CT, 6])
        self.mv = sbuf(stack, name + "_mv", [P, 2, CT, 2])
        self.ve = sbuf(stack, name + "_ve", [P, 2, CT])
        self.power = sbuf(stack, name + "_power", [P, CT])
        self.rstd = sbuf(stack, name + "_rstd", [P, 2, CT])
        self.taken, self.known, self.set, self.eps, self.rooted, self.ready, self.turn = (
            sem(name + n) for n in ("_taken", "_known", "_set", "_eps", "_rooted", "_ready", "_turn"))

    def stats(self, dve, c, h):
        tile = lambda k: self.src[:, ds(CT * c + k, 1), :].rearrange("p a d -> p (a d)")
        for k in range(CT):
            self.nc.vector.bn_stats(self.bn[:, h, k], tile(k)).then_inc(self.taken, 1)
        dve.wait_ge(self.taken, CT * c + CT)
        if more_than(c, 2):
            dve.wait_ge(self.ready, c - 1)
        dve.sem_inc(self.turn, 1)
        for k in range(CT):
            self.nc.vector.bn_aggr(self.mv[:, h, k], self.bn[:, h, k]).then_inc(self.known, 1)

    def start(self, pool):
        self.nc.gpsimd.memset(self.power[:], -0.5).then_inc(self.set, 1)
        pool.wait_ge(self.set, 1)

    def root(self, pool, c, h):
        pool.wait_ge(self.known, CT * c + CT)
        pool.sem_inc(self.turn, 1)
        self.nc.gpsimd.tensor_scalar(self.ve[:, h], self.mv[:, h, :, 1], EPS, None, ALU.add).then_inc(self.eps, 1)
        pool.wait_ge(self.eps, c + 1)
        self.nc.gpsimd.tensor_tensor(self.rstd[:, h], self.ve[:, h], self.power[:], op=ALU.pow).then_inc(self.rooted, 1)

    def apply(self, dve, c, h, dst):
        dve.wait_ge(self.rooted, c + 1)
        for k in range(CT):
            t = ds(CT * c + k, 1)
            last = self.nc.vector.tensor_scalar(dst(k), self.src[:, t, :].rearrange("p a d -> p (a d)"),
                                                self.mv[:, h, k, 0:1], self.rstd[:, h, k:k + 1], ALU.subtract, ALU.mult)
        last.then_inc(self.ready, 1)


def chunks(eng, body, first=False):
    if first:
        body(0, 0)
        body(1, 1)
    with eng.Fori(1 if first else 0, NC // 2 - 1) as i:
        body(2 * i, 0)
        body(2 * i + 1, 1)
    body(NC - 2, 0)
    body(NC - 1, 1)


def split_products(a, b):
    return ((a[0], b[0]), (a[1], b[0]), (a[0], b[1]))


is_first = lambda c: isinstance(c, int) and c == 0
more_than = lambda c, k: not isinstance(c, int) or c >= k
more = lambda c, k: not isinstance(c, int) or c + k < NC


class Count:

    def __init__(self, sem):
        self.sem, self.n = sem, 0

    def mark(self, ins):
        ins.then_inc(self.sem, 1)
        self.n += 1

    def wait(self, eng):
        eng.wait_ge(self.sem, self.n)


def transformer_kernel(nc, ins, out):
    (x_in, wq_in, wk_in, wv_in, wo_in, quad_in, fastb_in, wfc_in, wproj_in, u_in, v_in, gate_in,
     a_in, bm_in, cm_in, dm_in, lnw_in, lnb_in, wout_in, bout_in,
     wg_in, bg_in, bias_in, w1_in, b1_in, w2_in, b2_in) = ins
    x_rows = x_in.rearrange("b s d -> (b s) d")
    out_rows = out.rearrange("b s d -> (b s) d")
    x_tiles = x_rows.rearrange("(t p) d -> p t d", p=P)
    out_tiles = out_rows.rearrange("(t p) d -> p t d", p=P)
    by_k = lambda w: w.rearrange("(k p) n -> p k n", p=P)

    outer = ExitStack()
    phase_sems = []

    def sem(name):
        phase_sems.append(nc.alloc_semaphore(name))
        return phase_sems[-1]

    def reuse_sems():
        with nc.Block() as block:
            @block.gpsimd
            def _(pool):
                nc.clear_and_free_semaphores(phase_sems)
        phase_sems.clear()

    def sbuf(stack, name, shape, dt=F32):
        return stack.enter_context(nc.sbuf_tensor(name, shape, dt))

    with outer:
        ps = outer.enter_context(nc.psum_tensor("ps", [P, 8, BANK], F32))
        X = sbuf(outer, "X", [P, NT, D])
        ident = sbuf(outer, "ident", [P, P])
        identb = sbuf(outer, "identb", [P, P], BF16)
        pqk = nc.dram_tensor("qk_parts", [2, PARTS, DK, P, T], BF16, kind="Internal").ap()

        early = outer.enter_context(ExitStack())
        ssi = StateSpaceInputs(sbuf, early, a_in, bm_in, cm_in, dm_in)
        mid = ExitStack()
        with mid:
            ffw = FeedForwardWeights(sbuf, mid)
            with ExitStack() as st:
                V = sbuf(st, "V", [P, NT, D])
                KQ = [sbuf(st, f"KQ{r}", [P, 2, HG, SEQ], BF16) for r in range(2)]
                kq_loaded = [sem(f"kq_loaded{r}") for r in range(RING)]

                def load_qk(sp, u, r):
                    b, g = u // UPB, u % UPB
                    for side, pairs in ((1, PAIR_Q), (0, PAIR_K)):
                        for j, part in enumerate(pairs):
                            src = pqk.rearrange("s a k p t -> s a (k p) t").rearrange("s a (g h c) t -> s a g c h t", h=HG, c=HD)
                            sp.dma_start(KQ[r][j * HD:(j + 1) * HD, side],
                                         src[1 - side, part, ds(g, 1), :, :, ds(SEQ * b, SEQ)].rearrange("g c h t -> (g c) h t")).then_inc(kq_loaded[r], 16)

                with ExitStack() as s1:
                    W = sbuf(s1, "w_raw", [P, 3, DK, D])
                    Wq, Wk, Wv = range(3)
                    wsplit = [sbuf(s1, f"w_part{a}", [P, 3, DK, D], F32R) for a in range(2)]
                    wk = sbuf(s1, "wk", [P, DK, H, 2, HH])
                    wkt = sbuf(s1, "wkt", [P, DK, H, 2, HH])
                    quad = sbuf(s1, "quad", [P, 4])
                    qs = sbuf(s1, "qs", [P, 8])
                    xn = sbuf(s1, "xn", [P, 2, CT, D])
                    xT = [sbuf(s1, f"xT{a}", [P, 2, DK, CW], F32R) for a in range(2)]
                    parts = sbuf(s1, "parts", [P, 2, 2, PARTS, DK, CW], BF16)
                    part = lambda h, m, a: parts[:, h, m // DK, a, m % DK]
                    rest = sbuf(s1, "rest", [P, 2 * DK, CW])
                    norm = ChunkNorm(nc, sem, sbuf, s1, "ln1", X)
                    x_loaded = [sem(f"x_loaded{h}") for h in range(2)]
                    w_loaded = [sem(f"w{n}_loaded") for n in "qkv"]
                    quad_loaded, quad_steps, quad_max, quad_exp, k_mixed, w_hi, w_lo, idz, id_ready = (
                        sem(n) for n in ("quad_loaded", "quad_steps", "quad_max", "quad_exp", "k_mixed", "w_hi", "w_lo", "idz", "id_ready"))
                    xn_tr, xh_ready, xl_ready = sem("xn_tr"), sem("xh_ready"), sem("xl_ready")
                    qk_done, hi_ready, rest_ready, mid_ready, lo_ready = (sem(n) for n in ("qk_done", "hi_ready", "rest_ready", "mid_ready", "lo_ready"))
                    v_done, v_kept, parts_turn = sem("v_done"), sem("v_kept"), sem("parts_turn")
                    ones_set = sem("ones_set")
                    stored = [sem(f"parts_stored{h}") for h in range(2)]
                    with nc.Block() as block:
                        @block.sync
                        def _(sp):
                            for c in range(NC):
                                if c >= 2:
                                    sp.wait_ge(x_loaded[c % 2], 16 * (c // 2))
                                sp.dma_start(X[:, CT * c:CT * c + CT, :], x_tiles[:, CT * c:CT * c + CT, :]).then_inc(x_loaded[c % 2], 16)
                            for h in range(2):
                                sp.sem_inc(stored[h], 16)

                            def body(c, h):
                                if isinstance(c, int) and c == NC - 2:
                                    for h2 in range(2):
                                        sp.wait_ge(stored[h2], 16 * (NC // 2))
                                    for u in range(2):
                                        load_qk(sp, u, u)
                                sp.wait_ge(lo_ready, 2 * DK * (c + 2))
                                sp.sem_inc(parts_turn, 1)
                                sp.dma_start(pqk[:, :, :, :, ds(CW * c, CW)].rearrange("s a k p n -> p (s a k) n"),
                                             parts[:, h].rearrange("p s a k n -> p (s a k) n")).then_inc(stored[h], 16)
                            chunks(sp, body)
                            for h in range(2):
                                sp.wait_ge(stored[h], 16 * (NC // 2 + 1))

                        @block.gpsimd
                        def _(pool):
                            nc.gpsimd.memset(ident[:], 0.0).then_inc(idz, 1)
                            nc.gpsimd.memset(identb[:], 0.0).then_inc(idz, 1)
                            pool.wait_ge(idz, 2)
                            for m in (ident, identb):
                                nc.gpsimd.affine_select(out=m[:], in_=m[:], compare_op=ALU.not_equal, fill=1.0, base=0,
                                                        pattern=[[-1, P]], channel_multiplier=1).then_inc(id_ready, 1)
                            norm.start(pool)
                            for c in range(2):
                                norm.root(pool, c, c)
                            pool.wait_ge(norm.rooted, 2)
                            for r in range(2):
                                nc.gpsimd.memset(KQ[r][KROWS:AROWS, 0].rearrange("p h n -> p (h n)"), 1.0).then_inc(ones_set, 1)
                                pool.wait_ge(ones_set, r + 1)
                            pool.sem_inc(lo_ready, 2 * DK)

                            def body(c, h):
                                if more(c, 2):
                                    norm.root(pool, c + 2, h)
                                for m in range(2 * DK):
                                    pool.wait_ge(mid_ready, 2 * DK * c + m + 1)
                                    nc.gpsimd.tensor_tensor(part(h, m, 2), rest[:, m], part(h, m, 1), op=ALU.subtract).then_inc(lo_ready, 1)
                            chunks(pool, body)

                        @block.vector
                        def _(dve):
                            def stats(c, h):
                                dve.wait_ge(x_loaded[h], 16 * (c // 2) + 16)
                                norm.stats(dve, c, h)
                            stats(0, 0)
                            dve.wait_ge(quad_loaded, 16)
                            steps = Count(quad_steps)
                            steps.mark(nc.vector.reduce_max(qs[:, 0:1], quad[:], AX))
                            steps.wait(dve)
                            nc.vector.tensor_scalar_mul(qs[:, 1:2], qs[:, 0:1], -1.0).then_inc(quad_max, 1)
                            dve.wait_ge(quad_exp, 1)
                            steps.mark(nc.vector.reduce_sum(qs[:, 2:3], qs[:, 4:8], AX))
                            steps.wait(dve)
                            steps.mark(nc.vector.reciprocal(qs[:, 3:4], qs[:, 2:3]))
                            steps.wait(dve)
                            steps.mark(nc.vector.tensor_scalar(quad[:], qs[:, 4:8], qs[:, 3:4], float(HH) ** -0.5, ALU.mult, ALU.mult))
                            steps.wait(dve)
                            dve.wait_ge(w_loaded[Wk], 16)
                            half = W[:, Wk].rearrange("p k (h a c) -> p k h a c", h=H, a=2)
                            for a in range(2):
                                for k in range(DK):
                                    steps.mark(nc.vector.tensor_scalar(wkt[:, k, :, a, :], wk[:, k, :, 1, :], quad[:, 2 * a + 1:2 * a + 2], None, ALU.mult))
                            steps.wait(dve)
                            for a in range(2):
                                for k in range(DK):
                                    nc.vector.scalar_tensor_tensor(half[:, k, :, a, :], wk[:, k, :, 0, :], quad[:, 2 * a:2 * a + 1],
                                                                   wkt[:, k, :, a, :], op0=ALU.mult, op1=ALU.add).then_inc(k_mixed, 1)
                            stats(1, 1)
                            norm.apply(dve, 0, 0, lambda k: xn[:, 0, k])
                            dve.wait_ge(k_mixed, 2 * DK)

                            def low_weights(n, dst):
                                dve.wait_ge(w_hi, n + 1)
                                nc.vector.tensor_tensor(dst[1], W[:, n], dst[0].bitcast(F32), op=ALU.subtract).then_inc(w_lo, 1)
                            for n in (Wq, Wk, Wv):
                                low_weights(n, [w[:, n] for w in wsplit])

                            def low(c, h):
                                dve.wait_ge(xh_ready, c + 1)
                                nc.vector.tensor_tensor(xT[1][:, h].rearrange("p k n -> p (k n)"), ps[:, 0:2].rearrange("p a n -> p (a n)"),
                                                        xT[0][:, h].rearrange("p k n -> p (k n)").bitcast(F32), op=ALU.subtract).then_inc(xl_ready, 1)
                            low(0, 0)

                            def body(c, h):
                                if more(c, 1):
                                    norm.apply(dve, c + 1, 1 - h, lambda k: xn[:, 1 - h, k])
                                if more(c, 2):
                                    stats(c + 2, h)
                                for m in range(2 * DK):
                                    dve.wait_ge(hi_ready, 2 * DK * c + m + 1)
                                    dve.wait_ge(lo_ready, 2 * DK * c + m + 1)
                                    nc.vector.tensor_tensor(rest[:, m], ps[:, 2 + m], part(h, m, 0), op=ALU.subtract).then_inc(rest_ready, 1)
                                if more(c, 1):
                                    low(c + 1, 1 - h)
                            chunks(dve, body)

                        @block.scalar
                        def _(act):
                            act.dma_start(quad[:], quad_in.partition_broadcast(P)).then_inc(quad_loaded, 16)
                            act.dma_start(wk[:].rearrange("p k h a c -> p k (h a c)"), by_k(wk_in)).then_inc(w_loaded[Wk], 16)
                            for n, w in ((Wq, wq_in), (Wv, wv_in)):
                                act.dma_start(W[:, n], by_k(w)).then_inc(w_loaded[n], 16)
                            act.wait_ge(quad_max, 1)
                            nc.scalar.activation(qs[:, 4:8], quad[:], ACT.Exp, bias=qs[:, 1:2]).then_inc(quad_exp, 1)

                            def high(c, h):
                                act.wait_ge(xn_tr, c + 1)
                                nc.scalar.copy(xT[0][:, h].rearrange("p k n -> p (k n)"), ps[:, 0:2].rearrange("p a n -> p (a n)")).then_inc(xh_ready, 1)
                            for n in (Wq, Wk, Wv):
                                act.wait_ge(w_loaded[n], 16)
                                if n == Wk:
                                    act.wait_ge(k_mixed, 2 * DK)
                                nc.scalar.copy(wsplit[0][:, n], W[:, n]).then_inc(w_hi, 1)
                            high(0, 0)

                            def body(c, h):
                                act.wait_ge(stored[h], 16 * (c // 2) + 16)
                                for m in range(2 * DK):
                                    act.wait_ge(qk_done, 2 * DK * c + m + 1)
                                    nc.scalar.copy(part(h, m, 0), ps[:, 2 + m]).then_inc(hi_ready, 1)
                                if more(c, 1):
                                    high(c + 1, 1 - h)
                                for m in range(2 * DK):
                                    act.wait_ge(rest_ready, 2 * DK * c + m + 1)
                                    nc.scalar.copy(part(h, m, 1), rest[:, m]).then_inc(mid_ready, 1)
                                act.wait_ge(v_done, c + 1)
                                nc.scalar.copy(V[:, ds(CT * c, CT), :].rearrange("p t n -> p (t n)"), ps[:, 6:8].rearrange("p a n -> p (a n)")).then_inc(v_kept, 1)
                            chunks(act, body)

                        @block.tensor
                        def _(pe):
                            pe.sem_inc(v_kept, 1)
                            pe.wait_ge(id_ready, 2)

                            def turn(c, h):
                                pe.wait_ge(norm.ready, c + 1)
                                for dk in range(DK):
                                    for k in range(CT):
                                        last = nc.tensor.transpose(ps[:, dk, k * P:(k + 1) * P], xn[:, h, k, dk * P:(dk + 1) * P], ident[:])
                                last.then_inc(xn_tr, 1)
                            turn(0, 0)
                            pe.wait_ge(w_lo, 3)

                            def body(c, h):
                                pe.wait_ge(xl_ready, c + 1)
                                for m in range(2 * DK):
                                    pe.wait_ge(lo_ready, 2 * DK * c + m + 1)
                                    n, cols = m // DK, slice(m % DK * P, (m % DK + 1) * P)
                                    todo = [p for dk in range(DK) for p in split_products([w[:, n, dk, cols] for w in wsplit], [x[:, h, dk] for x in xT])]
                                    for j, (w, x) in enumerate(todo):
                                        last = nc.tensor.matmul(ps[:, 2 + m], w, x, start=(j == 0), stop=(j == len(todo) - 1))
                                    last.then_inc(qk_done, 1)
                                if more(c, 1):
                                    turn(c + 1, 1 - h)
                                pe.wait_ge(v_kept, c + 1)
                                for k in range(CT):
                                    todo = [p for dk in range(DK) for p in split_products([x[:, h, dk, k * P:(k + 1) * P] for x in xT], [w[:, Wv, dk] for w in wsplit])]
                                    for j, (x, w) in enumerate(todo):
                                        last = nc.tensor.matmul(ps[:, 6 + k // 2, (k % 2) * D:(k % 2 + 1) * D], x, w,
                                                                start=(j == 0 and k % 2 == 0), stop=(j == len(todo) - 1), skip_group_check=True)
                                last.then_inc(v_done, 1)
                            chunks(pe, body)

                ffw.load_buffers(sbuf, st, sem)
                ffw.inputs = fastb_in, by_k(wfc_in), by_k(wproj_in), by_k(u_in), v_in, gate_in, by_k(wo_in)
                with ExitStack() as s2:
                    attention(nc, sem, s2, sbuf, ps, ident, identb, KQ, kq_loaded, load_qk, V, ffw)

                output_projection(nc, sem, sbuf, ps, X, V, ident, ffw)

            reuse_sems()
            ssi.semaphores(sem)
            feed_forward(nc, sem, sbuf, ps, X, ident, ffw, ssi)
        ssm(nc, sem, sbuf, ps, X, ident, ssi, bm_in, cm_in, lnw_in, lnb_in, wout_in, bout_in, by_k)
        early.close()
        reuse_sems()
        moe(nc, sem, sbuf, ps, X, ident, out_tiles, wg_in, bg_in, bias_in, w1_in, b1_in, w2_in, b2_in)


FH = 1024
FK = FH // P
RANK = 16


class FeedForwardWeights:

    def __init__(self, sbuf, stack):
        self.wfT = [sbuf(stack, f"wfT{a}", [P, DK, FH], F32R) for a in range(2)]
        self.wpT = sbuf(stack, "wpT", [P, FK, D], F32R)
        self.pscale = sbuf(stack, "pscale", [P, D])

    def load_buffers(self, sbuf, stack, sem):
        self.wf = sbuf(stack, "wf", [P, FK, D])
        self.wp = sbuf(stack, "wp", [P, DK, FH])
        self.wo = sbuf(stack, "wo", [P, DK, D])
        self.u = sbuf(stack, "u", [P, FK, RANK])
        self.fb = sbuf(stack, "fb", [RANK, RANK])
        self.v = sbuf(stack, "v", [RANK, D])
        self.gate = sbuf(stack, "gate", [P, 1])
        self.NR = FK + DK
        self.sc = sbuf(stack, "sc", [P, 4, self.NR])
        self.rows = [self.wf[:, k] for k in range(FK)] + [self.wp[:, k] for k in range(DK)]
        self.f_loaded, self.p_loaded, self.small_loaded, self.mags, self.steps = (
            sem(n) for n in ("wf_loaded", "wp_loaded", "lowrank_loaded", "ffn_mags", "ffn_steps"))

    def load(self, sp):
        fb, wf, wp, u, v, gate, wo = self.inputs
        sp.dma_start(self.wf[:], wf).then_inc(self.f_loaded, 16)
        sp.dma_start(self.wp[:], wp).then_inc(self.p_loaded, 16)
        for dst, src in ((self.u, u), (self.fb, fb), (self.v, v), (self.gate, gate.partition_broadcast(P)), (self.wo, wo)):
            sp.dma_start(dst[:], src).then_inc(self.small_loaded, 16)

    def magnitudes(self, nc, act, scratch):
        act.wait_ge(self.f_loaded, 16)
        act.wait_ge(self.p_loaded, 16)
        for r, w in enumerate(self.rows):
            if r > 0:
                act.wait_ge(self.mags, r)
            nc.scalar.activation(scratch[:, 0:w.shape[-1]], w, ACT.Abs, accum_out=self.sc[:, 0, r:r + 1]).then_inc(self.mags, 1)

    def quantise(self, nc, pool, above):
        sc, steps = self.sc, Count(self.steps)

        def step(ins):
            steps.mark(ins)
            steps.wait(pool)
        pool.wait_ge(self.mags, self.NR)
        for a, b, n in ((0, FK, D), (FK, self.NR, FH)):
            step(nc.gpsimd.tensor_scalar(sc[:, 1, a:b], sc[:, 0, a:b], 1.0 / n, 1e-5, ALU.mult, ALU.max))
        for k, f in ((2, 0.5), (3, -0.5)):
            step(nc.gpsimd.tensor_scalar(sc[:, k], sc[:, 1], f, None, ALU.mult))
        for r, w in enumerate(self.rows):
            up = above[:, 0:w.shape[-1]]
            times = (sc[:, 1, r:r + 1], ALU.mult) if r < FK else (None,)
            step(nc.gpsimd.tensor_scalar(up, w, sc[:, 2, r:r + 1], times[0], ALU.is_gt, *times[1:]))
            step(nc.gpsimd.tensor_scalar(w, w, sc[:, 3, r:r + 1], times[0], ALU.is_lt, *times[1:]))
            step(nc.gpsimd.tensor_tensor(w, up, w, op=ALU.subtract))


def output_projection(nc, sem, sbuf, ps, X, ATT, ident, ffw):
    wfT, wpT, pscale, wf, wp, u, fb, v, gate, sc = ffw.wfT, ffw.wpT, ffw.pscale, ffw.wf, ffw.wp, ffw.u, ffw.fb, ffw.v, ffw.gate, ffw.sc
    with ExitStack() as s0:
        wo = [sbuf(s0, f"wo{a}", [P, DK, D], F32R) for a in range(2)]
        stage = sbuf(s0, "stage", [P, 2, CT, D])
        aT = [sbuf(s0, f"aT{a}", [P, 2, DK, CW], F32R) for a in range(2)]
        staged, at_tr, ah_ready, al_ready, o_done, o_added = (sem("a_" + n) for n in ("staged", "tr", "hi", "lo", "done", "added"))
        wo_hi, wo_lo = sem("a_wo_hi"), sem("a_wo_lo")
        uT = sbuf(s0, "uT", [RANK, FH])
        fbT = sbuf(s0, "fbT", [RANK, RANK])
        fv = sbuf(s0, "fv", [RANK, D])
        spread = sbuf(s0, "spread", [P, DK, P])
        f_rows, f_tr, f_lr, f_kept, t_done, t_hi, t_lo, s_spread = (
            sem(n) for n in ("ffn_rows", "lowrank_tr", "lowrank_done", "lowrank_kept", "ffn_w_tr", "ffn_w_hi", "ffn_w_lo", "ffn_spread"))
        two = lambda bank: ps[:, bank:bank + 2].rearrange("p a n -> p (a n)")
        flat = lambda v: v.rearrange("p k n -> p (k n)")
        LR = (6, 7, 4, 5)

        with nc.Block() as block:
            @block.gpsimd
            def _(pool):
                with pool.Fori(0, NC // 2) as i:
                    for h in range(2):
                        c = 2 * i + h
                        pool.wait_ge(at_tr, c + 1)
                        nc.gpsimd.tensor_copy(flat(stage[:, h]), flat(ATT[:, ds(CT * c, CT), :])).then_inc(staged, 1)

            @block.scalar
            def _(act):
                nc.scalar.copy(wo[0][:], ffw.wo[:]).then_inc(wo_hi, 1)
                act.wait_ge(f_tr, 1)
                nc.scalar.copy(uT[:], two(6)[0:RANK]).then_inc(f_kept, 1)
                nc.scalar.copy(fbT[:], ps[0:RANK, 2, 0:RANK]).then_inc(f_kept, 1)
                act.wait_ge(f_lr, 1)
                nc.scalar.copy(fv[:], ps[0:RANK, 3, 0:D]).then_inc(f_kept, 1)

                def body(c, h):
                    act.wait_ge(at_tr, c + 3)
                    nc.scalar.copy(flat(aT[0][:, h]), two(0)).then_inc(ah_ready, 1)
                chunks(act, body)
                for half, bank in enumerate((6, 2)):
                    act.wait_ge(t_done, half + 1)
                    nc.scalar.copy(flat(wpT[:])[:, half * FH:(half + 1) * FH], two(bank)).then_inc(t_hi, 1)
                for half, bank in enumerate((0, 4)):
                    act.wait_ge(t_done, half + 3)
                    nc.scalar.copy(wfT[0][:, half], two(bank)).then_inc(t_hi, 1)
                act.wait_ge(t_done, 5)
                nc.scalar.copy(pscale[:], ps[:, 6, 0:D]).then_inc(t_hi, 1)

            @block.vector
            def _(dve):
                dve.sem_inc(o_added, 2)
                dve.wait_ge(wo_hi, 1)
                nc.vector.tensor_tensor(wo[1][:], ffw.wo[:], wo[0][:].bitcast(F32), op=ALU.subtract).then_inc(wo_lo, 1)
                for k in range(DK):
                    nc.vector.tensor_scalar(spread[:, k], ident[:], 0.0, sc[:, 1, FK + k:FK + k + 1], ALU.mult, ALU.add).then_inc(s_spread, 1)
                dve.wait_ge(f_lr, 2)
                for k in range(FK):
                    nc.vector.scalar_tensor_tensor(wf[:, k], ps[:, LR[k // 2], (k % 2) * D:(k % 2 + 1) * D], gate[:], wf[:, k],
                                                   op0=ALU.mult, op1=ALU.add).then_inc(f_rows, 1)

                def low(c, h):
                    dve.wait_ge(ah_ready, c + 1)
                    nc.vector.tensor_tensor(flat(aT[1][:, h]), two(0), flat(aT[0][:, h]).bitcast(F32), op=ALU.subtract).then_inc(al_ready, 1)
                low(0, 0)

                def body(c, h):
                    if more(c, 1):
                        low(c + 1, 1 - h)
                    dve.wait_ge(o_done, c + 1)
                    chunk = flat(X[:, ds(CT * c, CT), :])
                    nc.vector.tensor_tensor(chunk, two(2 + 2 * h), chunk, op=ALU.add).then_inc(o_added, 1)
                chunks(dve, body)
                for half, bank in enumerate((0, 4)):
                    dve.wait_ge(t_hi, half + 3)
                    nc.vector.tensor_tensor(wfT[1][:, half], two(bank), wfT[0][:, half].bitcast(F32), op=ALU.subtract).then_inc(t_lo, 1)

            @block.tensor
            def _(pe):
                pe.sem_inc(at_tr, 2)

                def turn(c, h):
                    pe.wait_ge(staged, c + 1)
                    for dk in range(DK):
                        for k in range(CT):
                            last = nc.tensor.transpose(ps[:, dk, k * P:(k + 1) * P], stage[:, h, k, dk * P:(dk + 1) * P], ident[:])
                    last.then_inc(at_tr, 1)
                for k in range(FK):
                    nc.tensor.transpose(ps[0:RANK, 6 + k // 4, (k % 4) * P:(k % 4 + 1) * P], u[:, k], ident[:])
                nc.tensor.transpose(ps[0:RANK, 2, 0:RANK], fb[:], ident[0:RANK, 0:RANK]).then_inc(f_tr, 1)
                pe.wait_ge(f_kept, 2)
                nc.tensor.matmul(ps[0:RANK, 3, 0:D], fbT[:], v[:], start=True, stop=True).then_inc(f_lr, 1)
                turn(0, 0)
                pe.wait_ge(f_kept, 3)
                for k in range(FK):
                    last = nc.tensor.matmul(ps[:, LR[k // 2], (k % 2) * D:(k % 2 + 1) * D], uT[:, k * P:(k + 1) * P], fv[:],
                                            start=(k % 2 == 0), stop=True, skip_group_check=True)
                last.then_inc(f_lr, 1)
                pe.wait_ge(wo_lo, 1)

                def body(c, h):
                    pe.wait_ge(al_ready, c + 1)
                    if is_first(c):
                        pe.wait_ge(f_rows, FK)
                    if more(c, 1):
                        turn(c + 1, 1 - h)
                    pe.wait_ge(o_added, c + 1)
                    for k in range(CT):
                        todo = [p for dk in range(DK) for p in split_products([x[:, h, dk, k * P:(k + 1) * P] for x in aT], [w[:, dk] for w in wo])]
                        for j, (x, w) in enumerate(todo):
                            last = nc.tensor.matmul(ps[:, 2 + 2 * h + k // 2, (k % 2) * D:(k % 2 + 1) * D], x, w,
                                                    start=(j == 0 and k % 2 == 0), stop=(j == len(todo) - 1), skip_group_check=True)
                    last.then_inc(o_done, 1)
                chunks(pe, body)
                for half, bank in enumerate((6, 2)):
                    if bank == 2:
                        pe.wait_ge(o_added, NC + 1)
                    for k in range(FK):
                        kk, o = divmod(k + half * FK, DK)
                        last = nc.tensor.transpose(ps[:, bank + k // 4, (k % 4) * P:(k % 4 + 1) * P], wp[:, o, kk * P:(kk + 1) * P], ident[:])
                    last.then_inc(t_done, 1)
                for half, bank in enumerate((0, 4)):
                    if bank == 4:
                        pe.wait_ge(o_added, NC + 2)
                    for k in range(FK):
                        last = nc.tensor.transpose(ps[:, bank + k // 4, (k % 4) * P:(k % 4 + 1) * P], wf[:, k, half * P:(half + 1) * P], ident[:])
                    last.then_inc(t_done, 1)
                pe.wait_ge(s_spread, DK)
                pe.wait_ge(t_hi, 1)
                for k in range(DK):
                    last = nc.tensor.matmul(ps[:, 6, k * P:(k + 1) * P], spread[:, k], ident[:], start=True, stop=True, skip_group_check=True)
                last.then_inc(t_done, 1)


def feed_forward(nc, sem, sbuf, ps, X, ident, ffw, ssi):
    wfT, wpT, pscale = ffw.wfT, ffw.wpT, ffw.pscale
    with ExitStack() as s1:
        xn = sbuf(s1, "f_xn", [P, 2, CT, D])
        xT = [sbuf(s1, f"f_xT{a}", [P, 2, DK, CW], F32R) for a in range(2)]
        relu = sbuf(s1, "relu", [P, 2, CW])
        square = sbuf(s1, "square", [P, 2, CW])
        sq = [sbuf(s1, f"sq{a}", [P, 2, FK, CW], F32R) for a in range(2)]
        scaled = sbuf(s1, "scaled", [P, CT, D])
        norm = ChunkNorm(nc, sem, sbuf, s1, "ln2", X)
        n_tr, xh_ready, xl_ready, h_done, relu_ready, s_ready, hi_ready, lo_ready, o_done, o_scaled, o_added = (
            sem("f_" + n) for n in ("n_tr", "xh_ready", "xl_ready", "h_done", "relu_ready", "s_ready", "hi_ready", "lo_ready", "o_done", "o_scaled", "o_added"))
        HB = 4
        flat = lambda v: v.rearrange("p k n -> p (k n)")
        two = lambda bank: ps[:, bank:bank + 2].rearrange("p a n -> p (a n)")
        with nc.Block() as block:
            @block.sync
            def _(sp):
                ssi.load(sp)

            @block.gpsimd
            def _(pool):
                norm.start(pool)
                for c in range(2):
                    norm.root(pool, c, c)
                pool.sem_inc(o_added, 1)

                def add(c):
                    pool.wait_ge(o_scaled, c + 2)
                    chunk = flat(X[:, ds(CT * c, CT), :])
                    nc.gpsimd.tensor_tensor(chunk, flat(scaled[:]), chunk, op=ALU.add).then_inc(o_added, 1)

                def body(c, h):
                    if not (isinstance(c, int) and c < 2):
                        add(c - 2)
                    if more(c, 2):
                        norm.root(pool, c + 2, h)
                chunks(pool, body, first=True)
                add(NC - 2)
                add(NC - 1)

            @block.vector
            def _(dve):
                norm.stats(dve, 0, 0)
                norm.stats(dve, 1, 1)
                norm.apply(dve, 0, 0, lambda k: xn[:, 0, k])

                def low(c, h):
                    dve.wait_ge(xh_ready, c + 1)
                    nc.vector.tensor_tensor(flat(xT[1][:, h]), two(0), flat(xT[0][:, h]).bitcast(F32), op=ALU.subtract).then_inc(xl_ready, 1)
                low(0, 0)
                dve.sem_inc(o_scaled, 1)
                dve.sem_inc(lo_ready, 2)

                def sq_full(c, m):
                    dve.wait_ge(relu_ready, FK * c + m + HB + 1)
                    dve.wait_ge(lo_ready, FK * c + m + 1)
                    nc.vector.tensor_tensor(square[:, m % 2], relu[:, m % 2], relu[:, m % 2], op=ALU.mult).then_inc(s_ready, 1)

                def sq_low(c, h, m):
                    dve.wait_ge(hi_ready, FK * c + m + 1)
                    nc.vector.tensor_tensor(sq[1][:, h, m], square[:, m % 2], sq[0][:, h, m].bitcast(F32), op=ALU.subtract).then_inc(lo_ready, 1)

                def scale(c):
                    dve.wait_ge(o_done, c + 1)
                    dve.wait_ge(o_added, c + 1)
                    nc.vector.tensor_tensor(scaled[:], two(6).rearrange("p (k d) -> p k d", d=D),
                                            pscale[:].unsqueeze(1).broadcast_to([P, CT, D]), op=ALU.mult).then_inc(o_scaled, 1)

                def body(c, h):
                    for m in range(FK):
                        sq_full(c, m)
                        if m > 0:
                            sq_low(c, h, m - 1)
                        if m == 1 and more(c, 1):
                            norm.apply(dve, c + 1, 1 - h, lambda k: xn[:, 1 - h, k])
                        if m == 3 and not (isinstance(c, int) and c < 2):
                            scale(c - 2)
                        if m == 5 and more(c, 2):
                            norm.stats(dve, c + 2, h)
                    if more(c, 1):
                        low(c + 1, 1 - h)
                    sq_low(c, h, FK - 1)
                chunks(dve, body, first=True)
                scale(NC - 2)
                scale(NC - 1)

            @block.scalar
            def _(act):
                def high(c, h):
                    act.wait_ge(n_tr, c + 1)
                    nc.scalar.copy(flat(xT[0][:, h]), two(0)).then_inc(xh_ready, 1)
                high(0, 0)
                act.sem_inc(s_ready, 2)

                def sq_high(c, h, m):
                    act.wait_ge(s_ready, FK * c + m + 3)
                    nc.scalar.copy(sq[0][:, h, m], square[:, m % 2]).then_inc(hi_ready, 1)

                def body(c, h):
                    for m in range(FK):
                        act.wait_ge(h_done, FK * c + m + 1)
                        act.wait_ge(s_ready, FK * c + m + 1)
                        nc.scalar.activation(relu[:, m % 2], ps[:, 2 + m % HB], ACT.Relu).then_inc(relu_ready, 1)
                        if m > 0:
                            sq_high(c, h, m - 1)
                        if m == FK - 2 and more(c, 1):
                            high(c + 1, 1 - h)
                    sq_high(c, h, FK - 1)
                chunks(act, body)

            @block.tensor
            def _(pe):
                def turn(c, h):
                    pe.wait_ge(norm.ready, c + 1)
                    for dk in range(DK):
                        for k in range(CT):
                            last = nc.tensor.transpose(ps[:, dk, k * P:(k + 1) * P], xn[:, h, k, dk * P:(dk + 1) * P], ident[:])
                    last.then_inc(n_tr, 1)
                turn(0, 0)
                pe.sem_inc(relu_ready, HB)

                def body(c, h):
                    pe.wait_ge(xl_ready, c + 1)
                    for m in range(FK):
                        pe.wait_ge(relu_ready, FK * c + m + 1)
                        todo = [p for dk in range(DK) for p in split_products([w[:, dk, m * P:(m + 1) * P] for w in wfT], [x[:, h, dk] for x in xT])]
                        for j, (w, x) in enumerate(todo):
                            last = nc.tensor.matmul(ps[:, 2 + m % HB], w, x, start=(j == 0), stop=(j == len(todo) - 1))
                        last.then_inc(h_done, 1)
                        if m == FK - 3 and more(c, 1):
                            turn(c + 1, 1 - h)
                    if not is_first(c):
                        outputs(c - 1, 1 - h)

                def outputs(c, h):
                    pe.wait_ge(o_scaled, c + 1)
                    pe.wait_ge(lo_ready, FK * (c + 1) + 2)
                    for k in range(CT):
                        todo = [(a[:, h, m, k * P:(k + 1) * P], wpT[:, m]) for m in range(FK) for a in sq]
                        for j, (x, w) in enumerate(todo):
                            last = nc.tensor.matmul(ps[:, 6 + k // 2, (k % 2) * D:(k % 2 + 1) * D], x, w,
                                                    start=(j == 0 and k % 2 == 0), stop=(j == len(todo) - 1), skip_group_check=True)
                    last.then_inc(o_done, 1)
                chunks(pe, body, first=True)
                outputs(NC - 1, (NC - 1) % 2)


N = 16
GC = P // N
NG = D // GC
SLOT = 4
LEVELS = 7
TPB = SEQ // P
REACH = [1, 2, 4]
GT_, OB_, PT1_ = range(3)
KEPT = PT1_ + len(REACH)


class StateSpaceInputs:

    def __init__(self, sbuf, stack, *inputs):
        self.inputs = inputs
        self.vA = sbuf(stack, "vA", [P, NG, N])
        self.bB = sbuf(stack, "bB", [P, NG, N])
        self.rowsB = sbuf(stack, "rowsB", [NG, 2, P])
        self.rowsD = sbuf(stack, "rowsD", [NG, GC])

    def semaphores(self, sem):
        self.a_loaded, self.bb_loaded, self.bc_loaded = (sem("s_" + n) for n in ("a_loaded", "bb_loaded", "bc_loaded"))

    def load(self, sp):
        a, bm, cm, dm = self.inputs
        sp.dma_start(self.vA[:], a.rearrange("(g c) n m -> (c n) g m", c=GC)).then_inc(self.a_loaded, 16)
        for s, rows in enumerate((bm, cm)):
            sp.dma_start(self.rowsB[:, s], rows.rearrange("(g c) n -> g (c n)", c=GC)).then_inc(self.bc_loaded, 16)
        sp.dma_start(self.rowsD[:], dm.rearrange("(g c) -> g c", c=GC)).then_inc(self.bc_loaded, 16)
        for c in range(GC):
            sp.dma_start(self.bB[c * N:(c + 1) * N], bm.rearrange("(g c) m -> c g m", c=GC)[c].partition_broadcast(N)).then_inc(self.bb_loaded, 16)


def ssm(nc, sem, sbuf, ps, X, ident, ssi, bm_in, cm_in, lnw_in, lnb_in, wout_in, bout_in, by_k):
    zline = nc.dram_tensor("toeplitz_lines", [D, 2 * P], F32, kind="Internal").ap()
    NB = NG // SLOT
    HS = SLOT // 2
    W = GC * NT
    with ExitStack() as st:
        vA, bB, rowsB, rowsD = ssi.vA, ssi.bB, ssi.rowsB, ssi.rowsD
        a_loaded, bb_loaded, bc_loaded = ssi.a_loaded, ssi.bb_loaded, ssi.bc_loaded
        woT = sbuf(st, "woT", [P, DK, D])
        lnwb = sbuf(st, "lnwb", [P, 2, DK])
        turned = sbuf(st, "turned", [P, P])
        Y = sbuf(st, "Y", [P, NT, D])
        with ExitStack() as s0:
            mask = sbuf(s0, "mask", [P, GC])
            ab = sbuf(s0, "ab", [P, NG])
            abt = sbuf(s0, "abt", [P, NG, N])
            vBC = sbuf(s0, "vBC", [P, 2, NG])
            dcol = sbuf(s0, "dcol", [GC, NG])
            rowBC = sbuf(s0, "rowBC", [GC, 2, NG, N])
            wo = sbuf(s0, "wo_rows", [P, DK, D])
            rowsL = sbuf(s0, "rowsL", [DK, 2, P])
            bout = sbuf(s0, "bout", [P, D])
            cb = sbuf(s0, "cb", [GC, NG, N])
            k0 = sbuf(s0, "k0", [GC, NG])
            W1 = sbuf(s0, "W1", [P, SLOT, 2 * P])
            W2 = sbuf(s0, "W2", [P, SLOT, 2 * P])
            Cbd = sbuf(s0, "Cbd", [P, SLOT, GC])
            zk = sbuf(s0, "zk", [GC, 2, SLOT, P])
            zero = sbuf(s0, "zeros", [P, DK, P])
            KM = sbuf(s0, "KM", [P, 2, SLOT, KEPT, P])
            TB = sbuf(s0, "TB", [P, 2, SLOT, GC, P])
            xs = sbuf(s0, "xs", [P, 2, SLOT, GC, NT])
            yl = sbuf(s0, "yl", [P, SLOT, 2, P])
            gm = sbuf(s0, "gm", [P, HS, GC, NT])
            hs = sbuf(s0, "hs", [P, SLOT, NT])
            hm = sbuf(s0, "hm", [P, SLOT, GC, BATCH, TPB])
            rows_loaded, wo_loaded, small_kept, z_zeroed, z_turn, t_steps, mz, mask_ready, zero_ready = (
                sem("s_" + n) for n in ("rows_loaded", "wo_loaded", "small_kept", "z_zeroed", "z_turn", "turned_steps", "mask_steps", "mask_ready", "zero_ready"))
            bc_tr, wo_tr, ab_steps, built, o_copied, k_done, k_kept, gt_done, gt_kept = (
                sem("s_" + n) for n in ("bc_tr", "wo_tr", "ab_steps", "built", "o_copied", "k_done", "k_kept", "gt_done", "gt_kept"))
            x_steps, hmz, xs_ready, g_done, g_steps, T_done, T_kept, ks_done, hs_ready, hm_ready, y_done, y_kept = (
                sem("s_" + n) for n in ("x_steps", "hm_zeroed", "xs_ready", "g_done", "g_steps", "T_done", "T_kept", "ks_done", "hs_ready", "hm_ready", "y_done", "y_kept"))
            pool_turn = sem("s_pool_turn")
            norm = ChunkNorm(nc, sem, sbuf, s0, "ln3", X)
            xn_done = norm.ready
            assert NC <= LEVELS + 1
            stored = [sem(f"z_stored{z}") for z in range(2)]
            loaded = [[sem(f"t_loaded{z}{j}") for j in range(SLOT)] for z in range(2)]
            lv, w1r, w2r = ([sem(f"s_{n}{h}") for h in range(2)] for n in ("level", "w1_ready", "w2_ready"))
            LV, W1N, W2N = LEVELS + 3, LEVELS + 1, LEVELS + 3
            NS = len(REACH)
            HSN = 2 + NS
            SMALL = 4
            G_BANK, T_BANK, Y_BANK = (5, 6), (7, 5), (6, 7)
            slots = lambda h: range(HS * h, HS * h + HS)
            of_pair = lambda t, h: t[:, HS * h:HS * h + HS]

            def pair(side, h):
                return ps[:, 2 * h + side].rearrange("p (s n) -> p s n", s=HS)
            in_bank = lambda bank, j: ps[:, bank, (j % HS) * W:(j % HS + 1) * W]
            scan = lambda d: ps[:, SMALL, 0:SLOT * NT].rearrange("p (s n) -> p s n", s=SLOT)[:, :, 0:BATCH * (TPB - 1 - d)]
            by_batch = lambda v: v.rearrange("p s (b c) -> p s b c", b=BATCH)

            def batches(eng, body):
                body((0, 0), None)
                with eng.Fori(0, (NB - 2) // 2) as i:
                    body((2 * i + 1, 1), (2 * i, 0))
                    body((2 * i + 2, 0), (2 * i + 1, 1))
                body((NB - 1, 1), (NB - 2, 0))
                body(None, (NB - 1, 1))
            assert NB % 2 == 0

            with nc.Block() as block:
                @block.sync
                def _(sp):
                    sp.dma_start(wo[:], by_k(wout_in)).then_inc(wo_loaded, 16)
                    for s, row in enumerate((lnw_in, lnb_in)):
                        sp.dma_start(rowsL[:, s], row.rearrange("(k p) -> k p", p=P)).then_inc(wo_loaded, 16)
                    sp.dma_start(bout[:], bout_in.partition_broadcast(P)).then_inc(wo_loaded, 16)
                    for s, rows in enumerate((bm_in, cm_in)):
                        sp.dma_start(rowBC[:, s], rows.rearrange("(g c) n -> c g n", c=GC)).then_inc(rows_loaded, 16)
                    sp.wait_ge(zero_ready, 1)
                    sp.dma_start(zline.rearrange("(k p) n -> p k n", p=P)[:, :, P:2 * P], zero[:]).then_inc(z_zeroed, 16)
                    for z in range(2):
                        sp.sem_inc(stored[z], 16)
                    sp.sem_inc(T_done, 2)
                    sp.wait_ge(z_zeroed, 16)

                    def body(made, used):
                        if made is None:
                            return
                        b, z = made
                        sp.wait_ge(k_kept, 2 * b + 2)
                        sp.sem_inc(z_turn, 1)
                        sp.dma_start(zline.rearrange("(g c) n -> c g n", c=GC)[:, ds(SLOT * b, SLOT), 0:P], zk[:, z]).then_inc(stored[z], 16)
                        sp.wait_ge(stored[z], 16 * (b // 2) + 32)
                        if used is not None:
                            sp.wait_ge(T_done, 2 * b)
                        sp.sem_inc(z_turn, 1)
                        for j in range(SLOT):
                            line = zline.rearrange("(g c) n -> g c n", c=GC)[ds(SLOT * b + j, 1), :, 0:P]
                            sp.dma_start(TB[:, z, j], toeplitz(line)).then_inc(loaded[z][j], 16)
                    batches(sp, body)

                @block.gpsimd
                def _(pool):
                    nc.gpsimd.memset(mask[:], 1.0).then_inc(mz, 1)
                    nc.gpsimd.memset(turned[:], 0.0).then_inc(t_steps, 1)
                    pool.wait_ge(mz, 1)
                    nc.gpsimd.affine_select(out=mask[:], in_=mask[:], compare_op=ALU.is_ge, fill=0.0, base=0,
                                            pattern=[[-N, GC]], channel_multiplier=1).then_inc(mz, 1)
                    pool.wait_ge(mz, 2)
                    nc.gpsimd.affine_select(out=mask[:], in_=mask[:], compare_op=ALU.is_ge, fill=0.0, base=N - 1,
                                            pattern=[[N, GC]], channel_multiplier=-1).then_inc(mask_ready, 1)
                    pool.wait_ge(t_steps, 1)
                    nc.gpsimd.affine_select(out=turned[:], in_=turned[:], compare_op=ALU.not_equal, fill=1.0, base=1 - P,
                                            pattern=[[1, P]], channel_multiplier=1).then_inc(t_steps, 1)

                    nc.gpsimd.memset(zero[:], 0.0).then_inc(zero_ready, 1)
                    norm.start(pool)
                    for c in range(NC):
                        norm.root(pool, c, c % 2)
                    nc.gpsimd.memset(hm[:], 0.0).then_inc(hmz, 1)

                    def body(made, used):
                        if made is None:
                            return
                        b, z = made
                        def inputs():
                            pool.sem_inc(pool_turn, 1)
                            for j in range(SLOT):
                                nc.gpsimd.tensor_copy(xs[:, z, j], Y[:, :, ds(GC * (SLOT * b + j), GC)].rearrange("p t c -> p c t")).then_inc(xs_ready, 1)
                        if used is None:
                            pool.wait_ge(xn_done, NC)
                            inputs()
                        for h in range(2):
                            pool.wait_ge(w2r[h], W2N * b + LEVELS + 2)
                            pool.sem_inc(pool_turn, 1)
                            nc.gpsimd.tensor_copy(of_pair(KM[:, z], h)[:, :, OB_], of_pair(W2, h)[:, :, 0:P]).then_inc(o_copied, 1)
                        if used is None:
                            for c in range(NC):
                                chunk = lambda v: v[:, CT * c:CT * (c + 1), :].rearrange("p k d -> p (k d)")
                                nc.gpsimd.tensor_tensor(chunk(X), chunk(X), chunk(Y), op=ALU.add).then_inc(x_steps, 1)
                            pool.wait_ge(x_steps, NC)
                            pool.wait_ge(wo_loaded, 64)
                        else:
                            pool.wait_ge(T_done, 2 * b)
                            inputs()
                        tiles = ds(NT // NB * b, NT // NB)
                        nc.gpsimd.tensor_tensor(X[:, tiles, :], X[:, tiles, :], bout[:].unsqueeze(1).broadcast_to([P, NT // NB, D]), op=ALU.add)
                    batches(pool, body)

                @block.vector
                def _(dve):
                    dve.wait_ge(a_loaded, 16)
                    dve.wait_ge(bb_loaded, 16 * GC)
                    nc.vector.tensor_tensor(abt[:], vA[:], bB[:], op=ALU.mult).then_inc(ab_steps, 1)
                    dve.wait_ge(ab_steps, 1)
                    nc.vector.reduce_sum(ab[:], abt[:], AX).then_inc(ab_steps, 1)
                    dve.wait_ge(bc_tr, 1)
                    nc.vector.tensor_copy(vBC[:].rearrange("p s g -> p (s g)"), ps[:, 7, 0:2 * NG]).then_inc(ab_steps, 1)
                    nc.vector.tensor_copy(dcol[:], ps[0:GC, 7, 2 * NG:3 * NG]).then_inc(ab_steps, 1)
                    dve.wait_ge(ab_steps, 4)
                    dve.wait_ge(mask_ready, 1)

                    def build(b):
                        these = ds(SLOT * b, SLOT)
                        for h in range(2):
                            dve.wait_ge(w2r[h], W2N * b + 1)
                        dve.wait_ge(o_copied, 2 * b + 2)
                        spread = mask[:].unsqueeze(1).broadcast_to([P, SLOT, GC])
                        nc.vector.tensor_tensor(W1[:, :, P:2 * P].rearrange("p s (c n) -> p s c n", n=N),
                                                vA[:, these, :].unsqueeze(2).broadcast_to([P, SLOT, GC, N]),
                                                spread.unsqueeze(3).broadcast_to([P, SLOT, GC, N]), op=ALU.mult)
                        nc.vector.tensor_copy(W1[:, :, P - 1], ab[:, these])
                        nc.vector.tensor_copy(W2[:, :, P - 1], vBC[:, 1, these])
                        nc.vector.tensor_tensor(Cbd[:], vBC[:, 1, these].unsqueeze(2).broadcast_to([P, SLOT, GC]), spread, op=ALU.mult).then_inc(built, 1)

                    def keep_level(b, z, l):
                        m = 1 << l
                        for h in range(2):
                            if l <= LEVELS:
                                dve.wait_ge(lv[h], LV * b + l + 2)
                                src, dst = pair(0, h), of_pair(W1, h)
                                if l < LEVELS:
                                    nc.vector.tensor_copy(dst[:, :, P - 2 * m:P - m], src[:, :, 0:m])
                                o = m if l < LEVELS else 0
                                nc.vector.tensor_copy(dst[:, :, P:2 * P], src[:, :, o:o + P]).then_inc(w1r[h], 1)
                        small = ps[:, SMALL].rearrange("p (s n) -> p s n", n=P)
                        if l == LEVELS:
                            dve.wait_ge(k_done, b + 1)
                            dve.wait_ge(stored[z], 16 * (b // 2) + 16)
                            nc.vector.tensor_copy(zk[:, z, :, 0:P - 1], small[0:GC, :, 1:P]).then_inc(k_kept, 1)
                            nc.vector.tensor_copy(zk[:, z, :, P - 1:P], k0[:, ds(SLOT * b, SLOT)].unsqueeze(2)).then_inc(k_kept, 1)
                        if l == LEVELS + 1:
                            dve.wait_ge(gt_done, b + 1)
                            nc.vector.tensor_copy(KM[:, z, :, GT_], small).then_inc(gt_kept, 1)

                    def beside_first(l):
                        if l < NC:
                            norm.stats(dve, l, l % 2)
                        if 0 < l <= NC:
                            tiles = slice(CT * (l - 1), CT * l)
                            norm.apply(dve, l - 1, (l - 1) % 2, lambda k: Y[:, tiles.start + k])

                    def recur(b, l):
                        if l < 2:
                            p = l
                            dve.wait_ge(g_done, 2 * b + p + 1)
                            if p > 0:
                                dve.wait_ge(hs_ready, HSN * b + p)
                            for j in slots(p):
                                nc.vector.tensor_tensor(gm[:, j % HS], in_bank(G_BANK[p], j).rearrange("p (c t) -> p c t", c=GC),
                                                        mask[:].unsqueeze(2).broadcast_to([P, GC, NT]), op=ALU.mult).then_inc(g_steps, 1)
                            dve.wait_ge(g_steps, HS * (2 * b + p + 1))
                            nc.vector.reduce_sum(of_pair(hs, p), gm[:].rearrange("p s c t -> p s t c"), AX).then_inc(hs_ready, 1)
                        elif l < 2 + NS:
                            d = REACH[l - 2]
                            dve.wait_ge(ks_done, NS * b + l - 1)
                            dve.wait_ge(hs_ready, HSN * b + l)
                            for j in range(SLOT):
                                v = by_batch(hs[:, j:j + 1])[:, 0, :, d:TPB - 1]
                                last = nc.vector.tensor_tensor(v, by_batch(scan(d)[:, j:j + 1])[:, 0], v, op=ALU.add)
                            last.then_inc(hs_ready, 1)
                        elif l < 4 + NS:
                            dve.wait_ge(hs_ready, HSN * b + HSN)
                            for j in slots(l - 2 - NS):
                                before = by_batch(hs[:, j:j + 1])[:, 0, :, 0:TPB - 1]
                                nc.vector.tensor_tensor(hm[:, j, :, :, 1:TPB], before.unsqueeze(1).broadcast_to([P, GC, BATCH, TPB - 1]),
                                                        mask[:].unsqueeze(2).unsqueeze(3).broadcast_to([P, GC, BATCH, TPB - 1]), op=ALU.mult).then_inc(hm_ready, 1)

                    def body(made, used):
                        if made is not None:
                            build(made[0])
                        if used is None:
                            dve.wait_ge(rows_loaded, 32)
                            nc.vector.tensor_tensor(cb[:], rowBC[:, 0], rowBC[:, 1], op=ALU.mult).then_inc(ab_steps, 1)
                            dve.wait_ge(ab_steps, 5)
                            nc.vector.reduce_sum(k0[:], cb[:], AX).then_inc(ab_steps, 1)
                            dve.wait_ge(ab_steps, 6)
                            nc.vector.tensor_tensor(k0[:], k0[:], dcol[:], op=ALU.add).then_inc(ab_steps, 1)
                            dve.wait_ge(ab_steps, 7)
                        for l in range(LEVELS + 2):
                            if made is not None:
                                keep_level(*made, l)
                            if used is not None:
                                recur(used[0], l)
                            else:
                                beside_first(l)
                        if used is None:
                            dve.wait_ge(hmz, 1)
                    batches(dve, body)

                @block.scalar
                def _(act):
                    act.sem_inc(o_copied, 2)
                    for h in range(2):
                        act.sem_inc(w2r[h], 1)
                    act.sem_inc(T_kept, 2)
                    act.sem_inc(y_kept, 2)

                    def keep_level(b, z, l):
                        m = 1 << l
                        for h in range(2):
                            act.wait_ge(lv[h], LV * b + l + 2)
                            src, dst = pair(1, h), of_pair(W2, h)
                            o = m if l < LEVELS else 0
                            if l < LEVELS:
                                nc.scalar.copy(dst[:, :, P - 2 * m:P - m], src[:, :, 0:m])
                            if l >= LEVELS - 1:
                                last = nc.scalar.copy(of_pair(KM[:, z], h)[:, :, PT1_ + l - LEVELS + 1], src[:, :, o:o + P])
                            if l <= LEVELS:
                                last = nc.scalar.copy(dst[:, :, P:2 * P], src[:, :, o:o + P])
                            last.then_inc(w2r[h], 1)

                    def recur(b, l):
                        first = 2 + NS
                        if first <= l < first + 2:
                            p = l - first
                            act.wait_ge(T_done, 2 * b + p + 3)
                            nc.scalar.copy(of_pair(yl, p).rearrange("p s q n -> p (s q n)"), ps[:, T_BANK[p]]).then_inc(T_kept, 1)
                        elif first + 2 <= l:
                            p = l - first - 2
                            act.wait_ge(y_done, 2 * b + p + 1)
                            act.wait_ge(x_steps, NC)
                            nc.scalar.copy(Y[:, :, ds(GC * (SLOT * b + HS * p), HS * GC)], ps[:, Y_BANK[p]].rearrange("p (c t) -> p t c", t=NT)).then_inc(y_kept, 1)

                    def body(made, used):
                        if made is not None:
                            b = made[0]
                            for h in range(2):
                                act.wait_ge(lv[h], LV * b + 1)
                                nc.scalar.copy(of_pair(W2, h)[:, :, P:2 * P], pair(1, h)[:, :, 0:P]).then_inc(w2r[h], 1)
                        for l in range(LEVELS + 2):
                            if made is not None:
                                keep_level(*made, l)
                            if used is not None:
                                recur(used[0], l)
                        if used is None:
                            act.wait_ge(wo_tr, 1)
                            nc.scalar.copy(woT[:].rearrange("p k n -> p (k n)"), ps[:, 5]).then_inc(small_kept, 1)
                            nc.scalar.copy(lnwb[:].rearrange("p s k -> p (s k)"), ps[:, 6, 0:2 * DK]).then_inc(small_kept, 1)
                    batches(act, body)

                @block.tensor
                def _(pe):
                    pe.wait_ge(bc_loaded, 48)
                    for s in range(2):
                        nc.tensor.transpose(ps[:, 7, s * NG:(s + 1) * NG], rowsB[:, s], ident[0:NG, 0:NG])
                    nc.tensor.transpose(ps[0:GC, 7, 2 * NG:3 * NG], rowsD[:], ident[0:NG, 0:NG]).then_inc(bc_tr, 1)

                    def inputs(b, z, p):
                        if p == 0:
                            pe.wait_ge(gt_kept, b + 1)
                            pe.wait_ge(T_kept, 2 * b + 2)
                        else:
                            pe.wait_ge(y_kept, 2 * b + 1)
                        for j in slots(p):
                            pe.wait_ge(xs_ready, SLOT * b + j + 1)
                            last = nc.tensor.matmul(in_bank(G_BANK[p], j), KM[:, z, j, GT_], xs[:, z, j].rearrange("p c t -> p (c t)"), start=True, stop=True, skip_group_check=True)
                        last.then_inc(g_done, 1)

                    def recur(b, z, l):
                        if 2 <= l < 2 + NS:
                            k, d = l - 2, REACH[l - 2]
                            if k == 0:
                                for h in range(2):
                                    pe.wait_ge(w2r[h], W2N * b + W2N + 1)
                            pe.wait_ge(hs_ready, HSN * b + l)
                            for j in range(SLOT):
                                last = nc.tensor.matmul(scan(d)[:, j], KM[:, z, j, PT1_ + k], by_batch(hs[:, j:j + 1])[:, 0, :, 0:TPB - 1 - d],
                                                        start=True, stop=True, skip_group_check=True)
                            last.then_inc(ks_done, 1)
                        elif 2 + NS <= l < 4 + NS:
                            p = l - 2 - NS
                            if p == 0:
                                pe.wait_ge(y_kept, 2 * b + 2)
                            for j in slots(p):
                                pe.wait_ge(loaded[z][j], 16 * (b // 2) + 16)
                                for q in range(2):
                                    for c in range(4):
                                        last = nc.tensor.matmul(in_bank(T_BANK[p], j)[NT * c:NT * (c + 1), q * P:(q + 1) * P],
                                                                xs[:, z, j, 4 * q + c], TB[:, z, j, 4 * q + c], start=True, stop=True, skip_group_check=True)
                            last.then_inc(T_done, 1)
                        elif 4 + NS <= l:
                            p = l - 4 - NS
                            pe.wait_ge(o_copied, 2 * b + 4)
                            pe.wait_ge(T_kept, 2 * b + p + 3)
                            for j in slots(p):
                                pe.wait_ge(hm_ready, SLOT * b + j + 1)
                                nc.tensor.matmul(in_bank(Y_BANK[p], j), KM[:, z, j, OB_], hm[:, j].rearrange("p c b t -> p (c b t)"), start=True, stop=False, skip_group_check=True)
                                for q in range(2):
                                    last = nc.tensor.matmul(in_bank(Y_BANK[p], j)[:, q * P:(q + 1) * P], yl[:, j, q], ident[:], start=False, stop=(q == 1), skip_group_check=True)
                            last.then_inc(y_done, 1)

                    def level(b, l):
                        m = 1 << l
                        for h in range(2):
                            if l > 0:
                                pe.wait_ge(w1r[h], W1N * b + l)
                            pe.wait_ge(w2r[h], W2N * b + l + 2)
                            c = m if l < LEVELS else 0
                            for s in slots(h):
                                if l <= LEVELS:
                                    nc.tensor.matmul(pair(0, h)[:, s % HS, 0:c + P], W2[:, s, P:2 * P], W1[:, s, P - c:2 * P], start=True, stop=True, skip_group_check=True)
                                last = nc.tensor.matmul(pair(1, h)[:, s % HS, 0:c + P], W1[:, s, P:2 * P], W2[:, s, P - c:2 * P], start=True, stop=True, skip_group_check=True)
                            last.then_inc(lv[h], 1)

                    def body(made, used):
                        if used is not None:
                            for p in range(2):
                                inputs(*used, p)
                        if made is not None:
                            b = made[0]
                            pe.wait_ge(built, b + 1)
                            for h in range(2):
                                for s in slots(h):
                                    last = nc.tensor.transpose(pair(1, h)[:, s % HS, 0:P], W1[:, s, P:2 * P], ident[:])
                                last.then_inc(lv[h], 1)
                        for l in range(LEVELS + 2):
                            if made is not None:
                                if l == LEVELS:
                                    if used is not None:
                                        pe.wait_ge(hs_ready, HSN * b)
                                    for h in range(2):
                                        pe.wait_ge(w1r[h], W1N * b + l)
                                    for s in range(SLOT):
                                        last = nc.tensor.matmul(ps[0:GC, SMALL, s * P:(s + 1) * P], Cbd[:, s], W1[:, s, 0:P], start=True, stop=True, skip_group_check=True)
                                    last.then_inc(k_done, 1)
                                if l == LEVELS + 1:
                                    pe.wait_ge(k_kept, 2 * b + 1)
                                    for s in range(SLOT):
                                        last = nc.tensor.transpose(ps[:, SMALL, s * P:(s + 1) * P], W1[:, s, 0:P], ident[:])
                                    last.then_inc(gt_done, 1)
                                level(b, l)
                            if used is not None:
                                recur(*used, l)
                        if used is None:
                            pe.wait_ge(wo_loaded, 64)
                            for s in range(2):
                                nc.tensor.transpose(ps[:, 6, s * DK:(s + 1) * DK], rowsL[:, s], ident[0:DK, 0:DK])
                            for dk in range(DK):
                                for o in range(DK):
                                    last = nc.tensor.transpose(ps[:, 5, dk * D + o * P:dk * D + (o + 1) * P], wo[:, o, dk * P:(dk + 1) * P], ident[:])
                            last.then_inc(wo_tr, 1)
                            pe.wait_ge(small_kept, 2)
                    batches(pe, body)

        ssm_output(nc, sem, sbuf, ps, X, Y, ident, woT, lnwb, turned)


def toeplitz(line):
    a = line.rearrange("a c n -> (a c) n")
    return bass.AP(tensor=a.tensor, offset=a.offset, ap=[[1, P], *a.ap])


def ssm_output(nc, sem, sbuf, ps, X, Y, ident, woT, lnwb, turned):
    with ExitStack() as st:
        yn = sbuf(st, "yn", [P, 2, CT, D])
        gT = sbuf(st, "gT", [P, 2, DK, CW])
        norm = ChunkNorm(nc, sem, sbuf, st, "lny", Y)
        n_tr, g_ready, o_done, o_added = (sem("so_" + n) for n in ("n_tr", "g_ready", "done", "added"))
        with nc.Block() as block:
            @block.gpsimd
            def _(pool):
                norm.start(pool)
                for c in range(2):
                    norm.root(pool, c, c)

                def body(c, h):
                    if more(c, 2):
                        norm.root(pool, c + 2, h)
                chunks(pool, body)

            @block.vector
            def _(dve):
                dve.sem_inc(o_added, 2)
                norm.stats(dve, 0, 0)
                norm.stats(dve, 1, 1)
                norm.apply(dve, 0, 0, lambda k: yn[:, 0, k])

                def body(c, h):
                    if more(c, 2):
                        norm.stats(dve, c + 2, h)
                    if more(c, 1):
                        if not is_first(c):
                            dve.wait_ge(n_tr, c)
                        norm.apply(dve, c + 1, 1 - h, lambda k: yn[:, 1 - h, k])
                    if not is_first(c):
                        add(c - 1, 1 - h)

                def add(c, h):
                    dve.wait_ge(o_done, c + 1)
                    chunk = X[:, ds(CT * c, CT), :].rearrange("p k d -> p (k d)")
                    nc.vector.tensor_tensor(chunk, ps[:, 4 + 2 * h:6 + 2 * h].rearrange("p a n -> p (a n)"), chunk, op=ALU.add).then_inc(o_added, 1)
                chunks(dve, body, first=True)
                add(NC - 1, 1)

            @block.scalar
            def _(act):
                def body(c, h):
                    act.wait_ge(n_tr, c + 1)
                    act.wait_ge(o_added, c + 1)
                    for dk in range(DK):
                        nc.scalar.activation(gT[:, h, dk], ps[:, 2 * h + dk], ACT.Gelu, bias=lnwb[:, 1, dk:dk + 1], scale=lnwb[:, 0, dk:dk + 1]).then_inc(g_ready, 1)
                chunks(act, body)

            @block.tensor
            def _(pe):
                def turn(c, h):
                    pe.wait_ge(norm.ready, c + 1)
                    for dk in range(DK):
                        for k in range(CT):
                            last = nc.tensor.matmul(ps[:, 2 * h + dk, k * P:(k + 1) * P], yn[:, h, k, dk * P:(dk + 1) * P], turned[:],
                                                    start=True, stop=True, skip_group_check=True)
                    last.then_inc(n_tr, 1)
                turn(0, 0)

                def body(c, h):
                    if more(c, 1):
                        turn(c + 1, 1 - h)
                    pe.wait_ge(g_ready, DK * (c + 1))
                    pe.wait_ge(o_added, c + 1)
                    for k in range(CT):
                        for dk in range(DK):
                            last = nc.tensor.matmul(ps[:, 4 + 2 * h + k // 2, (k % 2) * D:(k % 2 + 1) * D], gT[:, h, dk, k * P:(k + 1) * P], woT[:, dk],
                                                    start=(dk == 0 and k % 2 == 0), stop=(dk == DK - 1), skip_group_check=True)
                    last.then_inc(o_done, 1)
                chunks(pe, body)


def moe(nc, sem, sbuf, ps, X, ident, out_tiles, wg_in, bg_in, bias_in, w1_in, b1_in, w2_in, b2_in):
    FREE = -(-MT // NT) * NT
    xrows = nc.dram_tensor("expert_inputs", [T, D], F32, kind="Internal").ap()
    y_rows = nc.dram_tensor("expert_outputs", [FREE * P + 2 * T, D], F32, kind="Internal").ap()
    with ExitStack() as st:
        W1 = sbuf(st, "eW1", [P, E, DK, EH])
        W2 = sbuf(st, "eW2", [P, E, EK, D])
        b1T = sbuf(st, "b1T", [P, E * EK])
        weight = sbuf(st, "weight", [P, 2, NT])
        owner = sbuf(st, "owner", [P, MT], I32)
        token = sbuf(st, "token", [P, MT], I32)
        y_row = sbuf(st, "y_row", [P, MT], I32)
        w_loaded = [sem(f"e_w_loaded{q}") for q in range(2)]
        with ExitStack() as s0:
            xc = sbuf(s0, "e_xn", [P, 2, CT, D])
            xT = sbuf(s0, "e_xT", [P, 2, DK, CW])
            wg = sbuf(s0, "wg", [P, DK, E])
            bgb = sbuf(s0, "bgb", [P, 2, E])
            b1r = sbuf(s0, "b1r", [E * EK, P])
            L, hot1, hot2, tmp, C = (sbuf(s0, "r_" + n, [P, NT, E]) for n in ("logits", "hot1", "hot2", "tmp", "sums"))
            assert CW <= NT * E
            lT = [t[0:E].rearrange("e t x -> e (t x)")[:, 0:CW] for t in (C, tmp)]
            top, at = (sbuf(s0, "r_" + n, [P, 2, NT]) for n in ("top", "at"))
            ex = sbuf(s0, "r_exp", [P, 3, NT])
            PLACES = 8
            ai, pi, ci = (sbuf(s0, "r_" + n, [P, w], I32) for n, w in (("ai", P), ("pi", 1), ("ci", 2 * NT)))
            oi, own = sbuf(s0, "r_oi", [P, MT], I32), sbuf(s0, "r_own", [P, MT])
            lane = sbuf(s0, "r_lane", [P, P], BF16)
            tile_no = sbuf(s0, "r_tile_no", [P, MT], BF16)
            part_no, row_tile = sbuf(s0, "r_part_no", [P, 1]), sbuf(s0, "r_row_tile", [P, 2, NT], BF16)
            place = sbuf(s0, "r_place", [P, 2, NT], I32)
            split = sbuf(s0, "r_split", [P, 2, 2, NT], I32)
            at2 = sbuf(s0, "r_at2", [P, 2, 2, NT], BF16)
            in_lane = sbuf(s0, "r_in_lane", [P, 2, PLACES, P], BF16)
            in_tile = sbuf(s0, "r_in_tile", [P, 2, PLACES, 2, MT], BF16)
            is_tile = sbuf(s0, "r_is_tile", [P, 2, PLACES, MT], BF16)
            tab = sbuf(s0, "r_tab", [P, MT])
            held = xT[:].rearrange("p h k n -> p (h k n)")[:, 0:MT * E].rearrange("p (m e) -> p m e", e=E)
            ended = sbuf(s0, "r_ended", [P, MT])
            ne = sbuf(s0, "r_ne", [P, 4, E])
            ni = sbuf(s0, "r_ni", [P, 2, E], I32)
            ei, ti = sbuf(s0, "r_ei", [P, E], I32), sbuf(s0, "r_ti", [P, MT], I32)
            ef, tf = sbuf(s0, "r_ef", [P, E]), sbuf(s0, "r_tf", [P, MT])
            before, ones = sbuf(s0, "r_before", [P, P], BF16), sbuf(s0, "r_ones", [P, P], BF16)
            chosen = sbuf(s0, "r_chosen", [P, NT, E], BF16)
            norm = ChunkNorm(nc, sem, sbuf, s0, "ln4", X)
            small, x_tr, xT_ready, lg_done, b1_tr, b1_kept, r_steps, r_exp, c_ready, c_done, iotas = (
                sem("r_" + n) for n in ("small_loaded", "x_tr", "xT_ready", "logits_done", "b1_tr", "b1_kept", "steps", "exp", "consts", "counted", "iotas"))
            lt_done, lt_kept = sem("r_lt_done"), sem("r_lt_kept")
            hot_ready, gap_ready, one_hot, with_part, with_tile, summed = (sem("r_" + n) for n in ("hot_ready", "gap_ready", "one_hot", "with_part", "with_tile", "summed"))
            stored = [sem(f"r_stored{h}") for h in range(2)]

            def places(body):
                for n in range(2 * NT // PLACES):
                    body(n, n % 2, n // 2 * PLACES)
            with nc.Block() as block:
                @block.sync
                def _(sp):
                    sp.dma_start(wg[:], wg_in.rearrange("(k p) e -> p k e", p=P)).then_inc(small, 16)
                    sp.dma_start(bgb[:, 0], bg_in.partition_broadcast(P)).then_inc(small, 16)
                    sp.dma_start(bgb[:, 1], bias_in.partition_broadcast(P)).then_inc(small, 16)
                    sp.dma_start(b1r[:], b1_in.rearrange("e (k p) -> (e k) p", p=P)).then_inc(small, 16)
                    for h in range(2):
                        sp.sem_inc(stored[h], 16)

                    def first_weights(e):
                        sp.dma_start(W1[:, e], w1_in[e].rearrange("(k p) h -> p k h", p=P)).then_inc(w_loaded[0], 16)
                    for c in range(NC):
                        sp.wait_ge(norm.ready, c + 1)
                        sp.dma_start(xrows[CW * c:CW * (c + 1)].rearrange("(k p) d -> p k d", p=P), xc[:, c % 2]).then_inc(stored[c % 2], 16)
                        first_weights(c)
                    for e in range(NC, E):
                        first_weights(e)
                    for q in range(NC):
                        es = slice(q * E // NC, (q + 1) * E // NC)
                        sp.dma_start(W2[:, es], w2_in[es].rearrange("e (k p) d -> p e k d", p=P)).then_inc(w_loaded[1], 16)
                    for h in range(2):
                        sp.wait_ge(stored[h], 16 * (NC // 2 + 1))

                @block.gpsimd
                def _(pool):
                    nc.gpsimd.memset(ones[:], 1.0).then_inc(c_ready, 1)
                    pool.wait_ge(c_ready, 1)
                    nc.gpsimd.affine_select(out=before[:], in_=ones[:], compare_op=ALU.is_ge, fill=0.0, base=-1,
                                            pattern=[[1, P]], channel_multiplier=-1).then_inc(c_ready, 1)
                    nc.gpsimd.iota(ei[:], pattern=[[1, E]], base=-E, channel_multiplier=0).then_inc(iotas, 1)
                    nc.gpsimd.iota(ti[:], pattern=[[1, MT]], base=0, channel_multiplier=0).then_inc(iotas, 1)
                    nc.gpsimd.iota(ai[:], pattern=[[1, P]], base=0, channel_multiplier=0).then_inc(iotas, 1)
                    nc.gpsimd.iota(oi[:], pattern=[[P, MT]], base=0, channel_multiplier=1).then_inc(iotas, 1)
                    nc.gpsimd.iota(pi[:], pattern=[[1, 1]], base=0, channel_multiplier=1).then_inc(iotas, 1)
                    nc.gpsimd.iota(ci[:], pattern=[[1, 2 * NT]], base=FREE, channel_multiplier=0).then_inc(iotas, 1)
                    norm.start(pool)
                    for c in range(2):
                        norm.root(pool, c, c)

                    def body(c, h):
                        if more(c, 2):
                            norm.root(pool, c + 2, h)
                    chunks(pool, body)

                    def tiles(n, s, i):
                        pool.wait_ge(one_hot, 2 * n + 1)
                        nc.gpsimd.tensor_tensor(in_tile[:, s, :, 1], is_tile[:, s], row_tile[:, s, i:i + PLACES].unsqueeze(2).broadcast_to([P, PLACES, MT]),
                                                op=ALU.mult).then_inc(with_tile, 1)
                    places(tiles)

                @block.vector
                def _(dve):
                    norm.stats(dve, 0, 0)
                    norm.stats(dve, 1, 1)
                    norm.apply(dve, 0, 0, lambda k: xc[:, 0, k])

                    def body(c, h):
                        if more(c, 2):
                            norm.stats(dve, c + 2, h)
                        if more(c, 1):
                            dve.wait_ge(x_tr, c + 1)
                            dve.wait_ge(stored[1 - h], 16 * ((c + 1) // 2) + 16)
                            norm.apply(dve, c + 1, 1 - h, lambda k: xc[:, 1 - h, k])
                    chunks(dve, body)
                    dve.wait_ge(b1_tr, 1)
                    nc.vector.tensor_copy(b1T[:], ps[:, 7, 0:E * EK]).then_inc(b1_kept, 1)
                    steps = Count(r_steps)

                    def step(ins):
                        steps.mark(ins)
                        steps.wait(dve)
                    of_e = lambda v: v.unsqueeze(1).broadcast_to([P, NT, E])
                    of_t = lambda v: v.unsqueeze(2).broadcast_to([P, NT, E])
                    dve.wait_ge(iotas, 6)
                    for dst, src in ((lane, ai), (tile_no, ti), (part_no, pi), (own, oi)):
                        steps.mark(nc.vector.tensor_copy(dst[:], src[:]))
                    steps.mark(nc.vector.tensor_copy(row_tile[:].rearrange("p s t -> p (s t)"), ci[:]))
                    steps.mark(nc.vector.tensor_copy(ef[:], ei[:]))
                    step(nc.vector.tensor_copy(tf[:], ti[:]))
                    dve.wait_ge(small, 64)
                    dve.wait_ge(lg_done, NC)
                    step(nc.vector.tensor_tensor(L[:], ps[:, 4].rearrange("p (t e) -> p t e", e=E), of_e(bgb[:, 0]), op=ALU.add))
                    step(nc.vector.tensor_tensor(L[:], L[:], of_e(bgb[:, 1]), op=ALU.add))
                    for s, hot in enumerate((hot1, hot2)):
                        step(nc.vector.reduce_max(top[:, s], L[:], AX))
                        step(nc.vector.tensor_tensor(tmp[:], L[:], of_t(top[:, s]), op=ALU.is_equal))
                        step(nc.vector.tensor_tensor(tmp[:], tmp[:], of_e(ef[:]), op=ALU.mult))
                        step(nc.vector.tensor_reduce(at[:, s], tmp[:], AX, ALU.min))
                        step(nc.vector.tensor_tensor(hot[:], of_t(at[:, s]), of_e(ef[:]), op=ALU.is_equal))
                        if s == 0:
                            step(nc.vector.scalar_tensor_tensor(L[:], hot[:], -3e38, L[:], op0=ALU.mult, op1=ALU.add))
                    nc.vector.tensor_tensor(chosen[:], hot1[:], hot2[:], op=ALU.add).then_inc(hot_ready, 1)
                    nc.vector.tensor_tensor(ex[:, 0], top[:, 1], top[:, 0], op=ALU.subtract).then_inc(gap_ready, 1)
                    dve.wait_ge(c_done, 1)
                    tot = ps[:, 6].rearrange("p (t e) -> p t e", e=E)
                    pre = ps[:, 5].rearrange("p (t e) -> p t e", e=E)
                    step(nc.vector.tensor_copy(C[:], tot))
                    a, b, d = C, L, 1
                    while d < NT:
                        steps.mark(nc.vector.tensor_tensor(b[:, d:NT], a[:, d:NT], a[:, 0:NT - d], op=ALU.add))
                        step(nc.vector.tensor_copy(b[:, 0:d], a[:, 0:d]))
                        a, b, d = b, a, 2 * d
                    step(nc.vector.tensor_scalar(ni[:, 0], a[:, NT - 1], float(P - 1), None, ALU.add))
                    step(nc.vector.tensor_scalar(ni[:, 1], ni[:, 0], P.bit_length() - 1, None, ALU.arith_shift_right))
                    step(nc.vector.tensor_copy(ne[:, 0], ni[:, 1]))
                    step(nc.vector.tensor_copy(ne[:, 1], ne[:, 0]))
                    x, y, d = 1, 2, 1
                    while d < E:
                        steps.mark(nc.vector.tensor_tensor(ne[:, y, d:E], ne[:, x, d:E], ne[:, x, 0:E - d], op=ALU.add))
                        step(nc.vector.tensor_copy(ne[:, y, 0:d], ne[:, x, 0:d]))
                        x, y, d = y, x, 2 * d
                    step(nc.vector.tensor_tensor(ne[:, 3], ne[:, x], ne[:, 0], op=ALU.subtract))
                    step(nc.vector.tensor_scalar_mul(ne[:, 3], ne[:, 3], float(P)))
                    S = b
                    step(nc.vector.tensor_tensor(S[:], a[:], tot, op=ALU.subtract))
                    step(nc.vector.tensor_tensor(S[:], S[:], pre, op=ALU.add))
                    step(nc.vector.tensor_tensor(S[:], S[:], of_e(ne[:, 3]), op=ALU.add))
                    for s, hot in enumerate((hot1, hot2)):
                        step(nc.vector.tensor_tensor(tmp[:], hot[:], S[:], op=ALU.mult))
                        step(nc.vector.reduce_sum(at[:, s], tmp[:], AX))
                    step(nc.vector.tensor_copy(place[:], at[:]))
                    steps.mark(nc.vector.tensor_scalar(split[:, 0], place[:], P.bit_length() - 1, None, ALU.arith_shift_right))
                    step(nc.vector.tensor_scalar(split[:, 1], place[:], P - 1, None, ALU.bitwise_and))
                    step(nc.vector.tensor_copy(at2[:], split[:]))
                    def rows(n, s, i):
                        dve.wait_ge(summed, n + 1)
                        some = slice(i, i + PLACES)
                        nc.vector.tensor_tensor(is_tile[:, s], tile_no[:].unsqueeze(1).broadcast_to([P, PLACES, MT]),
                                                at2[:, 0, s, some].unsqueeze(2).broadcast_to([P, PLACES, MT]), op=ALU.is_equal).then_inc(one_hot, 1)
                        nc.vector.tensor_tensor(in_lane[:, s], lane[:].unsqueeze(1).broadcast_to([P, PLACES, P]),
                                                at2[:, 1, s, some].unsqueeze(2).broadcast_to([P, PLACES, P]), op=ALU.is_equal).then_inc(one_hot, 1)
                    places(rows)
                    step(nc.vector.tensor_tensor(held, ne[:, x].unsqueeze(1).broadcast_to([P, MT, E]), tf[:].unsqueeze(2).broadcast_to([P, MT, E]), op=ALU.is_le))
                    step(nc.vector.reduce_sum(ended[:], held, AX))
                    step(nc.vector.tensor_scalar(owner[:], ended[:], float(E - 1), None, ALU.min))
                    dve.wait_ge(r_exp, 1)
                    step(nc.vector.tensor_scalar(ex[:, 2], ex[:, 1], 1.0, None, ALU.add))
                    step(nc.vector.reciprocal(weight[:, 0], ex[:, 2]))
                    step(nc.vector.tensor_tensor(weight[:, 1], ex[:, 1], weight[:, 0], op=ALU.mult))
                    dve.wait_ge(summed, 2 + 2 * NT // PLACES)
                    step(nc.vector.tensor_copy(tab[:], ps[:, 0, 0:MT]))
                    step(nc.vector.scalar_tensor_tensor(tab[:], ps[:, 0, MT:2 * MT], float(P), tab[:], op0=ALU.mult, op1=ALU.add))
                    step(nc.vector.scalar_tensor_tensor(own[:], tab[:], 0.0, own[:], op0=ALU.is_equal, op1=ALU.mult))
                    step(nc.vector.tensor_tensor(tab[:], tab[:], own[:], op=ALU.add))
                    step(nc.vector.tensor_copy(y_row[:], tab[:]))
                    step(nc.vector.tensor_scalar(token[:], y_row[:], T - 1, None, ALU.bitwise_and))

                @block.scalar
                def _(act):
                    def body(c, h):
                        act.wait_ge(x_tr, c + 2)
                        nc.scalar.copy(xT[:, h].rearrange("p k n -> p (k n)"), ps[:, 2 * h:2 * h + 2].rearrange("p a n -> p (a n)")).then_inc(xT_ready, 1)
                        if not is_first(c):
                            keep(c - 1, 1 - h)

                    def keep(c, h):
                        act.wait_ge(lt_done, c + 1)
                        nc.scalar.copy(lT[h], ps[0:E, 5 + h, 0:CW]).then_inc(lt_kept, 1)
                    chunks(act, body, first=True)
                    keep(NC - 1, 1)
                    act.wait_ge(gap_ready, 1)
                    nc.scalar.activation(ex[:, 1], ex[:, 0], ACT.Exp).then_inc(r_exp, 1)

                    def parts(n, s, i):
                        act.wait_ge(one_hot, 2 * n + 1)
                        nc.scalar.activation(in_tile[:, s, :, 0], is_tile[:, s], ACT.Copy, scale=part_no[:]).then_inc(with_part, 1)
                    places(parts)

                @block.tensor
                def _(pe):
                    pe.wait_ge(small, 64)
                    nc.tensor.transpose(ps[:, 7, 0:E * EK], b1r[:], ident[0:E * EK, 0:E * EK]).then_inc(b1_tr, 1)

                    pe.sem_inc(x_tr, 1)

                    def turn(c, h):
                        pe.wait_ge(norm.ready, c + 1)
                        for dk in range(DK):
                            for k in range(CT):
                                last = nc.tensor.transpose(ps[:, 2 * h + dk, k * P:(k + 1) * P], xc[:, h, k, dk * P:(dk + 1) * P], ident[:])
                        last.then_inc(x_tr, 1)
                    turn(0, 0)

                    def body(c, h):
                        if more(c, 1):
                            turn(c + 1, 1 - h)
                        pe.wait_ge(xT_ready, c + 1)
                        for dk in range(DK):
                            last = nc.tensor.matmul(ps[0:E, 5 + h, 0:CW], wg[:, dk], xT[:, h, dk], start=(dk == 0), stop=(dk == DK - 1))
                        last.then_inc(lt_done, 1)
                        if not is_first(c):
                            back(c - 1, 1 - h)

                    def back(c, h):
                        pe.wait_ge(lt_kept, c + 1)
                        for k in range(CT):
                            last = nc.tensor.matmul(ps[:, 4, ds(E * (CT * c + k), E)], lT[h][:, k * P:(k + 1) * P], ident[0:E, 0:E],
                                                    start=True, stop=True, skip_group_check=True)
                        last.then_inc(lg_done, 1)
                    chunks(pe, body, first=True)
                    back(NC - 1, 1)
                    pe.wait_ge(c_ready, 2)
                    pe.wait_ge(hot_ready, 1)
                    counted = chosen[:].rearrange("p t e -> p (t e)")
                    nc.tensor.matmul(ps[:, 5], before[:], counted, start=True, stop=True)
                    nc.tensor.matmul(ps[:, 6], ones[:], counted, start=True, stop=True).then_inc(c_done, 1)
                    pe.sem_inc(summed, 2)

                    def add(n, s, i):
                        pe.wait_ge(one_hot, 2 * n + 2)
                        pe.wait_ge(with_part, n + 1)
                        pe.wait_ge(with_tile, n + 1)
                        for j in range(PLACES):
                            last = nc.tensor.matmul(ps[:, 0, 0:2 * MT], in_lane[:, s, j], in_tile[:, s, j].rearrange("p a m -> p (a m)"),
                                                    start=(n == 0 and j == 0), stop=(n == 2 * NT // PLACES - 1 and j == PLACES - 1))
                        last.then_inc(summed, 1)
                    places(add)

        with ExitStack() as s1:
            AHEAD = 4
            xin = sbuf(s1, "e_xin", [P, AHEAD, D])
            xT = sbuf(s1, "e_xinT", [P, 2, DK, P])
            w1 = sbuf(s1, "e_w1", [P, 2, DK, EH])
            hT = sbuf(s1, "e_hiddenT", [P, 2, EK, P])
            y = sbuf(s1, "e_y", [P, 2, D])
            b2b = sbuf(s1, "b2b", [P, E, D])
            index = sbuf(s1, "e_index", [P, AHEAD], U32)
            y_index = sbuf(s1, "e_y_index", [P, 2], U32)
            index_ready, y_index_ready, fetch_turn = sem("e_index_ready"), sem("e_y_index_ready"), sem("e_x_turn")
            x_loaded = [sem(f"e_x_loaded{r}") for r in range(AHEAD)]
            stored = [sem(f"e_y_stored{z}") for z in range(2)]
            b2_loaded, w1_kept, xt_done, xt_kept, ht_done, hta_kept, htb_kept, m2_done, y_kept = (
                sem("e_" + n) for n in ("b2_loaded", "w1_kept", "xt_done", "xt_kept", "ht_done", "hta_kept", "htb_kept", "m2_done", "y_kept"))
            assert AHEAD % 2 == 0
            FIRST = AHEAD + 1
            XT_BANK, HA_BANK, HB_BANK, Y_BANK = (0, 7), (1, 2), (3, 4), (5, 6)
            HK = EK // 2
            of_tile = lambda eng, k: eng.value_load(owner[0:1, ds(k, 1)] if not isinstance(k, int) else owner[0:1, k:k + 1], min_val=0, max_val=E - 1)

            def tiles(eng, body):
                turns = (MT - 1 - FIRST) // AHEAD
                for k in range(FIRST):
                    body(k, k % AHEAD)
                with eng.Fori(0, turns) as i:
                    for r in range(FIRST, FIRST + AHEAD):
                        body(AHEAD * i + r, r % AHEAD)
                for k in range(FIRST + turns * AHEAD, MT):
                    body(k, k % AHEAD)
            with nc.Block() as block:
                @block.sync
                def _(sp):
                    sp.wait_ge(x_loaded[1], 16)
                    sp.dma_start(b2b[:], b2_in.partition_broadcast(P)).then_inc(b2_loaded, 16)

                @block.gpsimd
                def _(pool):
                    pool.sem_inc(xt_done, AHEAD)

                    def fetch(k, r):
                        pool.wait_ge(xt_done, k + 1)
                        pool.sem_inc(fetch_turn, 1)
                        nc.gpsimd.tensor_copy(index[:, r:r + 1], token[:, ds(k, 1)]).then_inc(index_ready, 1)
                        pool.wait_ge(index_ready, k + 1)
                        pool.sem_inc(fetch_turn, 1)
                        nc.gpsimd.indirect_dma_start(xin[:, r], None, xrows, bass.IndirectOffsetOnAxis(ap=index[:, r:r + 1], axis=0)).then_inc(x_loaded[r], 16)

                    def scatter(k, z):
                        pool.wait_ge(y_kept, k + 3)
                        pool.sem_inc(fetch_turn, 1)
                        nc.gpsimd.tensor_copy(y_index[:, z:z + 1], y_row[:, ds(k, 1)]).then_inc(y_index_ready, 1)
                        pool.wait_ge(y_index_ready, k + 1)
                        pool.sem_inc(fetch_turn, 1)
                        nc.gpsimd.indirect_dma_start(y_rows, bass.IndirectOffsetOnAxis(ap=y_index[:, z:z + 1], axis=0), y[:, z], None).then_inc(stored[z], 16)

                    def body(k, r):
                        fetch(k, r)
                        if not isinstance(k, int) or k >= FIRST:
                            scatter(k - FIRST, (r + 1) % 2)
                    tiles(pool, body)
                    for k in range(MT - FIRST, MT):
                        scatter(k, k % 2)
                    for z in range(2):
                        pool.wait_ge(stored[z], 16 * ((MT - z + 1) // 2))

                @block.scalar
                def _(act):
                    def body(k, r):
                        z = r % 2
                        act.wait_ge(xt_done, k + AHEAD + 1)
                        nc.scalar.copy(xT[:, z].rearrange("p k n -> p (k n)"), ps[:, XT_BANK[z], 0:D]).then_inc(xt_kept, 1)
                        if not is_first(k):
                            half(k - 1, 1 - z)
                        if not (isinstance(k, int) and k == MT - 1):
                            first_weights(k + 1, 1 - z)

                    def first_weights(k, z):
                        e = of_tile(act, k)
                        nc.scalar.copy(w1[:, z].rearrange("p k h -> p (k h)"), W1[:, ds(e, 1)].rearrange("p a k h -> p (a k h)")).then_inc(w1_kept, 1)

                    def half(k, z):
                        e = of_tile(act, k)
                        act.wait_ge(ht_done, k + 1)
                        for j in range(HK):
                            nc.scalar.activation(hT[:, z, j], ps[:, HA_BANK[z], j * P:(j + 1) * P], ACT.Relu, bias=b1T[:, ds(EK * e + j, 1)]).then_inc(hta_kept, 1)
                    act.wait_ge(w_loaded[0], 16 * E)
                    first_weights(0, 0)
                    tiles(act, body)
                    half(MT - 1, (MT - 1) % 2)

                @block.vector
                def _(dve):
                    def outputs(k, r):
                        z = r % 2
                        e = of_tile(dve, k)
                        dve.wait_ge(m2_done, k + 1)
                        if not isinstance(k, int) or k >= 2:
                            dve.wait_ge(stored[z], 16 * (k // 2))
                        nc.vector.tensor_tensor(y[:, z], ps[:, Y_BANK[z], 0:D], b2b[:, ds(e, 1), :].rearrange("p a d -> p (a d)"), op=ALU.add).then_inc(y_kept, 1)

                    def body(k, r):
                        z = r % 2
                        e = of_tile(dve, k)
                        dve.wait_ge(ht_done, k + 1)
                        for j in range(HK, EK):
                            nc.vector.tensor_scalar(hT[:, z, j], ps[:, HB_BANK[z], (j - HK) * P:(j - HK + 1) * P], b1T[:, ds(EK * e + j, 1)], 0.0, ALU.add, ALU.max).then_inc(htb_kept, 1)
                        if is_first(k):
                            dve.wait_ge(b2_loaded, 16)
                        else:
                            outputs(k - 1, r - 1)
                    tiles(dve, body)
                    outputs(MT - 1, MT - 1)

                @block.tensor
                def _(pe):
                    def turn_x(k, r):
                        z = r % 2
                        pe.wait_ge(x_loaded[r], 16 * (k // AHEAD) + 16)
                        for dk in range(DK):
                            last = nc.tensor.transpose(ps[:, XT_BANK[z], dk * P:(dk + 1) * P], xin[:, r, dk * P:(dk + 1) * P], ident[:])
                        last.then_inc(xt_done, 1)

                    def second(k, z):
                        e = of_tile(pe, k)
                        pe.wait_ge(y_kept, k + 1)
                        pe.wait_ge(hta_kept, HK * (k + 1))
                        pe.wait_ge(htb_kept, HK * (k + 1))
                        for j in range(EK):
                            last = nc.tensor.matmul(ps[:, Y_BANK[z], 0:D], hT[:, z, j], W2[:, ds(e, 1), j, :].rearrange("p a d -> p (a d)"), start=(j == 0), stop=(j == EK - 1))
                        last.then_inc(m2_done, 1)

                    def body(k, r):
                        z = r % 2
                        pe.wait_ge(w1_kept, k + 1)
                        pe.wait_ge(xt_kept, k + 1)
                        for j in range(EK):
                            bank = (HA_BANK if j < HK else HB_BANK)[z]
                            for dk in range(DK):
                                last = nc.tensor.matmul(ps[:, bank, j % HK * P:(j % HK + 1) * P], w1[:, z, dk, j * P:(j + 1) * P], xT[:, z, dk],
                                                        start=(dk == 0), stop=(dk == DK - 1), skip_group_check=True)
                        last.then_inc(ht_done, 1)
                        if not (isinstance(k, int) and k == MT - 1):
                            turn_x(k + 1, (r + 1) % AHEAD)
                        if not is_first(k):
                            second(k - 1, 1 - z)
                    pe.sem_inc(y_kept, 2)
                    pe.wait_ge(w_loaded[1], 16 * NC)
                    turn_x(0, 0)
                    tiles(pe, body)
                    second(MT - 1, (MT - 1) % 2)

        with ExitStack() as s2:
            LOADED = 4
            got = sbuf(s2, "e_got", [P, LOADED, 2, CT, D])
            w = sbuf(s2, "e_weight", [P, 2, 2, CT])
            loaded = [sem(f"e_y_loaded{r}") for r in range(LOADED)]
            load_turn, w_ready, added, out_turn, out_stored = (sem(n) for n in ("e_load_turn", "e_w_ready", "e_added", "out_turn", "out_stored"))
            with nc.Block() as block:
                @block.sync
                def _(sp):
                    sp.sem_inc(added, 2 * CT * LOADED)
                    with sp.Fori(0, NC // LOADED) as i:
                        for r in range(LOADED):
                            c = LOADED * i + r
                            sp.wait_ge(added, 2 * CT * (c + 1))
                            for s in range(2):
                                sp.sem_inc(load_turn, 1)
                                sp.dma_start(got[:, r, s], y_rows[ds(FREE * P + s * T + CW * c, CW), :].rearrange("(k p) d -> p k d", p=P)).then_inc(loaded[r], 16)

                @block.vector
                def _(dve):
                    with dve.Fori(0, NC // LOADED) as i:
                        for r in range(LOADED):
                            c = LOADED * i + r
                            n = 2 * CT * (c + LOADED)
                            dve.wait_ge(added, n)
                            dve.sem_inc(load_turn, 1)
                            nc.vector.tensor_copy(w[:, r % 2], weight[:, :, ds(CT * c, CT)]).then_inc(w_ready, 1)
                            dve.wait_ge(w_ready, c + 1)
                            dve.wait_ge(loaded[r], 32 * i + 32)
                            for s in range(2):
                                for k in range(CT):
                                    row = X[:, ds(CT * c + k, 1), :].rearrange("p a d -> p (a d)")
                                    nc.vector.scalar_tensor_tensor(row, got[:, r, s, k], w[:, r % 2, s, k:k + 1], row, op0=ALU.mult, op1=ALU.add).then_inc(added, 1)
                                if s == 0:
                                    dve.wait_ge(added, n + CT)

                @block.scalar
                def _(act):
                    with act.Fori(0, NC) as c:
                        act.wait_ge(added, 2 * CT * (c + 1 + LOADED))
                        act.sem_inc(out_turn, 1)
                        act.dma_start(out_tiles[:, ds(CT * c, CT), :], X[:, ds(CT * c, CT), :]).then_inc(out_stored, 16)
                    act.wait_ge(out_stored, 16 * NC)


def attention(nc, sem, stack, sbuf, ps, ident, identb, KQ, kq_loaded, load_qk, V, ffw):
    KQ.append(sbuf(stack, f"KQ{RING - 1}", [P, 2, HG, SEQ], BF16))
    kept = sbuf(stack, "ffn_above", [P, FH])
    PR = sbuf(stack, "PR", [P, 2, HG, SEQ])
    VO = sbuf(stack, "VO", [P, KT, HG, 2 * HD])
    OT = sbuf(stack, "OT", [P, SEQ])
    mx = sbuf(stack, "mx", [P, QC, HG, QT])
    mm = sbuf(stack, "mm", [P, HG * QT])
    rest = sbuf(stack, "nm_rest", [P, HG * QT])
    nmp = sbuf(stack, "nmp", [P, PARTS, HG * QT], BF16)
    nrow = sbuf(stack, "nrow", [PARTS * HG * QT, P], BF16)
    rec = sbuf(stack, "rec", [P, 2, QT // 2, HG])
    SLOTS = 3
    MAX_BANK, ST_BANK, OT_BANK = 0, SLOTS, 2 * SLOTS

    ready, ones_ready, freed, vo_turn = sem("att_ready"), sem("ones_ready"), sem("kq_first"), sem("vo_turn")
    row_loaded = [sem(f"row_loaded{r}") for r in range(RING)]
    st_done, exp_done, pv_done = sem("st_done"), sem("exp_done"), sem("pv_done")
    max_done, red_done = sem("max_done"), sem("red_done")
    nm_steps, nm_tr, nm_kept = sem("nm_steps"), sem("nm_tr"), sem("nm_kept")
    vo_ready, ot_kept, ot_tr, att_steps = sem("vo_ready"), sem("ot_kept"), sem("ot_tr"), sem("att_steps")
    BLOCKS, MAXES, NM = KT * HG * QC, HG * QT * QC, 5
    order = [(h, q, k) for h in range(HG) for q in range(QT) for k in range(QC)]
    LOADS = 2 * len(PAIR_Q)
    EARLY = 12
    TURN = EARLY + 8
    LATE = 5
    events = ([("max", t) for t in range(LATE)] + [("nm", 0)] + [("max", t) for t in range(LATE, TURN)]
              + [("heads", 0), ("heads", 1)] + [("max", t) for t in range(TURN, MAXES)])
    place = {event: e for e, event in enumerate(events)}
    assert RING == SLOTS and BLOCKS % SLOTS == 1 and len(events) % SLOTS == 1
    bank = lambda r, event: MAX_BANK + (r + place[event]) % SLOTS
    st_bank = lambda r, s: ST_BANK + (r + s) % SLOTS

    def unit_loop(eng, unit):
        known = lambda u: lambda k: (u + k, (u + k) // RING, (u + k) % RING) if u + k < UNITS else None
        unit(known(0))
        with eng.Fori(0, (UNITS - 4) // RING) as i:
            for j in range(1, RING + 1):
                unit(lambda k, j=j: (RING * i + j + k, i + (j + k) // RING, (j + k) % RING))
        for u in range(UNITS - 3, UNITS):
            unit(known(u))
    assert (UNITS - 4) % RING == 0
    is0 = lambda u: isinstance(u, int) and u == 0

    with nc.Block() as block:
        @block.vector
        def _(dve):
            nc.vector.memset(VO[:], 1.0).then_inc(ready, 1)

            def reduce(u, r, t):
                h, q, k = order[t]
                dve.wait_ge(max_done, MAXES * u + t + 1)
                nc.vector.reduce_max(mx[:, k, h, q:q + 1], ps[:, bank(r, ("max", t))], AX).then_inc(red_done, 1)

            def negate(u):
                dve.wait_ge(red_done, MAXES * u + MAXES)
                if not is0(u):
                    dve.wait_ge(nm_tr, u)
                m0, m1 = (mx[:, k].rearrange("p h q -> p (h q)") for k in range(QC))
                step = lambda ins: ins.then_inc(nm_steps, 1)
                step(nc.vector.tensor_tensor(mm[:], m0, m1, op=ALU.max))
                dve.wait_ge(nm_steps, NM * u + 1)
                step(nc.vector.tensor_scalar_mul(nmp[:, 0], mm[:], -1.0))
                dve.wait_ge(nm_steps, NM * u + 2)
                step(nc.vector.scalar_tensor_tensor(rest[:], mm[:], -1.0, nmp[:, 0], op0=ALU.mult, op1=ALU.subtract))
                dve.wait_ge(nm_steps, NM * u + 3)
                step(nc.vector.tensor_copy(nmp[:, 1], rest[:]))
                dve.wait_ge(nm_steps, NM * u + 4)
                step(nc.vector.tensor_tensor(nmp[:, 2], rest[:], nmp[:, 1], op=ALU.subtract))

            def heads_out(u, r):
                for k in range(2):
                    o = ps[:, bank(r, ("heads", k))].rearrange("p (q h c) -> p q h c", q=QT // 2, h=HG)
                    dve.wait_ge(ot_tr, 2 * u + k + 1)
                    nc.vector.reciprocal(rec[:, k], o[:, :, :, HD]).then_inc(att_steps, 1)
                    dve.wait_ge(att_steps, 4 * u + 2 * k + 1)
                    b, g = u // UPB, u % UPB
                    nc.vector.tensor_tensor(
                        V[:, ds(QT * b + QT // 2 * k, QT // 2), ds(HG * HD * g, HG * HD)].rearrange("p q (h c) -> p q h c", h=HG),
                        o[:, :, :, 0:HD], rec[:, k].unsqueeze(3).broadcast_to([P, QT // 2, HG, HD]), op=ALU.mult).then_inc(att_steps, 1)

            for t in range(MAXES):
                reduce(0, 0, t)
            negate(0)
            for t in range(EARLY):
                reduce(1, 1, t)

            def unit(at):
                (u, n, r), nxt, after = at(0), at(1), at(2)
                if nxt is not None:
                    for t in range(EARLY, TURN):
                        reduce(nxt[0], nxt[2], t)
                if not is0(u):
                    heads_out(u - 1, (r + 1) % RING)
                if nxt is not None:
                    for t in range(TURN, MAXES):
                        reduce(nxt[0], nxt[2], t)
                    negate(nxt[0])
                if after is not None:
                    for t in range(EARLY):
                        reduce(after[0], after[2], t)
            unit_loop(dve, unit)
            heads_out(UNITS - 1, (UNITS + 1) % RING)

        @block.scalar
        def _(act):
            def keep_rows(u, r):
                act.wait_ge(nm_tr, u + 1)
                if not is0(u):
                    act.wait_ge(freed, u)
                nc.scalar.copy(nrow[:], ps[0:PARTS * HG * QT, bank(r, ("nm", 0)), 0:P // 2].bitcast(BF16)).then_inc(nm_kept, 1)

            ffw.magnitudes(nc, act, kept)
            keep_rows(0, 1)

            def unit(at):
                (u, n, r), nxt = at(0), at(1)
                for s in range(BLOCKS):
                    kt, h, qc = s // (HG * QC), s // QC % HG, s % QC
                    act.wait_ge(st_done, BLOCKS * u + s + 1)
                    if h == 0 and qc == 0 and not (is0(u) and kt < 2):
                        act.wait_ge(pv_done, KT * u + kt - 1)
                    nc.scalar.activation(PR[:, kt % 2, h, qc * BANK:(qc + 1) * BANK], ps[:, st_bank(r, s)], ACT.Exp).then_inc(exp_done, 1)
                    if nxt is not None and s == (BLOCKS - 8 if at(2) is not None else BLOCKS - 1):
                        keep_rows(nxt[0], (nxt[2] + 1) % RING)
                act.wait_ge(pv_done, KT * u + KT)
                if not is0(u):
                    act.wait_ge(ot_tr, 2 * u)
                nc.scalar.copy(OT[:], ps[:, OT_BANK:OT_BANK + 2].rearrange("p a n -> p (a n)")).then_inc(ot_kept, 1)
            unit_loop(act, unit)

        @block.gpsimd
        def _(pool):
            nc.gpsimd.memset(KQ[RING - 1][KROWS:AROWS, 0].rearrange("p h n -> p (h n)"), 1.0).then_inc(ones_ready, 1)
            pool.wait_ge(ones_ready, 1)
            pool.wait_ge(ready, 1)

            def unit(at):
                u = at(0)[0]
                if not is0(u):
                    pool.wait_ge(pv_done, KT * u)
                pool.sem_inc(vo_turn, 1)
                b, g = u // UPB, u % UPB
                nc.gpsimd.tensor_copy(VO[:, :, :, 0:HD], V[:, ds(KT * b, KT), ds(HG * HD * g, HG * HD)].rearrange("p k (h c) -> p k h c", h=HG)).then_inc(vo_ready, 1)
                if is0(u):
                    ffw.quantise(nc, pool, kept)
            unit_loop(pool, unit)

        @block.sync
        def _(sp):
            def rows(u, r):
                sp.wait_ge(nm_kept, u + 1)
                for a in range(PARTS):
                    n = HG * QT
                    sp.dma_start(KQ[r][KROWS + a:KROWS + a + 1, 1].rearrange("p h (q n) -> p (h q) n", n=P),
                                 nrow[a * n:(a + 1) * n, :]).then_inc(row_loaded[r], 16)

            ffw.load(sp)
            rows(0, 0)

            def unit(at):
                (u, n, r), nxt, after = at(0), at(1), at(2)
                sp.wait_ge(row_loaded[r], 16 * PARTS * (n + 1))
                if after is not None and not is0(u):
                    sp.wait_ge(st_done, BLOCKS * u)
                sp.sem_inc(freed, 1)
                if after is not None:
                    load_qk(sp, after[0], after[2])
                if nxt is not None:
                    rows(nxt[0], nxt[2])
            unit_loop(sp, unit)

        @block.tensor
        def _(pe):
            def bank_read(u, e):
                while True:
                    u, e = (u, e - SLOTS) if e >= SLOTS else (u - 1, e - SLOTS + len(events))
                    if isinstance(u, int) and u < 0:
                        return
                    kind, t = events[e]
                    if isinstance(u, int) and (kind == "max" and u >= UNITS or kind == "nm" and u > UNITS):
                        continue
                    if kind == "max":
                        return pe.wait_ge(red_done, MAXES * u + t + 1)
                    if kind == "nm" and not is0(u):
                        return pe.wait_ge(nm_kept, u)
                    if kind == "heads" and (not isinstance(u, int) or u >= 2):
                        return pe.wait_ge(att_steps, 4 * (u - 2) + 2 * t + 2)

            def first_pass(u, n, r, t):
                h, q, k = order[t]
                if t == 0:
                    pe.wait_ge(kq_loaded[r], 16 * LOADS * (n + 1))
                bank_read(u, place["max", t])
                nc.tensor.matmul(ps[:, bank(r, ("max", t))], KQ[r][0:KROWS, 1, h, q * P:(q + 1) * P], KQ[r][0:KROWS, 0, h, k * BANK:(k + 1) * BANK],
                                 start=True, stop=True).then_inc(max_done, 1)

            def turn_max(u, r):
                pe.wait_ge(nm_steps, NM * u + NM)
                bank_read(u + 1, place["nm", 0])
                nc.tensor.transpose(ps[0:PARTS * HG * QT, bank(r, ("nm", 0)), 0:P // 2].bitcast(BF16), nmp[:].rearrange("p a n -> p (a n)"), identb[:]).then_inc(nm_tr, 1)

            def turn_heads(u, r, k):
                pe.wait_ge(ot_kept, u + 1)
                bank_read(u + 2, place["heads", k])
                for q in range(QT // 2):
                    last = nc.tensor.transpose(ps[:, bank(r, ("heads", k)), q * P:(q + 1) * P], OT[:, (k * QT // 2 + q) * P:(k * QT // 2 + q + 1) * P], ident[:])
                last.then_inc(ot_tr, 1)

            def weigh(u, kt, qc):
                if qc == 0:
                    pe.wait_ge(exp_done, BLOCKS * u + HG * QC * (kt + 1))
                if kt == 0 and qc == 0:
                    pe.wait_ge(vo_ready, u + 1)
                    if not is0(u):
                        pe.wait_ge(ot_kept, u)
                for h in range(HG):
                    last = nc.tensor.matmul(ps[2 * HD * h:2 * HD * (h + 1), OT_BANK + qc], VO[:, kt, h], PR[:, kt % 2, h, qc * BANK:(qc + 1) * BANK],
                                            start=(kt == 0), stop=(kt == KT - 1))
                if qc == QC - 1:
                    last.then_inc(pv_done, 1)

            for t in range(MAXES):
                first_pass(0, 0, 0, t)
            for t in range(LATE):
                first_pass(1, 0, 1, t)
            turn_max(0, 1)
            for t in range(LATE, EARLY):
                first_pass(1, 0, 1, t)

            def unit(at):
                (u, n, r), nxt, after = at(0), at(1), at(2)
                beside = [(first_pass, (*nxt, t)) for t in range(EARLY, TURN)] if nxt is not None else []
                if not is0(u):
                    beside += [(turn_heads, (u - 1, (r + 1) % RING, k)) for k in range(2)]
                if nxt is not None:
                    beside += [(first_pass, (*nxt, t)) for t in range(TURN, MAXES)]
                if after is not None:
                    beside += [(first_pass, (*after, t)) for t in range(LATE)]
                if nxt is not None:
                    beside += [(turn_max, (nxt[0], (nxt[2] + 1) % RING))]
                if after is not None:
                    beside += [(first_pass, (*after, t)) for t in range(LATE, EARLY)]
                pe.wait_ge(row_loaded[r], 16 * PARTS * (n + 1))
                if r == RING - 1:
                    pe.wait_ge(ones_ready, 1)
                done = 0
                for s in range(BLOCKS):
                    kt, h, qc = s // (HG * QC), s // QC % HG, s % QC
                    if not (is0(u) and s < SLOTS):
                        pe.wait_ge(exp_done, BLOCKS * u + s - SLOTS + 1)
                    nc.tensor.matmul(ps[:, st_bank(r, s)], KQ[r][0:AROWS, 0, h, kt * P:(kt + 1) * P],
                                     KQ[r][0:AROWS, 1, h, qc * BANK:(qc + 1) * BANK], start=True, stop=True).then_inc(st_done, 1)
                    if kt > 0 and h in (1, 3) and qc == 1:
                        weigh(u, kt - 1, h // 2)
                    while done < (s + 1) * len(beside) // BLOCKS:
                        what, given = beside[done]
                        what(*given)
                        done += 1
                for qc in range(QC):
                    weigh(u, KT - 1, qc)
            unit_loop(pe, unit)
            for k in range(2):
                turn_heads(UNITS - 1, (UNITS + 1) % RING, k)


_INS = ['L0_attn_x', 'L0_attn_Wq', 'L0_attn_Wk', 'L0_attn_Wv', 'L0_attn_Wo', 'L0_attn_quadrant_weights',
        'L0_ffn_fast_b', 'L0_ffn_w_fc', 'L0_ffn_w_proj', 'L0_ffn_u', 'L0_ffn_v', 'L0_ffn_gate',
        'L1_attn_A', 'L1_attn_Bm', 'L1_attn_Cm', 'L1_attn_Dm', 'L1_attn_ln_w', 'L1_attn_ln_b', 'L1_attn_W_out', 'L1_attn_b_out',
        'L1_ffn_Wg', 'L1_ffn_bg', 'L1_ffn_bias', 'L1_ffn_W1', 'L1_ffn_b1', 'L1_ffn_W2', 'L1_ffn_b2']


def kernel(**inputs):
    import numpy as np
    import concourse.bacc as bacc
    from concourse.bass_utils import run_bass_kernel_spmd

    nc = bacc.Bacc("TRN2", target_bir_lowering=False, num_devices=1)
    nc.disable_value_cache = True
    arrays, args = {}, []
    for name in _INS:
        a = np.ascontiguousarray(inputs[name])
        if a.ndim == 0:
            a = a.reshape(1)
        arrays[f"in_{name}"] = a
        args.append(nc.dram_tensor(f"in_{name}", a.shape, mybir.dt.from_np(a.dtype), kind="ExternalInput").ap())
    out = nc.dram_tensor("out", (BATCH, SEQ, D), F32, kind="ExternalOutput").ap()
    transformer_kernel(nc, args, out)
    r = run_bass_kernel_spmd(nc, [arrays], core_ids=[0])
    return r.results[0]["out"]
```
